# Optimizing a Trainium2 kernel written in Bass

```python
import numpy as np
import jax
import jax.numpy as jnp

def _softmax(x, axis=-1):
    return jax.nn.softmax(x, axis=axis)

def _gelu(x):
    return jax.nn.gelu(x, approximate=True)

def _silu(x):
    return jax.nn.silu(x)

def _sigmoid(x):
    return jax.nn.sigmoid(x)

def _layernorm(x, axis=-1, eps=1e-05):
    m = jnp.mean(x, axis=axis, keepdims=True)
    v = jnp.var(x, axis=axis, keepdims=True)
    return (x - m) / jnp.sqrt(v + eps)

def _scatter_add(tgt, idx, src, axis=0):
    return tgt.at[idx].add(src)

def _segment_sum(src, seg, n):
    return jax.ops.segment_sum(src, seg, n)
kernel_name = 'mk_flamingo_gated_d2_seqx_r8_84ec8c'

def setup_inputs(seed: int=0):
    np.random.seed(seed)
    _w = jnp.asarray

    def _rec_inputs():
        import jax
        import jax.numpy as jnp
        _rk = jax.random.key(seed)
        x = -0.0003929 + 0.9999 * jax.random.normal(jax.random.fold_in(_rk, 1), (8, 128, 512), jnp.float32)
        _lenS = 128 - jax.random.randint(jax.random.fold_in(_rk, 7), (8,), 0, max(1, 128 // 4) + 1, jnp.int32)
        _lenS2 = 128 - jax.random.randint(jax.random.fold_in(_rk, 8), (8,), 0, max(1, 128 // 4) + 1, jnp.int32)
        _ctx_4096P = jax.random.normal(jax.random.fold_in(_rk, 11), (8, 16, 512), jnp.float32)
        _ctx_4096c = jax.random.dirichlet(jax.random.fold_in(_rk, 511), 0.3 * jnp.ones((16,), jnp.float32), (8, 128))
        _ctx_4096t = jnp.einsum('bsk,bkd->bsd', _ctx_4096c, _ctx_4096P)
        _ctx_4096t = _ctx_4096t * jax.lax.rsqrt(jnp.mean(jnp.square(_ctx_4096t)) + 1e-12) * 0.953939
        ctx_4096 = 2.81802e-05 + 1.00001 * (_ctx_4096t + 0.3 * jax.random.normal(jax.random.fold_in(_rk, 611), (8, 128, 512), jnp.float32))
        _validS = jnp.arange(128)[None, :] < _lenS[:, None]
        _validS2 = jnp.arange(128)[None, :] < _lenS2[:, None]
        _causal = jnp.tril(jnp.ones((128, 128), dtype=bool))
        mask_SxS2_bk0 = jnp.logical_not(jnp.broadcast_to(_validS2[0:1, :], (128, 128)))
        _g = jax.random.normal(jax.random.fold_in(_rk, 9001), (2, 2), jnp.float32)
        _g = jnp.sign(_g) * jnp.maximum(jnp.abs(_g), 1.0) + (_g == 0) * 1.0
        g_xattn = _g[0]
        g_ffn = _g[1]
        return (x, ctx_4096, mask_SxS2_bk0, g_xattn, g_ffn)
    x, ctx_4096, mask_SxS2_bk0, g_xattn, g_ffn = _rec_inputs()

    def _L0_xattn_setup():
        import jax, jax.numpy as jnp
        import numpy as np
        HID = 512
        NHEAD = 32
        NKV = 8
        HDIM = 128
        G = NHEAD // NKV
        key = jax.random.key(seed)
        ks = jax.random.split(key, 6)
        s = 0.02
        B, L = (2, 256)
        return {'query': jax.random.normal(ks[0], (B, L, HID), jnp.float32), 'kv': jax.random.normal(ks[1], (B, L, HID), jnp.float32), 'Wq': jax.random.normal(ks[2], (HID, NHEAD * HDIM), jnp.float32) * s, 'bq': jnp.zeros((NHEAD * HDIM,), jnp.float32), 'Wkv': jax.random.normal(ks[3], (HID, 2 * NKV * HDIM), jnp.float32) * s, 'bkv': jnp.zeros((2 * NKV * HDIM,), jnp.float32), 'Wo': jax.random.normal(ks[4], (NHEAD * HDIM, HID), jnp.float32) * s, 'bo': jnp.zeros((HID,), jnp.float32)}
    _L0_xattn_all = _L0_xattn_setup()
    _L0_xattn_in = {k: v for k, v in _L0_xattn_all.items() if k in ('Wq', 'bq', 'Wkv', 'bkv', 'Wo', 'bo')}
    del _L0_xattn_all

    def _L0_ffn_setup():
        import jax, jax.numpy as jnp
        import numpy as np
        B, S, D, O, E, R = (4, 256, 512, 512, 8, 16)
        SCALING = 32.0 / 16.0
        MAX_THRESHOLD = 0.125
        key = jax.random.key(seed)
        ks = jax.random.split(key, 8)
        return {'x': jax.random.normal(ks[0], (B, S, D), jnp.float32), 'W_base': jax.random.normal(ks[1], (O, D), jnp.float32) * (1.0 / np.sqrt(D)), 'b_base': jax.random.normal(ks[2], (O,), jnp.float32) * 0.02, 'W_gate': jax.random.normal(ks[3], (E, D), jnp.float32) * (1.0 / np.sqrt(D)), 'W_thr': jax.random.normal(ks[4], (D,), jnp.float32) * (1.0 / np.sqrt(D)), 'b_thr': jax.random.normal(ks[5], (1,), jnp.float32) * 0.02, 'A_w': jax.random.normal(ks[6], (E, R, D), jnp.float32) * (1.0 / np.sqrt(D)), 'B_w': jax.random.normal(ks[7], (E, O, R), jnp.float32) * (1.0 / np.sqrt(R))}
    _L0_ffn_all = _L0_ffn_setup()
    _L0_ffn_in = {k: v for k, v in _L0_ffn_all.items() if k in ('W_base', 'b_base', 'W_gate', 'W_thr', 'b_thr', 'A_w', 'B_w')}
    del _L0_ffn_all

    def _L1_xattn_setup():
        import jax, jax.numpy as jnp
        import numpy as np
        N_HEAD = 32
        D_MODEL = 512
        N_KV_GROUPS = 8
        D_HEAD = D_MODEL // N_HEAD
        H_PER_G = N_HEAD // N_KV_GROUPS
        KV_DIM = N_KV_GROUPS * D_HEAD
        B, S = (2, 256)
        key = jax.random.key(seed)
        ks = jax.random.split(key, 8)
        q = jax.random.normal(ks[0], (B, S, D_MODEL), dtype=jnp.float32)
        k = jax.random.normal(ks[1], (B, S, D_MODEL), dtype=jnp.float32)
        v = jax.random.normal(ks[2], (B, S, D_MODEL), dtype=jnp.float32)
        mask = jnp.tril(jnp.ones((S, S), dtype=bool))
        w_q = jax.random.uniform(ks[3], (D_MODEL, D_MODEL), dtype=jnp.float32) * 0.02
        w_k = jax.random.uniform(ks[4], (KV_DIM, D_MODEL), dtype=jnp.float32) * 0.02
        w_v = jax.random.uniform(ks[5], (KV_DIM, D_MODEL), dtype=jnp.float32) * 0.02
        w_out = jax.random.uniform(ks[6], (D_MODEL, D_MODEL), dtype=jnp.float32) * 0.02
        return {'q': q, 'k': k, 'v': v, 'w_q': w_q, 'w_k': w_k, 'w_v': w_v, 'w_out': w_out, 'mask': mask}
    _L1_xattn_all = _L1_xattn_setup()
    _L1_xattn_in = {k: v for k, v in _L1_xattn_all.items() if k in ('w_q', 'w_k', 'w_v', 'w_out')}
    del _L1_xattn_all

    def _L1_ffn_setup():
        import jax, jax.numpy as jnp
        import numpy as np
        IN_CHN = 512
        OUT_CHN = 512

        def binarize_weights(weight):
            scale = jax.lax.stop_gradient(jnp.mean(jnp.abs(weight), axis=1, keepdims=True))
            bin_no_grad = scale * jnp.sign(weight)
            clipped = jnp.clip(weight, -1.0, 1.0)
            return jax.lax.stop_gradient(bin_no_grad) - jax.lax.stop_gradient(clipped) + clipped
        key = jax.random.key(seed)
        kx, kw = jax.random.split(key)
        x = jax.random.normal(kx, (4, 256, IN_CHN), dtype=jnp.float32)
        weight = jax.random.uniform(kw, (OUT_CHN, IN_CHN), dtype=jnp.float32) * 0.001
        return {'x': x, 'weight': weight}
    _L1_ffn_all = _L1_ffn_setup()
    _L1_ffn_in = {k: v for k, v in _L1_ffn_all.items() if k in ('weight',)}
    del _L1_ffn_all
    return {'x': x, 'ctx_4096': ctx_4096, 'mask_SxS2_bk0': mask_SxS2_bk0, 'g_xattn': g_xattn, 'g_ffn': g_ffn, 'L0_xattn_Wq': _L0_xattn_in['Wq'], 'L0_xattn_bq': _L0_xattn_in['bq'], 'L0_xattn_Wkv': _L0_xattn_in['Wkv'], 'L0_xattn_bkv': _L0_xattn_in['bkv'], 'L0_xattn_Wo': _L0_xattn_in['Wo'], 'L0_xattn_bo': _L0_xattn_in['bo'], 'L0_ffn_W_base': _L0_ffn_in['W_base'], 'L0_ffn_b_base': _L0_ffn_in['b_base'], 'L0_ffn_W_gate': _L0_ffn_in['W_gate'], 'L0_ffn_W_thr': _L0_ffn_in['W_thr'], 'L0_ffn_b_thr': _L0_ffn_in['b_thr'], 'L0_ffn_A_w': _L0_ffn_in['A_w'], 'L0_ffn_B_w': _L0_ffn_in['B_w'], 'L1_xattn_w_q': _L1_xattn_in['w_q'], 'L1_xattn_w_k': _L1_xattn_in['w_k'], 'L1_xattn_w_v': _L1_xattn_in['w_v'], 'L1_xattn_w_out': _L1_xattn_in['w_out'], 'L1_ffn_weight': _L1_ffn_in['weight']}

def reference(x, ctx_4096, mask_SxS2_bk0, g_xattn, g_ffn, L0_xattn_Wq, L0_xattn_bq, L0_xattn_Wkv, L0_xattn_bkv, L0_xattn_Wo, L0_xattn_bo, L0_ffn_W_base, L0_ffn_b_base, L0_ffn_W_gate, L0_ffn_W_thr, L0_ffn_b_thr, L0_ffn_A_w, L0_ffn_B_w, L1_xattn_w_q, L1_xattn_w_k, L1_xattn_w_v, L1_xattn_w_out, L1_ffn_weight):
    import jax
    import jax.numpy as jnp

    def _L0_xattn_ref(query, kv, Wq, bq, Wkv, bkv, Wo, bo):
        import jax, jax.numpy as jnp
        import numpy as np
        HID = 512
        NHEAD = 32
        NKV = 8
        HDIM = 128
        G = NHEAD // NKV
        B, L, _ = query.shape
        Lk = kv.shape[1]
        scale = jnp.asarray(1.0 / np.sqrt(HDIM), query.dtype)
        q = (query @ Wq + bq).reshape(B, L, NKV, G, HDIM)
        k_, v_ = jnp.split(kv @ Wkv + bkv, 2, axis=-1)
        k = k_.reshape(B, Lk, NKV, HDIM)
        v = v_.reshape(B, Lk, NKV, HDIM)
        scores = jnp.einsum('blkgd,bmkd->bkglm', q, k) * scale
        attn = jax.nn.softmax(scores, axis=-1)
        o = jnp.einsum('bkglm,bmkd->blkgd', attn, v).reshape(B, L, NHEAD * HDIM)
        return o @ Wo + bo

    def _L0_ffn_ref(x, W_base, b_base, W_gate, W_thr, b_thr, A_w, B_w):
        import jax, jax.numpy as jnp
        import numpy as np
        B, S, D, O, E, R = (4, 256, 512, 512, 8, 16)
        SCALING = 32.0 / 16.0
        MAX_THRESHOLD = 0.125
        base = jnp.einsum('bsd,od->bso', x, W_base) + b_base
        xf = x.reshape(-1, D)
        gate = jax.nn.softmax(xf @ W_gate.T, axis=-1)
        thr = jax.nn.sigmoid(xf @ W_thr + b_thr[0]) * MAX_THRESHOLD
        adapted = gate - thr[:, None]
        selected = (adapted >= 0).astype(x.dtype)
        w = adapted * selected
        wsum = jnp.sum(w, axis=-1, keepdims=True)
        wsum = jnp.where(wsum == 0, jnp.ones_like(wsum), wsum)
        w = w / wsum
        h = jnp.einsum('nd,erd->ner', xf, A_w)
        moe = jnp.einsum('ner,ne,eor->no', h, w, B_w) * SCALING
        return base + moe.reshape(base.shape)

    def _L1_xattn_ref(q, k, v, w_q, w_k, w_v, w_out, mask):
        import jax, jax.numpy as jnp
        import numpy as np
        N_HEAD = 32
        D_MODEL = 512
        N_KV_GROUPS = 8
        D_HEAD = D_MODEL // N_HEAD
        H_PER_G = N_HEAD // N_KV_GROUPS
        KV_DIM = N_KV_GROUPS * D_HEAD
        B, S = (2, 256)
        b, n, _ = q.shape
        s = k.shape[1]
        query = q @ w_q.T
        key = k @ w_k.T
        value = v @ w_v.T
        query = query.reshape(b, n, N_HEAD, D_HEAD).transpose(0, 2, 1, 3)
        query = query.reshape(b, N_KV_GROUPS, H_PER_G, n, D_HEAD)
        key = key.reshape(b, s, N_KV_GROUPS, D_HEAD).transpose(0, 2, 1, 3)
        value = value.reshape(b, s, N_KV_GROUPS, D_HEAD).transpose(0, 2, 1, 3)
        scores = jnp.einsum('bghnd,bgsd->bghns', query, key) / D_HEAD ** 0.5
        scores = jnp.where(mask, scores, jnp.finfo(scores.dtype).min)
        attention = jax.nn.softmax(scores, axis=-1)
        out = jnp.einsum('bghns,bgsd->bghnd', attention, value)
        out = out.transpose(0, 3, 1, 2, 4).reshape(b, n, D_MODEL)
        return out @ w_out.T

    def _L1_ffn_ref(x, weight):
        import jax, jax.numpy as jnp
        import numpy as np
        IN_CHN = 512
        OUT_CHN = 512

        def binarize_weights(weight):
            scale = jax.lax.stop_gradient(jnp.mean(jnp.abs(weight), axis=1, keepdims=True))
            bin_no_grad = scale * jnp.sign(weight)
            clipped = jnp.clip(weight, -1.0, 1.0)
            return jax.lax.stop_gradient(bin_no_grad) - jax.lax.stop_gradient(clipped) + clipped
        bw = binarize_weights(weight)
        return jnp.einsum('bsi,oi->bso', x, bw)
    x = x + jnp.tanh(g_xattn[0]) * _L0_xattn_ref(_layernorm(x, axis=-1), ctx_4096, L0_xattn_Wq, L0_xattn_bq, L0_xattn_Wkv, L0_xattn_bkv, L0_xattn_Wo, L0_xattn_bo)
    x = x + jnp.tanh(g_ffn[0]) * _L0_ffn_ref(_layernorm(x, axis=-1), L0_ffn_W_base, L0_ffn_b_base, L0_ffn_W_gate, L0_ffn_W_thr, L0_ffn_b_thr, L0_ffn_A_w, L0_ffn_B_w)
    x = x + jnp.tanh(g_xattn[1]) * _L1_xattn_ref(_layernorm(x, axis=-1), ctx_4096, ctx_4096, L1_xattn_w_q, L1_xattn_w_k, L1_xattn_w_v, L1_xattn_w_out, mask_SxS2_bk0)
    x = x + jnp.tanh(g_ffn[1]) * _L1_ffn_ref(_layernorm(x, axis=-1), L1_ffn_weight)
    return x

_drawn_inputs = setup_inputs


def setup_inputs(seed=0):
    import zlib

    import numpy as np

    out = dict(_drawn_inputs(seed))
    spreads = {'g_ffn': (-1.0, 0.6),
     'L0_xattn_bq': (0.0, 2.0),
     'L0_xattn_bkv': (0.0, 0.1),
     'L0_xattn_bo': (0.0, 0.1)}
    factors = {'L0_xattn_Wq': 3.247, 'L0_ffn_b_base': 6.479, 'L1_xattn_w_out': 6.735}
    for name, (base, spread) in spreads.items():
        noise = np.random.default_rng([zlib.crc32(name.encode()), seed]).standard_normal(out[name].shape)
        drawn = base * np.exp(spread * noise) if base else spread * noise
        out[name] = jnp.asarray(drawn.astype(out[name].dtype))
    for name, factor in factors.items():
        out[name] = (out[name] * factor).astype(out[name].dtype)
    return out
```

```python
from contextlib import ExitStack

import numpy as np

import concourse.bass as bass
from concourse import mybir

ALU = mybir.AluOpType
ACT = mybir.ActivationFunctionType
AX = mybir.AxisListType
F32 = mybir.dt.float32
F32R = mybir.dt.float32r
P = 128


def build(nc, x, ctx_in, mask, g_xattn, g_ffn, Wq, bq, Wkv, bkv, Wo, bo, W_base, b_base, W_gate, W_thr, b_thr, A_w, B_w,
          w_q, w_k, w_v, w_out, w_bin, out):
    BATCH, TOK, D = x.shape
    DH = P
    HEADS = Wq.shape[1] // DH
    KVH = Wkv.shape[1] // (2 * DH)
    G = HEADS // KVH
    C = D // P
    NT = BATCH
    HALF = NT * TOK // 2
    STEPS = NT
    SCALE0 = float(1.0 / np.sqrt(DH))
    EPS = 1e-5
    SLOTS = 2

    SLICES = [("q", 0), ("k", 0), ("q", 1), ("q", 2), ("o", 0), ("q", 3), ("v", 0), ("o", 1), ("o", 2), ("o", 3)]
    SPLIT_AT = {0: [0], 1: [1, 2], 2: [3, 4], 3: [5, 6], 4: [7], 5: [8], 6: [9], 7: []}
    NS = len(SLICES)

    E, R = A_w.shape[0], A_w.shape[1]
    NGT = E + 2
    ADAPT = 2.0
    THR_MAX = 0.125
    KV1 = w_k.shape[0]
    DH1 = D // HEADS
    G1 = KV1 // DH1
    J1 = HEADS // G1
    GH = G1 // 2
    SCALE1 = float(DH1) ** -0.5
    MASKED = float((2 - 2.0 ** -11) * 2.0 ** 127)
    UNITS = NT * 2 * J1
    HT = NT // 2

    x_rows = x.rearrange("b t d -> t b d")
    ctx_rows = ctx_in.rearrange("b t d -> t b d")
    wq_rows = Wq.rearrange("(c p) n -> p c n", p=P)
    wkv_rows = Wkv.rearrange("(c p) n -> p c n", p=P)
    wo_rows = Wo.rearrange("(h p) n -> h p n", p=P)

    with ExitStack() as es:
        def sb(name, shape, dt=F32, scope=es):
            return scope.enter_context(nc.sbuf_tensor(name, shape, dt))

        def sem(name):
            return es.enter_context(nc.semaphore(name))

        bank = [es.enter_context(nc.psum_tensor(f"bank{i}", [P, 512], F32)) for i in range(8)]
        ps_s, ps_pt, ps_o, ps_q, ps_out, ps_kv, ps_vt = bank[:7]

        xres = sb("xres", [P, NT, D])
        xT = [sb("xT_hi", [P, C, NT * TOK], F32R), sb("xT_lo", [P, C, NT * TOK], F32R)]
        ident = sb("ident", [P, P])
        ident_r = sb("ident_r", [P, P], F32R)
        gate_raw = sb("gate_raw", [P, 4])
        gate = sb("gate", [P, 4])
        stats = sb("stats", [P, NT, 6])
        moments = sb("moments", [P, NT, 2])
        rstd = sb("rstd", [P, NT])
        nmax1 = sb("nmax1", [P, 2, GH])
        rsum1 = sb("rsum1", [P, 2, GH])
        rinv1 = sb("rinv1", [P, 2, GH])
        power = sb("power", [P, NT])

        ctx_scope = ExitStack()
        cT = [sb("cT_hi", [P, C, NT * TOK], F32R, ctx_scope), sb("cT_lo", [P, C, NT * TOK], F32R, ctx_scope)]

        l0 = ExitStack()
        qT = [sb("qT_hi", [P, G, NT * TOK], F32R, l0), sb("qT_lo", [P, G, NT * TOK], F32R, l0)]
        kT = [sb("kT_hi", [P, NT * TOK], F32R, l0), sb("kT_lo", [P, NT * TOK], F32R, l0)]
        v = [sb("v_hi", [P, NT, DH], F32R, l0), sb("v_lo", [P, NT, DH], F32R, l0)]
        vT = sb("vT", [P, 4, TOK], F32, l0)
        wq = [sb("wq_hi", [P, G, C, DH], F32R, l0), sb("wq_lo", [P, G, C, DH], F32R, l0)]
        wk = [sb("wk_hi", [P, C, DH], F32R, l0), sb("wk_lo", [P, C, DH], F32R, l0)]
        wv = [sb("wv_hi", [P, C, DH], F32R, l0), sb("wv_lo", [P, C, DH], F32R, l0)]
        wo = [sb("wo_hi", [P, 2 * G * D], F32R, l0), sb("wo_lo", [P, 2 * G * D], F32R, l0)]
        stage = sb("stage", [P, SLOTS, 512], F32, l0)
        prob = sb("prob", [P, G, TOK], F32, l0)
        pT = [sb("pT_hi", [P, 512], F32R, l0), sb("pT_lo", [P, 512], F32R, l0)]
        oT = [sb("oT_hi", [P, G, TOK], F32R, l0), sb("oT_lo", [P, G, TOK], F32R, l0)]
        bias_all = sb("bias_all", [P, KVH * (G + 2)], F32, l0)
        bias = sb("bias", [P, G + 2], F32, l0)
        nmax = sb("nmax", [P, 2, G], F32, l0)
        rsum = sb("rsum", [P, G], F32, l0)
        rinv = sb("rinv", [P, G], F32, l0)

        s_ident0, s_ident = sem("ident_zeroed"), sem("ident_ready")
        s_x_in = [sem(f"x_in{b}") for b in range(NT)]
        s_ctx_in = [sem(f"ctx_in{b}") for b in range(NT)]
        s_small_in = sem("small_in")
        s_gate = sem("gate_ready")
        s_stats, s_moments, s_rstd = sem("stats"), sem("moments"), sem("rstd")
        s_pow = sem("rstd_ready")
        s_xn = sem("x_normalised")
        s_bo = sem("bo_gated")
        s_xres = sem("xres_ready")
        s_tr, s_tr_hi, s_tr_lo = sem("transposed"), sem("transposed_hi"), sem("transposed_lo")
        s_bias_tr, s_bias_all, s_bias = sem("bias_transposed"), sem("bias_all"), sem("bias_now")
        s_w_in = [sem(f"weight_in{i}") for i in range(SLOTS)]
        s_w_hi, s_w_lo = sem("weight_hi"), sem("weight_lo")
        s_qproj, s_q_hi, s_q_lo = sem("q_projected"), sem("q_hi"), sem("q_lo")
        s_kproj, s_k_hi, s_k_lo = sem("k_projected"), sem("k_hi"), sem("k_lo")
        s_vproj, s_vt, s_vtr, s_v_hi, s_v_lo = sem("v_projected"), sem("vT_ready"), sem("v_transposed"), sem("v_hi"), sem("v_lo")
        s_scores, s_max, s_nmax, s_exp = sem("scores"), sem("row_max"), sem("neg_max"), sem("exped")
        s_rinv, s_norm, s_ptr = sem("rsum_inverted"), sem("prob_normalised"), sem("prob_transposed")
        s_pt_hi, s_pt_lo, s_pv, s_o_hi, s_o_lo = sem("pT_hi"), sem("pT_lo"), sem("pv"), sem("oT_hi"), sem("oT_lo")
        s_out, s_acc = sem("out_projected"), sem("out_added")
        s_store = sem("stored")
        s_nat = [sem(f"natural_in{i}") for i in range(6)]
        s_small2 = sem("small2_in")
        s_gzero = sem("gate_rows_zeroed")
        s_made, s_hi, s_lo = sem("split_made"), sem("split_hi"), sem("split_lo")
        s_eps, s_pow2, s_xn2 = sem("variance_eps"), sem("rstd2_ready"), sem("xn_ready")
        s_bb, s_bbg, s_xb = sem("b_base_in"), sem("b_base_gated"), sem("b_base_added")
        s_h, s_el, s_ee, s_hw = sem("adapters_down"), sem("gate_logits"), sem("gate_exps"), sem("adapters_weighted")
        s_f0, s_x2 = sem("ffn0_done"), sem("x2_ready")
        s_bin = sem("w_bin_ready")
        s_idr, s_mask, s_grp0, s_grp1, s_grp = sem("ident_r"), sem("negmask"), sem("group0"), sem("group1"), sem("group_of")
        s_vz, s_kd, s_vd = sem("v_zeroed"), sem("k_by_group"), sem("v_by_group")
        s_s1, s_m1, s_e1, s_r1, s_n1 = sem("scores1"), sem("max1"), sem("exp1"), sem("rinv1"), sem("norm1")
        s_t1, s_t1h, s_t1l, s_pv1 = sem("p1_transposed"), sem("p1T_hi"), sem("p1T_lo"), sem("pv1")
        s_o1h, s_o1l, s_out1, s_x3 = sem("o1T_hi"), sem("o1T_lo"), sem("out1"), sem("x3_ready")
        s_f1, s_x4 = sem("ffn1_done"), sem("x4_ready")
        s_chain = sem("vector_chain")

        l0.close()
        pre = ExitStack()
        ctx_nat = sb("ctx_nat", [P, NT, D], F32, pre)
        xn_nat = sb("xn_nat", [P, NT, D], F32, pre)
        bias_nat = sb("bias_nat", [HEADS + 2 * KVH, DH], F32, pre)
        bo_bc = sb("bo_bc", [P, D], F32, pre)
        pre.close()

        def pair(name, shape, scope):
            return [sb(name + "_hi", shape, F32R, scope), sb(name + "_lo", shape, F32R, scope)]

        l1 = ExitStack()
        ffn = ExitStack()
        wb = pair("w_base", [P, C, D], ffn)
        wa = pair("w_adapt", [P, C, E * R], ffn)
        wg = pair("w_gates", [P, C, NGT], ffn)
        wB = pair("w_up", [E * R, D], ffn)
        nat = sb("nat", [P, 2, 4 * D], F32, ffn)
        proj = ExitStack()
        wq1 = pair("w_q1", [P, C, D], proj)
        wk1 = pair("w_k1", [P, C, KV1], proj)
        wv1 = pair("w_v1", [P, C, KV1], proj)
        wo1 = pair("w_o1", [P, J1, D], l1)
        wf1 = pair("w_f1", [P, C, D], l1)
        k1T = pair("k1T", [KV1, NT * TOK], l1)
        v1 = pair("v1", [P, NT, KV1], l1)
        xn = sb("xn", [P, 2, D], F32, l1)
        hw = sb("hw", [P, HT, E * R], F32, l1)
        hwT = pair("hwT", [E * R, HT * TOK], l1)
        b_base_bc = sb("b_base_bc", [P, D], F32, l1)
        nb_thr = sb("nb_thr", [P, 1], F32, l1)
        gl = sb("gate_work", [P, 16, HT * E], F32, l1)
        var_eps = sb("var_eps", [P, 1], F32, l1)
        for scope in (l1, proj, ffn):
            scope.close()
        ctx_scope.close()
        att = ExitStack()
        q1T = pair("q1T", [P, J1, NT * TOK], att)
        p1T = pair("p1T", [P, 2, GH, J1 * TOK], att)
        negmask = sb("negmask", [P, GH, TOK], F32R, att)
        mask_in = sb("mask_in", [P, TOK], mybir.dt.uint8, att)
        group_of = sb("group_of", [P, G1], F32, att)
        used = 2 * C * (D + E * R + NGT) * 4 + 2 * D * 4 + 2 * 4 * D * 4
        mine = 2 * 2 * GH * J1 * TOK * 4 + GH * TOK * 4 + TOK + G1 * 4
        sb("over_ffn_weights", [P, used - mine], mybir.dt.uint8, att)
        kd = pair("k_by_group", [KV1, 2, GH, TOK], att)
        vd = pair("v_by_group", [P, 2, GH, KV1], att)
        o1T = pair("o1T", [KV1, J1, TOK], att)
        prob1 = sb("prob1", [P, 2, GH, TOK], F32, att)
        att.close()
        NTR = 2 * NT

        def q_head_half(t):
            return (t - 3) % 8 % 4, 0 if 3 <= t <= 6 else 1

        def split_dst(kvh, i):
            kind, h = SLICES[i]
            if kind == "q":
                return tuple(w[:, h, :, :].rearrange("p c n -> p (c n)") for w in wq)
            if kind == "o":
                return tuple(w[:, bass.ds((kvh % 2) * (G * D) + h * D, D)] for w in wo)
            return tuple(w[:, :, :].rearrange("p c n -> p (c n)") for w in (wk if kind == "k" else wv))

        ORDER = ([("base", c) for c in range(C)] + [("adapt", 0), ("gates", 0), ("up", 0), ("wk", 0), ("wv", 0)]
                 + [("k", 0), ("k", 1), ("v", 0), ("v", 1)]
                 + [("x0", b) for b in range(HT)] + [("wq", c) for c in range(C)] + [("x0", b) for b in range(HT, NT)]
                 + [("hw", 0), ("hw", 1)] + [("wo", j) for j in range(J1)]
                 + [("x1", b) for b in range(HT)] + [("bin", c) for c in range(C)] + [("x1", b) for b in range(HT, NT)]
                 + [("q", i) for i in range(2 * J1)] + [("x2", b) for b in range(NT)])
        NTH = {name: i for i, name in enumerate(ORDER)}

        def split_bank(i):
            return bank[4 + i % 4] if ORDER[i][0] != "x2" else bank[7]

        def split_views(i):
            kind, n = ORDER[i]
            acc = split_bank(i)
            four = acc[:, :].rearrange("p (c n) -> p c n", c=4)
            tok = slice(n * TOK, (n + 1) * TOK)
            half = slice(n * HALF, (n + 1) * HALF)
            if kind == "base":
                return acc[:, :], wb[0][:, n, :], wb[1][:, n, :]
            if kind == "adapt":
                return four, wa[0][:, :, :], wa[1][:, :, :]
            if kind == "gates":
                return acc[:, 0:C * NGT].rearrange("p (c n) -> p c n", c=C), wg[0][:, :, :], wg[1][:, :, :]
            if kind == "up":
                return acc[:, :], wB[0][:, :], wB[1][:, :]
            if kind == "wk":
                return four, wk1[0][:, :, :], wk1[1][:, :, :]
            if kind == "wv":
                return four, wv1[0][:, :, :], wv1[1][:, :, :]
            if kind == "k":
                return acc[:, :], k1T[0][:, half], k1T[1][:, half]
            if kind == "v":
                return four, v1[0][:, n * HT:(n + 1) * HT, :], v1[1][:, n * HT:(n + 1) * HT, :]
            if kind in ("x0", "x1", "x2"):
                return four, xT[0][:, :, tok], xT[1][:, :, tok]
            if kind == "wq":
                return acc[:, :], wq1[0][:, n, :], wq1[1][:, n, :]
            if kind == "hw":
                return acc[:, :], hwT[0][:, :], hwT[1][:, :]
            if kind == "wo":
                return acc[:, :], wo1[0][:, n, :], wo1[1][:, n, :]
            if kind == "bin":
                return acc[:, :], wf1[0][:, n, :], wf1[1][:, n, :]
            half = slice(n // J1 * HALF, (n // J1 + 1) * HALF)
            return acc[:, :], q1T[0][:, n % J1, half], q1T[1][:, n % J1, half]

        N_C = NTH[("hw", 0)]

        block = es.enter_context(nc.Block())

        @block.sync
        def _(sp):
            for b in range(NT):
                sp.dma_start(ctx_nat[:, b, :], ctx_rows[:, b, :]).then_inc(s_ctx_in[b], 16)
                sp.dma_start(xres[:, b, :], x_rows[:, b, :]).then_inc(s_x_in[b], 16)

            def load(kvh, i):
                kind, h = SLICES[i]
                if kind == "o":
                    dst, src = stage[:, i % SLOTS, :], wo_rows[bass.ds(kvh * G + h, 1), :, :].rearrange("a p n -> p (a n)")
                else:
                    dst = stage[:, i % SLOTS, :].rearrange("p (c n) -> p c n", c=C)
                    if kind == "q":
                        src = wq_rows[:, :, bass.ds(kvh * (G * DH) + h * DH, DH)]
                    elif kind == "k":
                        src = wkv_rows[:, :, bass.ds(kvh * DH, DH)]
                    else:
                        src = wkv_rows[:, :, bass.ds(kvh * DH + KVH * DH, DH)]
                sp.dma_start(dst, src).then_inc(s_w_in[i % SLOTS], 16)

            for i in range(NS):
                if i >= SLOTS:
                    sp.wait_ge(s_w_lo, i - SLOTS + 1)
                load(0, i)
            with sp.Fori(1, KVH) as kvh:
                for i in range(NS):
                    sp.wait_ge(s_w_lo, kvh * NS + (i - SLOTS + 1))
                    load(kvh, i)
            sp.wait_ge(s_acc, KVH * STEPS)

            def tiles(w, n):
                return w.rearrange("(i p) n -> p i n", p=P)

            def natural(half, lo, hi):
                return nat[:, half, lo:hi]

            sp.dma_start(natural(0, 0, 4 * D).rearrange("p (i n) -> p i n", i=4), tiles(W_base, 4)).then_inc(s_nat[0], 16)
            sp.dma_start(natural(1, 0, D), A_w.rearrange("e r d -> (e r) d")).then_inc(s_nat[1], 16)
            for i in range(4):
                sp.dma_start(natural(1, D + i * P, D + (i + 1) * P).rearrange("p (e r) -> p e r", e=E),
                             B_w[:, i * P:(i + 1) * P, :].rearrange("e p r -> p e r")).then_inc(s_nat[1], 16)
            sp.wait_ge(s_gzero, 1)
            sp.dma_start(nat[0:E, 1, 2 * D:3 * D], W_gate).then_inc(s_nat[1], 16)
            sp.dma_start(nat[E:E + 1, 1, 2 * D:3 * D], W_thr.rearrange("(a d) -> a d", a=1)).then_inc(s_nat[1], 16)
            sp.wait_ge(s_made, NTH[("base", C - 1)] + 1)
            sp.dma_start(natural(0, 0, D), w_k).then_inc(s_nat[2], 16)
            sp.dma_start(natural(0, D, 2 * D), w_v).then_inc(s_nat[2], 16)
            sp.wait_ge(s_made, NTH[("up", 0)] + 1)
            for j in range(J1):
                sp.dma_start(natural(1, j * D, (j + 1) * D), w_q.rearrange("(g j d) n -> j g d n", j=J1, d=DH1)[j]
                             ).then_inc(s_nat[3], 16)
            sp.wait_ge(s_made, NTH[("wv", 0)] + 1)
            for i in range(4):
                for j in range(J1):
                    sp.dma_start(natural(0, i * D + j * P, i * D + (j + 1) * P).rearrange("p (g d) -> p g d", d=DH1),
                                 w_out[i * P:(i + 1) * P, :].rearrange("p (g j d) -> j p g d", j=J1, d=DH1)[j]
                                 ).then_inc(s_nat[4], 16)
            sp.wait_ge(s_made, NTH[("wq", C - 1)] + 1)
            sp.dma_start(natural(1, 0, 4 * D).rearrange("p (i n) -> p i n", i=4), tiles(w_bin, 4)).then_inc(s_nat[5], 16)
            sp.wait_ge(s_made, NTH[("bin", C - 1)] + 1)
            sp.wait_ge(s_x2, NT)
            sp.dma_start(mask_in[:, :], mask).then_inc(s_small2, 16)
            for b in range(NT):
                sp.wait_ge(s_x4, b + 1)
                sp.dma_start(out.rearrange("b t d -> t b d")[:, b, :], xres[:, b, :]).then_inc(s_store, 16)
            sp.wait_ge(s_store, 16 * NT)

        @block.gpsimd
        def _(pool):
            nc.gpsimd.memset(ident[:, :], 0.0).then_inc(s_ident0, 1)
            pool.wait_ge(s_ident0, 1)
            nc.gpsimd.affine_select(out=ident[:, :], in_=ident[:, :], compare_op=ALU.not_equal, fill=1.0, base=0,
                                    pattern=[[-1, P]], channel_multiplier=1).then_inc(s_ident, 1)
            pool.dma_start(gate_raw[:, 0:2], g_xattn.partition_broadcast(P)).then_inc(s_small_in, 16)
            pool.dma_start(gate_raw[:, 2:4], g_ffn.partition_broadcast(P)).then_inc(s_small_in, 16)
            pool.dma_start(bo_bc[:, :], bo.partition_broadcast(P)).then_inc(s_small_in, 16)
            pool.dma_start(bias_nat[0:HEADS, :], bq.rearrange("(h d) -> h d", d=DH)).then_inc(s_small_in, 16)
            pool.dma_start(bias_nat[HEADS:, :], bkv.rearrange("(h d) -> h d", d=DH)).then_inc(s_small_in, 16)
            pool.wait_ge(s_rstd, 2)
            nc.gpsimd.tensor_tensor(rstd[:, :], rstd[:, :], power[:, :], ALU.pow).then_inc(s_pow, 1)
            pool.wait_ge(s_bo, 1)
            for b in range(NT):
                pool.wait_ge(s_xn, b + 1)
                nc.gpsimd.tensor_tensor(xres[:, b, :], xres[:, b, :], bo_bc[:, :], ALU.add).then_inc(s_xres, 1)

            def step(k, t, attend_next, split):
                if attend_next:
                    n = k * STEPS + t + 1
                    pool.wait_ge(s_rinv, n + 1)
                    nc.gpsimd.tensor_tensor(prob[:, :, :], prob[:, :, :], rinv[:, :].unsqueeze(2).broadcast_to([P, G, TOK]),
                                            ALU.mult).then_inc(s_norm, 1)
                if split:
                    for i in SPLIT_AT[t]:
                        hi, lo = split_dst(k + 1, i)
                        pool.wait_ge(s_w_hi, (k + 1) * NS + i + 1)
                        nc.gpsimd.tensor_tensor(lo, stage[:, i % SLOTS, :], hi.bitcast(F32), ALU.subtract).then_inc(s_w_lo, 1)

            for t in range(STEPS):
                step(-1, t, t == STEPS - 1, True)
            with pool.Fori(0, KVH - 1) as k:
                for t in range(STEPS):
                    step(k, t, True, True)
            for t in range(STEPS):
                step(KVH - 1, t, t < STEPS - 1, False)

            pool.wait_ge(s_acc, KVH * STEPS)
            nc.gpsimd.memset(nat[0:NGT, 1, 2 * D:3 * D], 0.0).then_inc(s_gzero, 1)
            pool.dma_start(b_base_bc[:, :], b_base.partition_broadcast(P)).then_inc(s_bb, 16)
            pool.dma_start(nb_thr[:, :], b_thr.partition_broadcast(P)).then_inc(s_bb, 16)
            pool.wait_ge(s_eps, 1)
            nc.gpsimd.tensor_tensor(rstd[:, :], rstd[:, :], power[:, :], ALU.pow).then_inc(s_pow2, 1)
            pool.wait_ge(s_bbg, 1)
            for b in range(NT):
                pool.wait_ge(s_xn2, b + 1)
                nc.gpsimd.tensor_tensor(xres[:, b, :], xres[:, b, :], b_base_bc[:, :], ALU.add).then_inc(s_xb, 1)

            def inverse_root(n):
                pool.wait_ge(s_eps, n + 2)
                col = slice(n % NT, n % NT + 1)
                nc.gpsimd.tensor_tensor(rstd[:, col], rstd[:, col], power[:, 0:1], ALU.pow).then_inc(s_pow2, 1)

            for b in range(NT):
                inverse_root(b)

            pool.wait_ge(s_made, NTH[("q", 2 * J1 - 1)] + 1)
            nc.gpsimd.memset(group_of[:, :], 1.0).then_inc(s_grp0, 1)
            pool.wait_ge(s_grp0, 1)
            nc.gpsimd.affine_select(out=group_of[:, :], in_=group_of[:, :], compare_op=ALU.is_ge, fill=0.0, base=0,
                                    pattern=[[-DH1, G1]], channel_multiplier=1).then_inc(s_grp1, 1)
            pool.wait_ge(s_grp1, 1)
            nc.gpsimd.affine_select(out=group_of[:, :], in_=group_of[:, :], compare_op=ALU.is_ge, fill=0.0, base=DH1 - 1,
                                    pattern=[[DH1, G1]], channel_multiplier=-1).then_inc(s_grp, 1)
            for part in vd:
                nc.gpsimd.memset(part[:, :, :, :].bitcast(F32), 0.0).then_inc(s_vz, 1)

            def k_by_group(B, part):
                b, gh = B // 2, B % 2
                if B >= 2:
                    pool.wait_ge(s_s1, J1 * (B - 1))
                nc.gpsimd.tensor_tensor(kd[part][:, gh, :, :],
                                        k1T[part][:, b * TOK:(b + 1) * TOK].bitcast(F32).unsqueeze(1).broadcast_to([KV1, GH, TOK]),
                                        group_of[:, gh * GH:(gh + 1) * GH].unsqueeze(2).broadcast_to([KV1, GH, TOK]),
                                        ALU.mult).then_inc(s_kd, 1)

            def v_by_group(B, part):
                b, gh = B // 2, B % 2
                if B >= 2:
                    pool.wait_ge(s_pv1, GH * (B - 1))
                step_ = KV1 + DH1
                flat = vd[part][:, gh, :, :].rearrange("p g n -> p (g n)")
                for i in range(GH):
                    at = i * step_ + gh * GH * DH1
                    ins = nc.gpsimd.tensor_copy(flat[:, at:at + DH1],
                                                v1[part][:, b, (gh * GH + i) * DH1:(gh * GH + i + 1) * DH1].bitcast(F32))
                ins.then_inc(s_vd, 1)

            def norm1(u):
                pool.wait_ge(s_r1, u + 1)
                nc.gpsimd.tensor_tensor(prob1[:, u % 2, :, :], prob1[:, u % 2, :, :],
                                        rinv1[:, u % 2, :].unsqueeze(2).broadcast_to([P, GH, TOK]), ALU.mult).then_inc(s_n1, 1)

            pool.wait_ge(s_grp, 1)
            for B in (0, 1):
                for part in (0, 1):
                    k_by_group(B, part)
            pool.wait_ge(s_vz, 2)
            for B in (0, 1):
                for part in (0, 1):
                    v_by_group(B, part)
            norm1(0)
            norm1(1)
            for u in range(UNITS):
                if u + 2 < UNITS:
                    norm1(u + 2)
                B = u // J1
                if u % J1 in (2, 3) and B + 2 < 2 * NT:
                    k_by_group(B + 2, u % J1 - 2)
                if u % J1 in (0, 1) and B >= 2:
                    v_by_group(B, u % J1)
                if u % 8 == 6 and u >= 8:
                    inverse_root(NT + u // 8 - 1)
            inverse_root(NT + NT - 1)

        @block.scalar
        def _(act):
            act.wait_ge(s_small_in, 80)
            nc.scalar.activation(gate[:, :], gate_raw[:, :], ACT.Tanh).then_inc(s_gate, 1)
            act.wait_ge(s_ident, 1)
            nc.scalar.activation(ident_r[:, :], ident[:, :], ACT.Copy).then_inc(s_idr, 1)
            for i in range(NTR):
                act.wait_ge(s_tr, i + 1)
                dst = (cT if i < NT else xT)[0][:, :, (i % NT) * TOK:(i % NT + 1) * TOK]
                nc.scalar.activation(dst, bank[4 + i % 2][:, :].rearrange("p (c n) -> p c n", c=C), ACT.Copy).then_inc(s_tr_hi, 1)

            def step(k, t, attend_next, project, split, started=True):
                g = k * STEPS + t
                n = g + 1
                b = n % NT if isinstance(n, int) else (t + 1) % NT
                if attend_next and started:
                    o_hi(n - 1)
                if attend_next:
                    act.wait_ge(s_nmax, n + 1)
                    for j in range(G):
                        e = nc.scalar.activation(prob[:, j, :], ps_s[:, j * TOK:(j + 1) * TOK], ACT.Exp, bias=nmax[:, 1, j:j + 1],
                                                 scale=SCALE0, accum_out=rsum[:, j:j + 1])
                    e.then_inc(s_exp, 1)
                if split:
                    for i in SPLIT_AT[t]:
                        kind, h = SLICES[i]
                        act.wait_ge(s_w_in[i % SLOTS], (k + 1) * (16 * NS // SLOTS) + 16 * (i // SLOTS + 1))
                        if started:
                            if kind == "q":
                                act.wait_ge(s_qproj, g + 5)
                            elif kind == "k":
                                act.wait_ge(s_kproj, 2 * k + 2)
                            elif kind == "v":
                                act.wait_ge(s_vproj, 2 * k + 2)
                            else:
                                act.wait_ge(s_out, k * STEPS + 1)
                        nc.scalar.activation(split_dst(k + 1, i)[0], stage[:, i % SLOTS, :], ACT.Copy).then_inc(s_w_hi, 1)
                if project:
                    h, half = q_head_half(t)
                    act.wait_ge(s_qproj, g + 6)
                    if t == 3:
                        act.wait_ge(s_bias, k + 2)
                    nc.scalar.activation(qT[0][:, h, half * HALF:(half + 1) * HALF], ps_q[:, :], ACT.Identity,
                                         bias=bias[:, h:h + 1]).then_inc(s_q_hi, 1)
                if attend_next:
                    act.wait_ge(s_ptr, n + 1)
                    nc.scalar.activation(pT[0][:, :], ps_pt[:, :], ACT.Copy).then_inc(s_pt_hi, 1)
                if t == 3 and started:
                    act.wait_ge(s_vtr, 2 * k + 2)
                    nc.scalar.activation(v[0][:, 4:8, :].rearrange("p b d -> p (b d)"), ps_vt[:, :], ACT.Copy).then_inc(s_v_hi, 1)
                if t == 7 and attend_next:
                    act.wait_ge(s_vtr, 2 * k + 3)
                    nc.scalar.activation(v[0][:, 0:4, :].rearrange("p b d -> p (b d)"), ps_vt[:, :], ACT.Copy).then_inc(s_v_hi, 1)
                if project and t in (0, 4):
                    c, half = (2, 1) if t == 0 else (3, 0)
                    act.wait_ge(s_kproj, 2 * k + c)
                    if not started:
                        act.wait_ge(s_xres, NT)
                    nc.scalar.activation(kT[0][:, half * HALF:(half + 1) * HALF], ps_kv[:, :], ACT.Identity,
                                         bias=bias[:, G:G + 1]).then_inc(s_k_hi, 1)
                if project and t in (2, 6):
                    c = 2 if t == 2 else 3
                    act.wait_ge(s_vproj, 2 * k + c)
                    nc.scalar.activation(vT[:, :, :].rearrange("p b t -> p (b t)"), ps_kv[:, :], ACT.Identity,
                                         bias=bias[:, G + 1:G + 2]).then_inc(s_vt, 1)

            def o_hi(n):
                act.wait_ge(s_pv, n + 1)
                nc.scalar.activation(oT[0][:, :, :].rearrange("p g t -> p (g t)"), ps_o[:, :], ACT.Copy).then_inc(s_o_hi, 1)

            for t in range(STEPS):
                step(-1, t, t == STEPS - 1, t >= 3, True, started=False)
            with act.Fori(0, KVH - 1) as k:
                for t in range(STEPS):
                    step(k, t, True, True, True)
            for t in range(STEPS):
                step(KVH - 1, t, t < STEPS - 1, t < 3, False)
            o_hi(KVH * STEPS - 1)

            def hi(i):
                act.wait_ge(s_made, i + 1)
                acc, dst, _ = split_views(i)
                if ORDER[i][0] == "q":
                    nc.scalar.activation(dst, acc, ACT.Copy, scale=SCALE1).then_inc(s_hi, 1)
                else:
                    nc.scalar.activation(dst, acc, ACT.Copy).then_inc(s_hi, 1)

            act.wait_ge(s_acc, KVH * STEPS)
            for i in range(NTH[("x0", HT - 1)] + 1):
                hi(i)

            def gate_exps(hf):
                act.wait_ge(s_el, hf + 1)
                if hf == 0:
                    act.wait_ge(s_bbg, 2)
                nc.scalar.activation(gl[:, 1, :], gl[:, 0, :], ACT.Exp)
                nc.scalar.activation(gl[:, 2, 0:HT], bank[2 + hf][:, 0:HT * NGT].rearrange("p (t n) -> p t n", n=NGT)[:, :, E],
                                     ACT.Exp, scale=-1.0, bias=nb_thr[:, :]).then_inc(s_ee, 1)

            for i in range(NTH[("wq", 0)], NTH[("wq", C - 1)] + 1):
                hi(i)
            gate_exps(0)
            for i in range(NTH[("x0", HT)], NTH[("x0", NT - 1)] + 1):
                hi(i)
            gate_exps(1)
            for i in range(NTH[("hw", 0)], NTH[("x2", 0)]):
                hi(i)

            def exp1(u):
                act.wait_ge(s_m1, u + 1)
                if u >= 2:
                    act.wait_ge(s_t1, u - 1)
                for i in range(GH):
                    e = nc.scalar.activation(prob1[:, u % 2, i, :], bank[u % 2][:, i * TOK:(i + 1) * TOK], ACT.Exp,
                                             bias=nmax1[:, u % 2, i:i + 1], accum_out=rsum1[:, u % 2, i:i + 1])
                e.then_inc(s_e1, 1)

            def o1_hi(b):
                act.wait_ge(s_pv1, 2 * GH * (b + 1))
                nc.scalar.activation(o1T[0][:, :, :].rearrange("p j t -> p (j t)"), bank[4][:, :], ACT.Copy).then_inc(s_o1h, 1)

            exp1(0)
            exp1(1)
            for u in range(UNITS):
                if u % 8 == 4 and u >= 8:
                    o1_hi(u // 8 - 1)
                if u + 2 < UNITS:
                    exp1(u + 2)
                act.wait_ge(s_t1, u + 1)
                B = u // J1
                nc.scalar.activation(p1T[0][:, B % 2, :, (u % J1) * TOK:(u % J1 + 1) * TOK],
                                     bank[2 + u % 2][:, :].rearrange("p (g n) -> p g n", g=GH), ACT.Copy).then_inc(s_t1h, 1)
                if u % 8 == 1 and u >= 16:
                    hi(NTH[("x2", u // 8 - 2)])
            hi(NTH[("x2", NT - 2)])
            o1_hi(NT - 1)
            hi(NTH[("x2", NT - 1)])

        @block.vector
        def _(dve):
            for b in range(NT):
                dve.wait_ge(s_x_in[b], 16)
                nc.vector.bn_stats(stats[:, b, :], xres[:, b, :]).then_inc(s_stats, 1)
            for b in range(NT):
                dve.wait_ge(s_stats, b + 1)
                nc.vector.bn_aggr(moments[:, b, :], stats[:, b, :]).then_inc(s_moments, 1)
            dve.wait_ge(s_moments, NT)
            nc.vector.tensor_scalar(rstd[:, :], moments[:, :, 1], EPS, None, ALU.add).then_inc(s_rstd, 1)
            nc.vector.memset(power[:, :], -0.5).then_inc(s_rstd, 1)
            dve.wait_ge(s_pow, 1)
            for b in range(NT):
                nc.vector.tensor_scalar(xn_nat[:, b, :], xres[:, b, :], moments[:, b, 0:1], rstd[:, b:b + 1],
                                        ALU.subtract, ALU.mult).then_inc(s_xn, 1)
            dve.wait_ge(s_gate, 1)
            nc.vector.tensor_scalar(bo_bc[:, :], bo_bc[:, :], gate[:, 0:1], None, ALU.mult).then_inc(s_bo, 1)
            for i in range(NTR):
                dve.wait_ge(s_tr_hi, i + 1)
                cols = slice((i % NT) * TOK, (i % NT + 1) * TOK)
                hi, lo = cT if i < NT else xT
                nc.vector.tensor_tensor(lo[:, :, cols], bank[4 + i % 2][:, :].rearrange("p (c n) -> p c n", c=C),
                                        hi[:, :, cols].bitcast(F32), ALU.subtract).then_inc(s_tr_lo, 1)
            dve.wait_ge(s_bias_tr, 1)
            cols = bias_all[:, :].rearrange("p (k j) -> p k j", j=G + 2)
            nc.vector.tensor_copy(cols[:, :, 0:G], bank[6][:, 0:HEADS].rearrange("p (k j) -> p k j", j=G))
            nc.vector.tensor_copy(cols[:, :, G], bank[6][:, HEADS:HEADS + KVH])
            nc.vector.tensor_copy(cols[:, :, G + 1], bank[6][:, HEADS + KVH:HEADS + 2 * KVH]).then_inc(s_bias_all, 1)
            dve.wait_ge(s_bias_all, 1)

            def minus_hi(lo, acc, hi, bias_col=None):
                if bias_col is None:
                    return nc.vector.tensor_tensor(lo, acc, hi.bitcast(F32), ALU.subtract)
                return nc.vector.scalar_tensor_tensor(lo, acc, bias_col, hi.bitcast(F32), ALU.add, ALU.subtract)

            def step(k, t, attend_next, project, started=True, attend=True):
                g = k * STEPS + t
                n = g + 1
                if t == 3 and project:
                    if started:
                        dve.wait_ge(s_vt, 2 * k + 2)
                        dve.wait_ge(s_q_lo, g + 5)
                    nc.vector.tensor_copy(bias[:, :], bias_all[:, bass.ds((k + 1) * (G + 2), G + 2)]).then_inc(s_bias, 1)
                    dve.wait_ge(s_bias, k + 2)
                if attend_next:
                    dve.wait_ge(s_scores, n + 1)
                    nc.vector.tensor_reduce(nmax[:, 0, :], ps_s[:, :].rearrange("p (g m) -> p g m", g=G), AX.X, ALU.max,
                                            negate=True).then_inc(s_max, 1)
                    dve.wait_ge(s_max, n + 1)
                    nc.vector.tensor_scalar(nmax[:, 1, :], nmax[:, 0, :], SCALE0, None, ALU.mult).then_inc(s_nmax, 1)
                if attend_next and started:
                    o_lo(n - 1)
                if attend_next:
                    dve.wait_ge(s_exp, n + 1)
                    nc.vector.reciprocal(rinv[:, :], rsum[:, :]).then_inc(s_rinv, 1)
                if project:
                    h, half = q_head_half(t)
                    cols = slice(half * HALF, (half + 1) * HALF)
                    dve.wait_ge(s_q_hi, g + 6)
                    minus_hi(qT[1][:, h, cols], ps_q[:, :], qT[0][:, h, cols], bias[:, h:h + 1]).then_inc(s_q_lo, 1)
                if attend_next:
                    dve.wait_ge(s_pt_hi, n + 1)
                    minus_hi(pT[1][:, :], ps_pt[:, :], pT[0][:, :]).then_inc(s_pt_lo, 1)
                if started and attend:
                    if k is not None and t is not None:
                        add_out(g, t)
                if (t == 3 and started) or (t == 7 and attend_next):
                    c, bs = (2, slice(4, 8)) if t == 3 else (3, slice(0, 4))
                    dve.wait_ge(s_v_hi, 2 * k + c)
                    minus_hi(v[1][:, bs, :].rearrange("p b d -> p (b d)"), ps_vt[:, :],
                             v[0][:, bs, :].rearrange("p b d -> p (b d)")).then_inc(s_v_lo, 1)
                if project and t in (0, 4):
                    c, half = (2, 1) if t == 0 else (3, 0)
                    cols = slice(half * HALF, (half + 1) * HALF)
                    dve.wait_ge(s_k_hi, 2 * k + c)
                    minus_hi(kT[1][:, cols], ps_kv[:, :], kT[0][:, cols], bias[:, G:G + 1]).then_inc(s_k_lo, 1)

            def o_lo(n):
                dve.wait_ge(s_o_hi, n + 1)
                minus_hi(oT[1][:, :, :].rearrange("p g t -> p (g t)"), ps_o[:, :],
                         oT[0][:, :, :].rearrange("p g t -> p (g t)")).then_inc(s_o_lo, 1)

            def add_out(g, b):
                dve.wait_ge(s_out, g + 1)
                if isinstance(g, int):
                    dve.wait_ge(s_xres, b + 1)
                nc.vector.scalar_tensor_tensor(xres[:, b, :], ps_out[:, :], gate[:, 0:1], xres[:, b, :],
                                               ALU.mult, ALU.add).then_inc(s_acc, 1)

            for t in range(STEPS):
                step(-1, t, t == STEPS - 1, t >= 3, started=False)
            dve.wait_ge(s_xres, NT)
            with dve.Fori(0, KVH - 1) as k:
                for t in range(STEPS):
                    step(k, t, True, True)
            for t in range(STEPS):
                if t == STEPS - 1:
                    o_lo(KVH * STEPS - 1)
                step(KVH - 1, t, t < STEPS - 1, t < 3)

            links = [0]

            def link(ins):
                links[0] += 1
                ins.then_inc(s_chain, 1)
                dve.wait_ge(s_chain, links[0])

            dve.wait_ge(s_acc, KVH * STEPS)
            for b in range(NT):
                ins = nc.vector.bn_stats(stats[:, b, :], xres[:, b, :])
            link(ins)
            for b in range(NT):
                ins = nc.vector.bn_aggr(moments[:, b, :], stats[:, b, :])
            link(ins)
            nc.vector.tensor_scalar(rstd[:, :], moments[:, :, 1], EPS, None, ALU.add).then_inc(s_eps, 1)
            dve.wait_ge(s_bb, 32)
            nc.vector.tensor_scalar(b_base_bc[:, :], b_base_bc[:, :], gate[:, 2:3], None, ALU.mult).then_inc(s_bbg, 1)
            nc.vector.tensor_scalar(nb_thr[:, :], nb_thr[:, :], -1.0, None, ALU.mult).then_inc(s_bbg, 1)

            def lo(i):
                dve.wait_ge(s_hi, i + 1)
                acc, hi, dst = split_views(i)
                if ORDER[i][0] == "q":
                    nc.vector.scalar_tensor_tensor(dst, acc, SCALE1, hi.bitcast(F32), ALU.mult, ALU.subtract).then_inc(s_lo, 1)
                else:
                    nc.vector.tensor_tensor(dst, acc, hi.bitcast(F32), ALU.subtract).then_inc(s_lo, 1)

            def normalise(n, made_before):
                b = n % NT
                if made_before:
                    dve.wait_ge(s_made, made_before)
                nc.vector.tensor_scalar(xn[:, n % 2, :], xres[:, b, :], moments[:, b, 0:1], rstd[:, b:b + 1],
                                        ALU.subtract, ALU.mult).then_inc(s_xn2, 1)

            def tile_stats(b):
                link(nc.vector.bn_stats(stats[:, b, :], xres[:, b, :]))
                link(nc.vector.bn_aggr(moments[:, b, :], stats[:, b, :]))
                nc.vector.tensor_scalar(rstd[:, b:b + 1], moments[:, b, 1:2], EPS, None, ALU.add).then_inc(s_eps, 1)

            dve.wait_ge(s_pow2, 1)
            normalise(0, 0)
            normalise(1, 0)
            for i in range(NTH[("x0", 0)]):
                lo(i)
            for b in range(HT):
                lo(NTH[("x0", b)])
                normalise(b + 2, NTH[("x0", b)] + 1)

            def gate_logits(hf):
                dve.wait_ge(s_h, hf + 1)
                g3 = bank[2 + hf][:, 0:HT * NGT].rearrange("p (t n) -> p t n", n=NGT)[:, :, 0:E]
                link(nc.vector.tensor_reduce(gl[:, 3, 0:HT], g3, AX.X, ALU.max, negate=True))
                nc.vector.tensor_tensor(gl[:, 0, :].rearrange("p (t e) -> p t e", e=E), g3,
                                        gl[:, 3, 0:HT].unsqueeze(2).broadcast_to([P, HT, E]), ALU.add).then_inc(s_el, 1)

            def weigh(hf):
                dve.wait_ge(s_ee, hf + 1)

                def te(i):
                    return gl[:, i, :].rearrange("p (t e) -> p t e", e=E)

                def over_e(i):
                    return gl[:, i, 0:HT].unsqueeze(2).broadcast_to([P, HT, E])

                link(nc.vector.tensor_reduce(gl[:, 4, 0:HT], te(1), AX.X, ALU.add))
                link(nc.vector.reciprocal(gl[:, 5, 0:HT], gl[:, 4, 0:HT]))
                link(nc.vector.tensor_tensor(te(6), te(1), over_e(5), ALU.mult))
                link(nc.vector.tensor_scalar(gl[:, 7, 0:HT], gl[:, 2, 0:HT], 1.0, None, ALU.add))
                link(nc.vector.reciprocal(gl[:, 8, 0:HT], gl[:, 7, 0:HT]))
                link(nc.vector.tensor_scalar(gl[:, 9, 0:HT], gl[:, 8, 0:HT], THR_MAX, None, ALU.mult))
                link(nc.vector.tensor_tensor(te(10), te(6), over_e(9), ALU.subtract))
                link(nc.vector.tensor_scalar(gl[:, 11, :], gl[:, 10, :], 0.0, None, ALU.max))
                link(nc.vector.tensor_reduce(gl[:, 12, 0:HT], te(11), AX.X, ALU.add))
                link(nc.vector.scalar_tensor_tensor(gl[:, 13, 0:HT], gl[:, 12, 0:HT], 0.0, gl[:, 12, 0:HT],
                                                    ALU.is_equal, ALU.add))
                link(nc.vector.reciprocal(gl[:, 14, 0:HT], gl[:, 13, 0:HT]))
                link(nc.vector.tensor_tensor(te(15), te(11), over_e(14), ALU.mult))
                if hf:
                    dve.wait_ge(s_made, NTH[("hw", 0)] + 1)
                nc.vector.scalar_tensor_tensor(hw[:, :, :].rearrange("p t (e r) -> p (t e) r", r=R),
                                               bank[hf][:, :].rearrange("p (n r) -> p n r", r=R), ADAPT,
                                               gl[:, 15, :].unsqueeze(2).broadcast_to([P, HT * E, R]),
                                               ALU.mult, ALU.mult).then_inc(s_hw, 1)

            for c in range(C):
                lo(NTH[("wq", c)])
            gate_logits(0)
            weigh(0)
            for b in range(HT, NT):
                lo(NTH[("x0", b)])
                if b + 2 < NT:
                    normalise(b + 2, NTH[("x0", b)] + 1)
            gate_logits(1)
            lo(NTH[("hw", 0)])
            weigh(1)

            def add_ffn0(b):
                dve.wait_ge(s_f0, b + 1)
                dve.wait_ge(s_xb, b + 1)
                nc.vector.scalar_tensor_tensor(xres[:, b, :], bank[0 if b % 2 == 0 else 2][:, :], gate[:, 2:3], xres[:, b, :],
                                               ALU.mult, ALU.add).then_inc(s_x2, 1)
                dve.wait_ge(s_x2, b + 1)
                tile_stats(b)

            for b in range(HT):
                add_ffn0(b)
            lo(NTH[("hw", 1)])
            for b in (0, 1):
                dve.wait_ge(s_pow2, b + 2)
                normalise(NT + b, NTH[("x0", NT - 2 + b)] + 1)
            for j in range(J1):
                lo(NTH[("wo", j)])
            for b in range(HT, NT):
                add_ffn0(b)
                lo(NTH[("x1", b - HT)])
                dve.wait_ge(s_pow2, b - HT + 2 + 2)
                normalise(NT + b - HT + 2, NTH[("x1", b - HT)] + 1)

            dve.wait_ge(s_nat[5], 16)
            link(nc.vector.tensor_reduce(gl[:, 0, 0:4], nat[:, 1, :].rearrange("p (i n) -> p i n", i=4), AX.X, ALU.add,
                                         apply_absolute_value=True))
            link(nc.vector.tensor_scalar(gl[:, 1, 0:4], gl[:, 0, 0:4], -1.0 / D, None, ALU.mult))
            t1 = hw[:, :, :].rearrange("p t n -> p (t n)")
            dve.wait_ge(s_made, NTH[("hw", 1)] + 1)
            for i in range(4):
                w = nat[:, 1, i * D:(i + 1) * D]
                link(nc.vector.tensor_scalar(t1, w, 0.0, None, ALU.is_gt))
                link(nc.vector.scalar_tensor_tensor(t1, w, 0.0, t1, ALU.is_lt, ALU.subtract))
                link(nc.vector.tensor_scalar(w, w, -1.0, 1.0, ALU.max, ALU.min))
                link(nc.vector.scalar_tensor_tensor(t1, t1, gl[:, 1, i:i + 1], w, ALU.mult, ALU.subtract))
                ins = nc.vector.tensor_tensor(w, t1, w, ALU.add)
                if i < 3:
                    link(ins)
            ins.then_inc(s_bin, 1)
            for c in range(C):
                lo(NTH[("bin", c)])
            for b in range(HT, NT):
                lo(NTH[("x1", b)])
                if b + 2 < NT:
                    dve.wait_ge(s_pow2, b + 2 + 2)
                    normalise(NT + b + 2, NTH[("x1", b)] + 1)
            for i in range(2 * J1):
                lo(NTH[("q", i)])

            dve.wait_ge(s_small2, 16)
            for i in range(GH):
                ins = nc.vector.tensor_scalar(negmask[:, i, :], mask_in[:, :], MASKED, -MASKED, ALU.mult, ALU.add)
            ins.then_inc(s_mask, 1)

            def softmax1(u):
                dve.wait_ge(s_s1, u + 1)
                nc.vector.tensor_reduce(nmax1[:, u % 2, :], bank[u % 2][:, :].rearrange("p (g m) -> p g m", g=GH), AX.X, ALU.max,
                                        negate=True).then_inc(s_m1, 1)
                dve.wait_ge(s_e1, u + 1)
                if u >= 2:
                    dve.wait_ge(s_n1, u - 1)
                nc.vector.reciprocal(rinv1[:, u % 2, :], rsum1[:, u % 2, :]).then_inc(s_r1, 1)

            def o1_lo(b):
                dve.wait_ge(s_o1h, b + 1)
                minus_hi(o1T[1][:, :, :].rearrange("p j t -> p (j t)"), bank[4][:, :],
                         o1T[0][:, :, :].rearrange("p j t -> p (j t)")).then_inc(s_o1l, 1)

            def add_out1(b):
                dve.wait_ge(s_out1, b + 1)
                nc.vector.scalar_tensor_tensor(xres[:, b, :], bank[5][:, :], gate[:, 1:2], xres[:, b, :],
                                               ALU.mult, ALU.add).then_inc(s_x3, 1)
                dve.wait_ge(s_x3, b + 1)
                tile_stats(b)

            def norm_x3(b):
                dve.wait_ge(s_pow2, 1 + NT + b + 1)
                normalise(2 * NT + b, NTH[("x1", NT - 2 + b)] + 1 if b < 2 else NTH[("x2", b - 2)] + 1)

            def add_ffn1(b):
                dve.wait_ge(s_f1, b + 1)
                nc.vector.scalar_tensor_tensor(xres[:, b, :], bank[6][:, :], gate[:, 3:4], xres[:, b, :],
                                               ALU.mult, ALU.add).then_inc(s_x4, 1)

            softmax1(0)
            softmax1(1)
            for u in range(UNITS):
                if u % 8 == 4 and u >= 8:
                    o1_lo(u // 8 - 1)
                if u + 2 < UNITS:
                    softmax1(u + 2)
                dve.wait_ge(s_t1h, u + 1)
                B = u // J1
                cols = slice((u % J1) * TOK, (u % J1 + 1) * TOK)
                nc.vector.tensor_tensor(p1T[1][:, B % 2, :, cols], bank[2 + u % 2][:, :].rearrange("p (g n) -> p g n", g=GH),
                                        p1T[0][:, B % 2, :, cols].bitcast(F32), ALU.subtract).then_inc(s_t1l, 1)
                if u % 8 == 5 and u >= 8:
                    add_out1(u // 8 - 1)
                if u % 8 == 7 and u >= 8:
                    norm_x3(u // 8 - 1)
                if u % 8 == 1 and u >= 16:
                    lo(NTH[("x2", u // 8 - 2)])
                if u % 8 == 2 and u >= 16:
                    add_ffn1(u // 8 - 2)
            lo(NTH[("x2", NT - 2)])
            add_ffn1(NT - 2)
            o1_lo(NT - 1)
            add_out1(NT - 1)
            norm_x3(NT - 1)
            lo(NTH[("x2", NT - 1)])
            add_ffn1(NT - 1)

        @block.tensor
        def _(pe):
            pe.wait_ge(s_ident, 1)
            for i in range(NTR):
                b = i % NT
                if i < NT:
                    pe.wait_ge(s_ctx_in[b], 16)
                else:
                    pe.wait_ge(s_xn, b + 1)
                if i >= 2:
                    pe.wait_ge(s_tr_lo, i - 1)
                src = ctx_nat if i < NT else xn_nat
                for c in range(C):
                    mm = nc.tensor.transpose(bank[4 + i % 2][:, c * P:(c + 1) * P], src[:, b, c * P:(c + 1) * P], ident[:, :])
                mm.then_inc(s_tr, 1)
            pe.wait_ge(s_small_in, 80)
            nb = HEADS + 2 * KVH
            nc.tensor.transpose(bank[6][:, 0:nb], bias_nat[:, :], ident[0:nb, 0:nb]).then_inc(s_bias_tr, 1)

            def product(acc, pairs):
                todo = [(st[a], mv[b]) for st, mv in pairs for a, b in ((1, 0), (0, 1), (0, 0))]
                for i, (st, mv) in enumerate(todo):
                    mm = nc.tensor.matmul(acc, st, mv, start=(i == 0), stop=(i == len(todo) - 1))
                return mm

            def part(acc, pairs, first, last):
                todo = [(st[a], mv[b]) for st, mv in pairs for a, b in ((1, 0), (0, 1), (0, 0))]
                for i, (st, mv) in enumerate(todo):
                    mm = nc.tensor.matmul(acc, st, mv, start=(first and i == 0), stop=(last and i == len(todo) - 1))
                return mm

            def both(pair, *index):
                return [a[index] for a in pair]

            def step(k, t, attend_next, project, started=True, attend=True, split=True):
                g = k * STEPS + t
                n = g + 1
                b = (t + 1) % NT
                if attend_next:
                    if started:
                        pe.wait_ge(s_exp, n)
                    if b == 0:
                        pe.wait_ge(s_q_lo, k * STEPS + 12)
                        pe.wait_ge(s_k_lo, 2 * k + 3)
                    if b == 4:
                        pe.wait_ge(s_q_lo, k * STEPS + 8)
                        pe.wait_ge(s_k_lo, 2 * k + 2)
                    tok = slice(b * TOK, (b + 1) * TOK)
                    for j in range(G):
                        mm = product(ps_s[:, j * TOK:(j + 1) * TOK], [(both(qT, slice(None), j, tok), both(kT, slice(None), tok))])
                    mm.then_inc(s_scores, 1)
                if project:
                    h, half = q_head_half(t)
                    cols = slice(half * HALF, (half + 1) * HALF)
                    if t == 3 and not started:
                        pe.wait_ge(s_tr_lo, NTR)
                    if 3 <= t <= 6:
                        pe.wait_ge(s_w_lo, (k + 1) * NS + SLICES.index(("q", h)) + 1)
                    if started or t > 3:
                        pe.wait_ge(s_q_lo, g + 5)
                    product(ps_q[:, :], [(both(wq, slice(None), h, c, slice(None)), both(xT, slice(None), c, cols))
                                         for c in range(C)]).then_inc(s_qproj, 1)

                def out_part(js):
                    m = part(ps_out[:, :], [(both(oT, slice(None), j, slice(None)),
                                             both(wo, slice(None), bass.ds((k % 2) * (G * D) + j * D, D))) for j in js],
                             js[0] == 0, js[-1] == G - 1)
                    if js[-1] == G - 1:
                        m.then_inc(s_out, 1)

                if started and attend:
                    if t == 0:
                        pe.wait_ge(s_w_lo, (k + 1) * NS)
                        if not isinstance(k, int):
                            pass
                    pe.wait_ge(s_o_lo, g + 1)
                    if t > 0:
                        pe.wait_ge(s_acc, g)
                    else:
                        pe.wait_ge(s_nmax, g + 2)
                    out_part([0, 1])
                if attend_next:
                    if started:
                        pe.wait_ge(s_pt_lo, n)
                    pe.wait_ge(s_norm, n + 1)
                    for j in range(G):
                        mm = nc.tensor.transpose(ps_pt[:, j * TOK:(j + 1) * TOK], prob[:, j, :], ident[:, :])
                    mm.then_inc(s_ptr, 1)
                if started and attend:
                    out_part([2, 3])
                if project:
                    key = t in (3, 4, 7, 0)
                    first = t in (3, 7, 1, 5)
                    half = 0 if 3 <= t <= 6 else 1
                    w = wk if key else wv
                    if t == 3:
                        pe.wait_ge(s_w_lo, (k + 1) * NS + SLICES.index(("k", 0)) + 1)
                        if started:
                            pe.wait_ge(s_vt, 2 * k + 2)
                    if t == 7:
                        pe.wait_ge(s_vt, 2 * k + 3)
                    if t == 5:
                        pe.wait_ge(s_w_lo, (k + 1) * NS + SLICES.index(("v", 0)) + 1)
                        pe.wait_ge(s_k_lo, 2 * k + 3)
                    if t == 1:
                        pe.wait_ge(s_k_lo, 2 * k + 2)
                    mm = part(ps_kv[:, :], [(both(w, slice(None), c, slice(None)), both(xT if False else cT, slice(None), c, slice(half * HALF, (half + 1) * HALF)))
                                            for c in ((0, 1) if first else (2, 3))], first, not first)
                    if not first:
                        mm.then_inc(s_kproj if key else s_vproj, 1)
                if (t == 3 and started) or (t == 7 and attend_next):
                    c = 2 if t == 3 else 3
                    pe.wait_ge(s_vt, 2 * k + c)
                    if started:
                        pe.wait_ge(s_v_lo, 2 * k + c - 1)
                    for i in range(4):
                        mm = nc.tensor.transpose(ps_vt[:, i * DH:(i + 1) * DH], vT[:, i, :], ident[:, :])
                    mm.then_inc(s_vtr, 1)
                if attend_next:
                    pe.wait_ge(s_pt_lo, n + 1)
                    if b == 0:
                        pe.wait_ge(s_v_lo, 2 * k + 3)
                    if b == 4:
                        pe.wait_ge(s_v_lo, 2 * k + 2)
                    product(ps_o[:, :], [(both(v, slice(None), b, slice(None)), both(pT, slice(None), slice(None)))]).then_inc(s_pv, 1)

            for t in range(STEPS):
                step(-1, t, t == STEPS - 1, t >= 3, started=False)
            with pe.Fori(0, KVH - 1) as k:
                for t in range(STEPS):
                    step(k, t, True, True)
            for t in range(STEPS):
                step(KVH - 1, t, t < STEPS - 1, t < 3)

            def turn(name, sources):
                i = NTH[name]
                acc = split_bank(i)
                bank_free(i)
                at = 0
                for src in sources:
                    n, m = src.shape[0], P
                    mm = nc.tensor.transpose(acc[:, at:at + n], src, ident[0:n, 0:n])
                    at += n
                mm.then_inc(s_made, 1)

            def bank_free(i):
                if ORDER[i][0] == "x2":
                    pe.wait_ge(s_lo, i if ORDER[i - 1][0] == "x2" else max(j for j in range(i) if j % 4 == 3) + 1)
                elif i >= 4:
                    pe.wait_ge(s_lo, i - 3)

            def nat_blocks(half, c, lo=0, n=4):
                return [nat[:, half, lo + i * D + c * P:lo + i * D + (c + 1) * P] for i in range(n)]

            def xn_blocks(n):
                pe.wait_ge(s_xn2, n + 1)
                return [xn[:, n % 2, c * P:(c + 1) * P] for c in range(C)]

            pe.wait_ge(s_acc, KVH * STEPS)
            pe.wait_ge(s_nat[0], 16)
            for c in range(C):
                turn(("base", c), nat_blocks(0, c))
            pe.wait_ge(s_nat[1], 16 * 7)
            turn(("adapt", 0), [nat[:, 1, c * P:(c + 1) * P] for c in range(C)])
            turn(("gates", 0), [nat[0:NGT, 1, 2 * D + c * P:2 * D + (c + 1) * P] for c in range(C)])
            turn(("up", 0), [nat[:, 1, D + i * P:D + (i + 1) * P] for i in range(4)])
            pe.wait_ge(s_nat[2], 32)
            turn(("wk", 0), [nat[:, 0, c * P:(c + 1) * P] for c in range(C)])
            turn(("wv", 0), [nat[:, 0, D + c * P:D + (c + 1) * P] for c in range(C)])

            def project(name, pairs):
                i = NTH[name]
                bank_free(i)
                product(split_bank(i)[:, :], pairs).then_inc(s_made, 1)

            every = slice(None)
            for hf in (0, 1):
                cols = slice(hf * HALF, (hf + 1) * HALF)
                pe.wait_ge(s_lo, NTH[("wk", 0)] + 1)
                project(("k", hf), [(both(wk1, every, c, every), both(cT, every, c, cols)) for c in range(C)])
            for hf in (0, 1):
                i = NTH[("v", hf)]
                bank_free(i)
                pe.wait_ge(s_lo, NTH[("wv", 0)] + 1)
                for b in range(HT):
                    tok = slice((hf * HT + b) * TOK, (hf * HT + b + 1) * TOK)
                    mm = product(split_bank(i)[:, b * KV1:(b + 1) * KV1],
                                 [(both(cT, every, c, tok), both(wv1, every, c, every)) for c in range(C)])
                mm.then_inc(s_made, 1)

            def adapters_down(hf):
                for t in range(HT):
                    b = hf * HT + t
                    tok = slice(b * TOK, (b + 1) * TOK)
                    pe.wait_ge(s_lo, NTH[("x0", b)] + 1)
                    product(bank[hf][:, t * E * R:(t + 1) * E * R],
                            [(both(xT, every, c, tok), both(wa, every, c, every)) for c in range(C)])
                    mm = product(bank[2 + hf][:, t * NGT:(t + 1) * NGT],
                                 [(both(xT, every, c, tok), both(wg, every, c, every)) for c in range(C)])
                mm.then_inc(s_h, 1)

            for b in range(HT):
                turn(("x0", b), xn_blocks(b))
            adapters_down(0)
            pe.wait_ge(s_nat[3], 64)
            for c in range(C):
                turn(("wq", c), nat_blocks(1, c))
            for b in range(HT, NT):
                turn(("x0", b), xn_blocks(b))
            adapters_down(1)

            def ffn0(b):
                tok = slice(b * TOK, (b + 1) * TOK)
                t = b % HT
                if b >= 2:
                    pe.wait_ge(s_x2, b - 1)
                pe.wait_ge(s_lo, NTH[("hw", b // HT)] + 1)
                product(bank[0 if b % 2 == 0 else 2][:, :],
                        [(both(xT, every, c, tok), both(wb, every, c, every)) for c in range(C)]
                        + [(both(hwT, every, slice(t * TOK, (t + 1) * TOK)), both(wB, every, every))]).then_inc(s_f0, 1)

            pe.wait_ge(s_hw, 1)
            turn(("hw", 0), [hw[:, t, :] for t in range(HT)])
            for b in range(HT):
                ffn0(b)
            pe.wait_ge(s_hw, 2)
            turn(("hw", 1), [hw[:, t, :] for t in range(HT)])
            pe.wait_ge(s_nat[4], 16 * 4 * J1)
            for j in range(J1):
                turn(("wo", j), nat_blocks(0, j))
            for b in range(HT, NT):
                ffn0(b)
                turn(("x1", b - HT), xn_blocks(NT + b - HT))
            pe.wait_ge(s_bin, 1)
            for c in range(C):
                turn(("bin", c), nat_blocks(1, c))
            for b in range(HT, NT):
                turn(("x1", b), xn_blocks(NT + b))
            for i in range(2 * J1):
                j, hf = i % J1, i // J1
                pe.wait_ge(s_lo, NTH[("x1", HT - 1 if hf == 0 else NT - 1)] + 1)
                project(("q", i), [(both(wq1, every, c, slice(j * P, (j + 1) * P)), both(xT, every, c, slice(hf * HALF, (hf + 1) * HALF)))
                                   for c in range(C)])

            def scores1(u):
                B, j = u // J1, u % J1
                b, gh = B // 2, B % 2
                tok = slice(b * TOK, (b + 1) * TOK)
                if u >= 2:
                    pe.wait_ge(s_e1, u - 1)
                if u == 0:
                    pe.wait_ge(s_lo, NTH[("q", 2 * J1 - 1)] + 1)
                    pe.wait_ge(s_mask, 1)
                    pe.wait_ge(s_idr, 1)
                pe.wait_ge(s_kd, 2 * (B + 1))
                acc = bank[u % 2][:, :]
                nc.tensor.matmul(acc, ident_r[:, :], negmask[:, :, :].rearrange("p g m -> p (g m)"), start=True, stop=False)
                for i, (a, c) in enumerate(((1, 0), (0, 1), (0, 0))):
                    mm = nc.tensor.matmul(acc, q1T[a][:, j, tok], kd[c][:, gh, :, :].rearrange("p g m -> p (g m)"),
                                          start=False, stop=(i == 2))
                mm.then_inc(s_s1, 1)

            def pv1(B, i):
                b, gh = B // 2, B % 2
                if i == 0:
                    pe.wait_ge(s_t1l, J1 * (B + 1))
                    pe.wait_ge(s_vd, 2 * (B + 1))
                    if gh == 0 and b >= 1:
                        pe.wait_ge(s_o1l, b)
                part(bank[4][:, :], [(both(vd, every, gh, i, every), both(p1T, every, gh, i, every))],
                     gh == 0 and i == 0, gh == 1 and i == GH - 1).then_inc(s_pv1, 1)

            def turn_prob1(u):
                pe.wait_ge(s_n1, u + 1)
                if u >= 2:
                    pe.wait_ge(s_t1l, u - 1)
                for i in range(GH):
                    mm = nc.tensor.transpose(bank[2 + u % 2][:, i * TOK:(i + 1) * TOK], prob1[:, u % 2, i, :], ident[:, :])
                mm.then_inc(s_t1, 1)

            def out1(b):
                pe.wait_ge(s_o1l, b + 1)
                if b >= 1:
                    pe.wait_ge(s_x3, b)
                product(bank[5][:, :], [(both(o1T, every, j, every), both(wo1, every, j, every)) for j in range(J1)]).then_inc(s_out1, 1)

            def turn_x3(b):
                turn(("x2", b), xn_blocks(2 * NT + b))

            def ffn1(b):
                pe.wait_ge(s_lo, NTH[("x2", b)] + 1)
                if b >= 1:
                    pe.wait_ge(s_x4, b)
                tok = slice(b * TOK, (b + 1) * TOK)
                product(bank[6][:, :], [(both(xT, every, c, tok), both(wf1, every, c, every)) for c in range(C)]).then_inc(s_f1, 1)

            scores1(0)
            scores1(1)
            for u in range(UNITS):
                B = u // J1
                if u + 2 < UNITS:
                    scores1(u + 2)
                if B >= 1:
                    pv1(B - 1, u % J1)
                turn_prob1(u)
                if u % 8 == 5 and u >= 8:
                    out1(u // 8 - 1)
                if u % 8 == 1 and u >= 16:
                    turn_x3(u // 8 - 2)
                if u % 8 == 2 and u >= 16:
                    ffn1(u // 8 - 2)
            for i in range(GH):
                pv1(2 * NT - 1, i)
            turn_x3(NT - 2)
            ffn1(NT - 2)
            out1(NT - 1)
            turn_x3(NT - 1)
            ffn1(NT - 1)


_INS = ["x", "ctx_4096", "mask_SxS2_bk0", "g_xattn", "g_ffn", "L0_xattn_Wq", "L0_xattn_bq", "L0_xattn_Wkv", "L0_xattn_bkv",
        "L0_xattn_Wo", "L0_xattn_bo", "L0_ffn_W_base", "L0_ffn_b_base", "L0_ffn_W_gate", "L0_ffn_W_thr", "L0_ffn_b_thr",
        "L0_ffn_A_w", "L0_ffn_B_w", "L1_xattn_w_q", "L1_xattn_w_k", "L1_xattn_w_v", "L1_xattn_w_out", "L1_ffn_weight"]
_OUTS = [((8, 128, 512), "float32")]


def kernel(**inputs):
    import numpy as _np
    import concourse.bacc as _bacc
    from concourse import mybir as _mybir
    from concourse.bass_utils import run_bass_kernel_spmd as _run

    nc = _bacc.Bacc("TRN2", target_bir_lowering=False, num_devices=1)
    arrays, args = {}, []
    for name in _INS:
        a = _np.ascontiguousarray(inputs[name])
        arrays[f"in_{name}_dram"] = a
        args.append(nc.dram_tensor(f"in_{name}_dram", a.shape, _mybir.dt.from_np(a.dtype), kind="ExternalInput").ap())
    for i, (shape, dtype) in enumerate(_OUTS):
        dt = _mybir.dt.from_np(_np.dtype(dtype))
        args.append(nc.dram_tensor(f"out_{i}_dram", shape, dt, kind="ExternalOutput").ap())
    build(nc, *args)
    r = _run(nc, [arrays], core_ids=[0])
    return r.results[0]["out_0_dram"]
```

```python
from contextlib import ExitStack

import numpy as np

import concourse.bass as bass
from concourse import mybir

ALU = mybir.AluOpType
ACT = mybir.ActivationFunctionType
AX = mybir.AxisListType
F32 = mybir.dt.float32
F32R = mybir.dt.float32r
P = 128


def build(nc, x, ctx_in, mask, g_xattn, g_ffn, Wq, bq, Wkv, bkv, Wo, bo, W_base, b_base, W_gate, W_thr, b_thr, A_w, B_w,
          w_q, w_k, w_v, w_out, w_bin, out):
    BATCH, TOK, D = x.shape
    DH = P
    HEADS = Wq.shape[1] // DH
    KVH = Wkv.shape[1] // (2 * DH)
    G = HEADS // KVH
    C = D // P
    NT = BATCH
    HALF = NT * TOK // 2
    STEPS = NT
    SCALE0 = float(1.0 / np.sqrt(DH))
    EPS = 1e-5
    SLOTS = 2

    SLICES = [("q", 0), ("k", 0), ("q", 1), ("q", 2), ("o", 0), ("q", 3), ("v", 0), ("o", 1), ("o", 2), ("o", 3)]
    SPLIT_AT = {0: [0], 1: [1, 2], 2: [3, 4], 3: [5, 6], 4: [7], 5: [8], 6: [9], 7: []}
    NS = len(SLICES)

    E, R = A_w.shape[0], A_w.shape[1]
    NGT = E + 2
    ADAPT = 2.0
    THR_MAX = 0.125
    KV1 = w_k.shape[0]
    DH1 = D // HEADS
    G1 = KV1 // DH1
    J1 = HEADS // G1
    GH = G1 // 2
    SCALE1 = float(DH1) ** -0.5
    MASKED = float((2 - 2.0 ** -11) * 2.0 ** 127)
    UNITS = NT * 2 * J1
    HT = NT // 2

    x_rows = x.rearrange("b t d -> t b d")
    ctx_rows = ctx_in.rearrange("b t d -> t b d")
    wq_rows = Wq.rearrange("(c p) n -> p c n", p=P)
    wkv_rows = Wkv.rearrange("(c p) n -> p c n", p=P)
    wo_rows = Wo.rearrange("(h p) n -> h p n", p=P)

    with ExitStack() as es:
        def sem(name):
            return es.enter_context(nc.semaphore(name))

        bank = [es.enter_context(nc.psum_tensor(f"bank{i}", [P, 512], F32)) for i in range(8)]
        ps_s, ps_pt, ps_o, ps_q, ps_out, ps_kv, ps_vt = bank[:7]

        KI = 1024
        first_byte = -(-nc.sbuf_base // 64) * 64

        def at(kib, name, shape, dt=F32):
            return nc.alloc_sbuf_tensor_at(name, shape, dt, offset=first_byte + int(kib * KI))

        def pair(kib, name, shape, lo_kib=None):
            size = 4 * int(np.prod(shape[1:])) / KI
            return [at(kib, name + "_hi", shape, F32R), at(kib + size if lo_kib is None else lo_kib, name + "_lo", shape, F32R)]

        xres = at(0, "xres", [P, NT, D])
        xT = pair(16, "xT", [P, C, NT * TOK])
        cT = pair(48, "cT", [P, C, NT * TOK])
        A0 = 80
        qT = pair(A0, "qT", [P, G, NT * TOK])
        kT = pair(A0 + 32, "kT", [P, NT * TOK])
        v = pair(A0 + 40, "v", [P, NT, DH])
        vT = at(A0 + 48, "vT", [P, 4, TOK])
        wq = pair(A0 + 50, "wq", [P, G, C, DH])
        wk = pair(A0 + 66, "wk", [P, C, DH])
        wv = pair(A0 + 70, "wv", [P, C, DH])
        wo = pair(A0 + 74, "wo", [P, 2 * G * D])
        stage = at(A0 + 106, "stage", [P, SLOTS, 512])
        prob = at(A0 + 110, "prob", [P, G, TOK])
        pT = pair(A0 + 112, "pT", [P, 512])
        oT = pair(A0 + 116, "oT", [P, G, TOK])
        ctx_nat = at(A0, "ctx_nat", [P, NT, D])
        xn_nat = at(A0 + 16, "xn_nat", [P, NT, D])
        bias_nat = at(A0 + 32, "bias_nat", [HEADS + 2 * KVH, DH])
        bo_bc = at(A0 + 118, "bo_bc", [P, D])
        stage_v = at(A0 + 40, "stage_v", [P, 4, 512])
        stage_p = at(A0 + 110, "stage_p", [P, 4, 512])
        first_stage = [stage[:, i, :] for i in (0, 1)] + [stage_v[:, i, :] for i in range(4)] + [stage_p[:, i, :] for i in range(4)]
        wb = pair(A0, "w_base", [P, C, D])
        wa = pair(A0 + 16, "w_adapt", [P, C, E * R])
        wB = pair(A0 + 20, "w_up", [E * R, D])
        wq1 = pair(A0 + 66, "w_q1", [P, C, D], A0 + 24)
        wo1 = pair(A0 + 40, "w_o1", [P, J1, D], A0 + 82)
        b_base_bc = at(A0 + 48, "b_base_bc", [P, D])
        nat = at(A0 + 50, "nat", [P, 2, 4 * D])
        wk1 = pair(A0 + 66, "w_k1", [P, C, KV1])
        wv1 = pair(A0 + 70, "w_v1", [P, C, KV1])
        k1T = pair(A0 + 74, "k1T", [KV1, NT * TOK])
        v1 = pair(A0 + 90, "v1", [P, NT, KV1])
        wf1 = pair(A0 + 98, "w_f1", [P, C, D], A0 + 110)
        xn = at(A0 + 106, "xn", [P, 2, D])
        wide = at(A0 + 118, "weights_wide", [P, HT, E * R])
        gates_nat = at(A0 + 120, "gates_nat", [NGT, D])
        hwT = [pair(A0 + (120, 98)[hf], f"hwT{hf}", [E * R, HT * TOK]) for hf in (0, 1)]
        gl = at(48, "gate_work", [P, 16, HT * E])
        hw = at(50, "adapters_weighted", [P, HT * TOK])
        gatesT = at(52, "gatesT", [NGT, 2, HT * TOK])
        bin_nat = at(56, "w_bin_nat", [P, 4, D])
        q1_nat = at(64, "w_q1_nat", [P, J1, D])
        o1_nat = at(72, "w_o1_nat", [P, 4, D])
        sign = at(A0 + 110, "sign", [P, 4, D])
        q1T = pair(48, "q1T", [P, J1, NT * TOK])
        p1T = pair(A0, "p1T", [P, 2, GH, J1 * TOK])
        o1T = pair(A0 + 32, "o1T", [KV1, J1, TOK])
        prob1 = at(A0 + 36, "prob1", [P, 2, GH, TOK])
        negmask = at(A0 + 48, "negmask", [P, GH, TOK], F32R)
        kd = pair(A0 + 50, "k_by_group", [KV1, 2, GH, TOK])
        vd = pair(A0 + 58, "v_by_group", [P, 2, GH, KV1])
        small_at = [A0 + 124.0]

        def small(name, shape, dt=F32):
            size = -(-int(np.prod(shape[1:])) * (1 if dt == mybir.dt.uint8 else 4) // 32) * 32
            small_at[0] += size / KI
            return at(small_at[0] - size / KI, name, shape, dt)

        ident = small("ident", [P, P])
        ident_r = small("ident_r", [P, P], F32R)
        gate_raw = small("gate_raw", [P, 4])
        gate = small("gate", [P, 4])
        stats = small("stats", [P, NT, 6])
        moments = small("moments", [P, NT, 2])
        rstd = small("rstd", [P, NT])
        power = small("power", [P, NT])
        bias_all = small("bias_all", [P, KVH * (G + 2)])
        bias = small("bias", [P, G + 2])
        nmax = small("nmax", [P, 2, G])
        rsum = small("rsum", [P, G])
        rinv = small("rinv", [P, G])
        wg = [small("w_gates_hi", [P, C, NGT], F32R), small("w_gates_lo", [P, C, NGT], F32R)]
        nb_thr = small("nb_thr", [P, 1])
        scale = small("w_bin_scale_cols", [P, 2, 4])
        mask_in = small("mask_in", [P, TOK], mybir.dt.uint8)
        group_of = small("group_of", [P, G1])
        nmax1 = small("nmax1", [P, 2, GH])
        rsum1 = small("rsum1", [P, 2, GH])
        rinv1 = small("rinv1", [P, 2, GH])

        s_ident0, s_ident = sem("ident_zeroed"), sem("ident_ready")
        s_x_in = [sem(f"x_in{b}") for b in range(NT)]
        s_ctx_in = [sem(f"ctx_in{b}") for b in range(NT)]
        s_small_in = sem("small_in")
        s_gate = sem("gate_ready")
        s_stats, s_moments, s_rstd = sem("stats"), sem("moments"), sem("rstd")
        s_pow = sem("rstd_ready")
        s_xn = sem("x_normalised")
        s_bo = sem("bo_gated")
        s_xres = sem("xres_ready")
        s_tr, s_tr_hi, s_tr_lo = sem("transposed"), sem("transposed_hi"), sem("transposed_lo")
        s_bias_tr, s_bias_all, s_bias = sem("bias_transposed"), sem("bias_all"), sem("bias_now")
        s_w0_in = [sem(f"first_weight_in{i}") for i in range(NS)]
        s_w_in = [sem(f"weight_in{i}") for i in range(SLOTS)]
        s_w_hi, s_w_lo = sem("weight_hi"), sem("weight_lo")
        s_qproj, s_q_hi, s_q_lo = sem("q_projected"), sem("q_hi"), sem("q_lo")
        s_kproj, s_k_hi, s_k_lo = sem("k_projected"), sem("k_hi"), sem("k_lo")
        s_vproj, s_vt, s_vtr, s_v_hi, s_v_lo = sem("v_projected"), sem("vT_ready"), sem("v_transposed"), sem("v_hi"), sem("v_lo")
        s_scores, s_max, s_nmax, s_exp = sem("scores"), sem("row_max"), sem("neg_max"), sem("exped")
        s_rinv, s_norm, s_ptr = sem("rsum_inverted"), sem("prob_normalised"), sem("prob_transposed")
        s_pt_hi, s_pt_lo, s_pv, s_o_hi, s_o_lo = sem("pT_hi"), sem("pT_lo"), sem("pv"), sem("oT_hi"), sem("oT_lo")
        s_out, s_acc = sem("out_projected"), sem("out_added")
        s_store = sem("stored")
        s_nat = [sem(f"natural_in{i}") for i in range(6)]
        s_thr_in, s_wscale, s_sign, s_clip, s_unclipped = (sem("b_thr_in"), sem("w_bin_scale"), sem("w_bin_sign"),
                                                           sem("w_bin_clipped"), sem("w_bin_less_clip"))
        s_perm, s_gtmade, s_gt, s_gturned = sem("w_out_permuted"), sem("gatesT_made"), sem("gatesT_copied"), sem("gates_turned")
        s_small2 = sem("small2_in")
        s_gzero = sem("gate_rows_zeroed")
        s_made, s_hi, s_lo = sem("split_made"), sem("split_hi"), sem("split_lo")
        s_eps, s_pow2, s_xn2 = sem("variance_eps"), sem("rstd2_ready"), sem("xn_ready")
        s_bb, s_bbg, s_xb = sem("b_base_in"), sem("b_base_gated"), sem("b_base_added")
        s_el, s_ee, s_hw = sem("gate_logits"), sem("gate_exps"), sem("adapters_weighted")
        s_wide, s_wideT = sem("weights_wide"), sem("weights_wide_transposed")
        s_f0, s_x2 = sem("ffn0_done"), sem("x2_ready")
        s_bin = sem("w_bin_ready")
        s_idr, s_mask, s_grp0, s_grp1, s_grp = sem("ident_r"), sem("negmask"), sem("group0"), sem("group1"), sem("group_of")
        s_vz, s_kd, s_vd = sem("v_zeroed"), sem("k_by_group"), sem("v_by_group")
        s_s1, s_m1, s_e1, s_r1, s_n1 = sem("scores1"), sem("max1"), sem("exp1"), sem("rinv1"), sem("norm1")
        s_t1, s_t1h, s_t1l, s_pv1 = sem("p1_transposed"), sem("p1T_hi"), sem("p1T_lo"), sem("pv1")
        s_o1h, s_o1l, s_out1, s_x3 = sem("o1T_hi"), sem("o1T_lo"), sem("out1"), sem("x3_ready")
        s_f1, s_x4 = sem("ffn1_done"), sem("x4_ready")
        s_chain = sem("vector_chain")

        NTR = 2 * NT

        def q_head_half(t):
            return (t - 3) % 8 % 4, 0 if 3 <= t <= 6 else 1

        def split_dst(kvh, i):
            kind, h = SLICES[i]
            if kind == "q":
                return tuple(w[:, h, :, :].rearrange("p c n -> p (c n)") for w in wq)
            if kind == "o":
                return tuple(w[:, bass.ds((kvh % 2) * (G * D) + h * D, D)] for w in wo)
            return tuple(w[:, :, :].rearrange("p c n -> p (c n)") for w in (wk if kind == "k" else wv))

        TURNED = [("ctx", b) for b in range(HT)] + [("x", b) for b in range(HT)] \
            + [(what, b) for b in range(HT, NT) for what in ("ctx", "x")]
        turn_banks = [bank[i] for i in (0, 1, 2, 4)]
        TURN_AT = {3: [8, 9], 4: [10, 11], 5: [12, 13], 6: [14, 15]}

        def turned(i):
            what, b = TURNED[i]
            return [part[:, :, b * TOK:(b + 1) * TOK] for part in (cT if what == "ctx" else xT)]

        AHEAD = {3: [], 4: [], 5: [], 6: [], 7: [("v", 1)]}
        BEHIND = {3: [("wk", 0), ("wv", 0), ("x0", 0)], 4: [("k", 0), ("x0", 1)], 5: [("k", 1), ("x0", 2), ("x0", 3)],
                  6: [("v", 0), ("x0", 4)],
                  7: [("base", c) for c in range(C)] + [("adapt", 0), ("gates", 0), ("up", 0), ("x0", 5)]}
        NORMALISED = {2: [0], 3: [1], 4: [2, 3], 5: [4], 6: [5], 7: [6]}
        ORDER = ([name for t in range(3, STEPS) for name in AHEAD[t] + BEHIND[t]]
                 + [("x0", 6), ("wq", 0), ("wq", 1), ("x0", 7), ("wq", 2), ("wq", 3), ("hw", 0)] + [("wo", j) for j in range(J1)]
                 + [("hw", 1)] + [("x1", b) for b in range(HT)] + [("bin", c) for c in range(C)] + [("x1", HT)]
                 + [name for i in range(J1) for name in [("q", i)] + ([("x1", HT + 1 + i)] if HT + 1 + i < NT else [])]
                 + [("q", J1 + j) for j in range(J1)]
                 + [("x2", b) for b in range(NT)])
        NTH = {name: i for i, name in enumerate(ORDER)}
        RING = [bank[i] for i in (3, 7, 5, 6)]

        def split_bank(i):
            return RING[i % 4] if ORDER[i][0] != "x2" else bank[7]

        def split_views(i):
            kind, n = ORDER[i]
            acc = split_bank(i)
            four = acc[:, :].rearrange("p (c n) -> p c n", c=4)
            tok = slice(n * TOK, (n + 1) * TOK)
            half = slice(n * HALF, (n + 1) * HALF)
            if kind == "base":
                return acc[:, :], wb[0][:, n, :], wb[1][:, n, :]
            if kind == "adapt":
                return four, wa[0][:, :, :], wa[1][:, :, :]
            if kind == "gates":
                return acc[:, 0:C * NGT].rearrange("p (c n) -> p c n", c=C), wg[0][:, :, :], wg[1][:, :, :]
            if kind == "up":
                return acc[:, :], wB[0][:, :], wB[1][:, :]
            if kind == "wk":
                return four, wk1[0][:, :, :], wk1[1][:, :, :]
            if kind == "wv":
                return four, wv1[0][:, :, :], wv1[1][:, :, :]
            if kind == "k":
                return acc[:, :], k1T[0][:, half], k1T[1][:, half]
            if kind == "v":
                return four, v1[0][:, n * HT:(n + 1) * HT, :], v1[1][:, n * HT:(n + 1) * HT, :]
            if kind in ("x0", "x1", "x2"):
                return four, xT[0][:, :, tok], xT[1][:, :, tok]
            if kind == "wq":
                return acc[:, :], wq1[0][:, n, :], wq1[1][:, n, :]
            if kind == "hw":
                return hw[:, :], hwT[n][0][:, :], hwT[n][1][:, :]
            if kind == "wo":
                return acc[:, :], wo1[0][:, n, :], wo1[1][:, n, :]
            if kind == "bin":
                return acc[:, :], wf1[0][:, n, :], wf1[1][:, n, :]
            half = slice(n // J1 * HALF, (n // J1 + 1) * HALF)
            return acc[:, :], q1T[0][:, n % J1, half], q1T[1][:, n % J1, half]

        def adaptersT(hf):
            return bank[(2, 4)[hf]]

        def gates_of(hf):
            return bank[hf][:, 0:HT * NGT].rearrange("p (t n) -> p t n", n=NGT)

        turned1 = (bank[2], bank[4])
        ps_pv1 = bank[3]

        block = es.enter_context(nc.Block())

        @block.sync
        def _(sp):
            def load(kvh, i, slot, arrived):
                kind, h = SLICES[i]
                if kind == "o":
                    dst, src = slot, wo_rows[bass.ds(kvh * G + h, 1), :, :].rearrange("a p n -> p (a n)")
                else:
                    dst = slot.rearrange("p (c n) -> p c n", c=C)
                    if kind == "q":
                        src = wq_rows[:, :, bass.ds(kvh * (G * DH) + h * DH, DH)]
                    elif kind == "k":
                        src = wkv_rows[:, :, bass.ds(kvh * DH, DH)]
                    else:
                        src = wkv_rows[:, :, bass.ds(kvh * DH + KVH * DH, DH)]
                sp.dma_start(dst, src).then_inc(arrived, 16)

            for half in (0, 1):
                for b in range(half * HT, (half + 1) * HT):
                    sp.dma_start(ctx_nat[:, b, :], ctx_rows[:, b, :]).then_inc(s_ctx_in[b], 16)
                for i in (range(2) if half == 0 else range(2, NS)):
                    load(0, i, first_stage[i], s_w0_in[i])
            with sp.Fori(1, KVH) as kvh:
                for i in range(NS):
                    sp.wait_ge(s_w_lo, kvh * NS + (i - SLOTS + 1))
                    load(kvh, i, stage[:, i % SLOTS, :], s_w_in[i % SLOTS])
            sp.wait_ge(s_qproj, KVH * STEPS)

            def rows(lo):
                return nat[:, :, :].rearrange("p a n -> p (a n)")[:, lo * D:(lo + 1) * D]

            def tiled(lo, w):
                sp_dst = nat[:, :, :].rearrange("p a n -> p (a n)")[:, lo * D:(lo + 4) * D]
                return sp_dst.rearrange("p (i n) -> p i n", i=4), w.rearrange("(i p) n -> p i n", p=P)

            sp.dma_start(rows(4), w_k).then_inc(s_nat[0], 16)
            sp.dma_start(rows(5), w_v).then_inc(s_nat[0], 16)
            sp.dma_start(*tiled(0, W_base)).then_inc(s_nat[1], 16)
            sp.dma_start(rows(6), A_w.rearrange("e r d -> (e r) d")).then_inc(s_nat[2], 16)
            for i in range(4):
                sp.dma_start(rows(7)[:, i * P:(i + 1) * P].rearrange("p (e r) -> p e r", e=E),
                             B_w[:, i * P:(i + 1) * P, :].rearrange("e p r -> p e r")).then_inc(s_nat[2], 16)
            sp.wait_ge(s_gzero, 1)
            sp.dma_start(gates_nat[0:E, :], W_gate).then_inc(s_nat[2], 16)
            sp.dma_start(gates_nat[E:E + 1, :], W_thr.rearrange("(a d) -> a d", a=1)).then_inc(s_nat[2], 16)
            sp.wait_ge(s_vtr, 2 * KVH)
            sp.dma_start(b_base_bc[:, :], b_base.partition_broadcast(P)).then_inc(s_bb, 16)
            sp.dma_start(mask_in[:, :], mask).then_inc(s_small2, 16)
            sp.wait_ge(s_made, NTH[("v", 1)] + 1)
            for j in range(J1):
                sp.dma_start(q1_nat[:, j, :], w_q.rearrange("(g j d) n -> j g d n", j=J1, d=DH1)[j]).then_inc(s_nat[3], 16)
            sp.dma_start(o1_nat[:, :, :], w_out.rearrange("(i p) n -> p i n", p=P)).then_inc(s_nat[4], 16)
            sp.dma_start(bin_nat[:, :, :], w_bin.rearrange("(i p) n -> p i n", p=P)).then_inc(s_nat[5], 16)
            for b in range(NT):
                sp.wait_ge(s_x4, b + 1)
                sp.dma_start(out.rearrange("b t d -> t b d")[:, b, :], xres[:, b, :]).then_inc(s_store, 16)
            sp.wait_ge(s_store, 16 * NT)

        @block.gpsimd
        def _(pool):
            nc.gpsimd.memset(ident[:, :], 0.0).then_inc(s_ident0, 1)
            pool.wait_ge(s_ident0, 1)
            nc.gpsimd.affine_select(out=ident[:, :], in_=ident[:, :], compare_op=ALU.not_equal, fill=1.0, base=0,
                                    pattern=[[-1, P]], channel_multiplier=1).then_inc(s_ident, 1)
            nc.gpsimd.memset(gates_nat[:, :], 0.0).then_inc(s_gzero, 1)
            pool.dma_start(gate_raw[:, 0:2], g_xattn.partition_broadcast(P)).then_inc(s_small_in, 16)
            pool.dma_start(gate_raw[:, 2:4], g_ffn.partition_broadcast(P)).then_inc(s_small_in, 16)
            pool.dma_start(bo_bc[:, :], bo.partition_broadcast(P)).then_inc(s_small_in, 16)
            pool.dma_start(bias_nat[0:HEADS, :], bq.rearrange("(h d) -> h d", d=DH)).then_inc(s_small_in, 16)
            pool.dma_start(bias_nat[HEADS:, :], bkv.rearrange("(h d) -> h d", d=DH)).then_inc(s_small_in, 16)
            for half in (0, 1):
                pool.wait_ge(s_rstd, 2 + half)
                cols = slice(half * HT, (half + 1) * HT)
                nc.gpsimd.tensor_tensor(rstd[:, cols], rstd[:, cols], power[:, cols], ALU.pow).then_inc(s_pow, 1)
            pool.dma_start(nb_thr[:, :], b_thr.partition_broadcast(P)).then_inc(s_thr_in, 16)

            def add_bo(b):
                pool.wait_ge(s_bo, 1)
                pool.wait_ge(s_xn, b + 1)
                nc.gpsimd.tensor_tensor(xres[:, b, :], xres[:, b, :], bo_bc[:, :], ALU.add).then_inc(s_xres, 1)

            def step(k, t, attend_next, split):
                if split:
                    for i in SPLIT_AT[t]:
                        hi, lo = split_dst(k + 1, i)
                        pool.wait_ge(s_w_hi, (k + 1) * NS + i + 1)
                        src = first_stage[i] if isinstance(k, int) else stage[:, i % SLOTS, :]
                        nc.gpsimd.tensor_tensor(lo, src, hi.bitcast(F32), ALU.subtract).then_inc(s_w_lo, 1)
                if attend_next:
                    n = k * STEPS + t + 1
                    pool.wait_ge(s_rinv, n + 1)
                    nc.gpsimd.tensor_tensor(prob[:, :, :], prob[:, :, :], rinv[:, :].unsqueeze(2).broadcast_to([P, G, TOK]),
                                            ALU.mult).then_inc(s_norm, 1)

            def inverse_root(n):
                pool.wait_ge(s_eps, n + 1)
                col = slice(n % NT, n % NT + 1)
                nc.gpsimd.tensor_tensor(rstd[:, col], rstd[:, col], power[:, 0:1], ALU.pow).then_inc(s_pow2, 1)

            for t in range(STEPS):
                step(-1, t, False, True)
                if t in (2, 5):
                    for b in (range(HT) if t == 2 else range(HT, NT)):
                        add_bo(b)
            step(-1, STEPS - 1, True, False)
            with pool.Fori(0, KVH - 1) as k:
                for t in range(STEPS):
                    step(k, t, True, True)
            for t in range(STEPS):
                step(KVH - 1, t, t < STEPS - 1, False)
                if t > 0:
                    inverse_root(t - 1)
            inverse_root(NT - 1)

            pool.wait_ge(s_bbg, 1)
            for b in range(NT):
                pool.wait_ge(s_xn2, b + 1)
                nc.gpsimd.tensor_tensor(xres[:, b, :], xres[:, b, :], b_base_bc[:, :], ALU.add).then_inc(s_xb, 1)

            pool.wait_ge(s_nat[4], 16)
            pool.wait_ge(s_made, NTH[("up", 0)] + 1)
            for i in range(4):
                ins = nc.gpsimd.tensor_copy(nat[:, 1, i * D:(i + 1) * D].rearrange("p (j g d) -> p j g d", j=J1, d=DH1),
                                            o1_nat[:, i, :].rearrange("p (g j d) -> p j g d", j=J1, d=DH1))
            ins.then_inc(s_perm, 1)

            pool.wait_ge(s_sign, 1)
            pool.wait_ge(s_wscale, 1)
            for i in range(4):
                ins = nc.gpsimd.tensor_scalar(bin_nat[:, i, :], bin_nat[:, i, :], -1.0, 1.0, ALU.max, ALU.min)
            ins.then_inc(s_clip, 1)
            for n in range(NT, NT + HT):
                inverse_root(n)
            pool.wait_ge(s_unclipped, 1)
            for i in range(4):
                ins = nc.gpsimd.tensor_tensor(bin_nat[:, i, :], sign[:, i, :], bin_nat[:, i, :], ALU.add)
            ins.then_inc(s_bin, 1)
            for n in range(NT + HT, 2 * NT):
                inverse_root(n)

            nc.gpsimd.memset(group_of[:, :], 1.0).then_inc(s_grp0, 1)
            pool.wait_ge(s_grp0, 1)
            nc.gpsimd.affine_select(out=group_of[:, :], in_=group_of[:, :], compare_op=ALU.is_ge, fill=0.0, base=0,
                                    pattern=[[-DH1, G1]], channel_multiplier=1).then_inc(s_grp1, 1)
            pool.wait_ge(s_grp1, 1)
            nc.gpsimd.affine_select(out=group_of[:, :], in_=group_of[:, :], compare_op=ALU.is_ge, fill=0.0, base=DH1 - 1,
                                    pattern=[[DH1, G1]], channel_multiplier=-1).then_inc(s_grp, 1)
            pool.wait_ge(s_made, NTH[("wo", J1 - 1)] + 1)
            for part in vd:
                nc.gpsimd.memset(part[:, :, :, :].bitcast(F32), 0.0).then_inc(s_vz, 1)

            def k_by_group(B, part):
                b, gh = B // 2, B % 2
                if B >= 2:
                    pool.wait_ge(s_s1, J1 * (B - 1))
                nc.gpsimd.tensor_tensor(kd[part][:, gh, :, :],
                                        k1T[part][:, b * TOK:(b + 1) * TOK].bitcast(F32).unsqueeze(1).broadcast_to([KV1, GH, TOK]),
                                        group_of[:, gh * GH:(gh + 1) * GH].unsqueeze(2).broadcast_to([KV1, GH, TOK]),
                                        ALU.mult).then_inc(s_kd, 1)

            def v_by_group(B, part):
                b, gh = B // 2, B % 2
                if B >= 2:
                    pool.wait_ge(s_pv1, GH * (B - 1))
                step_ = KV1 + DH1
                flat = vd[part][:, gh, :, :].rearrange("p g n -> p (g n)")
                for i in range(GH):
                    at = i * step_ + gh * GH * DH1
                    ins = nc.gpsimd.tensor_copy(flat[:, at:at + DH1],
                                                v1[part][:, b, (gh * GH + i) * DH1:(gh * GH + i + 1) * DH1].bitcast(F32))
                ins.then_inc(s_vd, 1)

            def norm1(u):
                pool.wait_ge(s_r1, u + 1)
                nc.gpsimd.tensor_tensor(prob1[:, u % 2, :, :], prob1[:, u % 2, :, :],
                                        rinv1[:, u % 2, :].unsqueeze(2).broadcast_to([P, GH, TOK]), ALU.mult).then_inc(s_n1, 1)

            pool.wait_ge(s_grp, 1)
            for B in (0, 1):
                for part in (0, 1):
                    k_by_group(B, part)
            pool.wait_ge(s_vz, 2)
            for B in (0, 1):
                for part in (0, 1):
                    v_by_group(B, part)
            norm1(0)
            norm1(1)
            for u in range(UNITS):
                if u % 8 == 6 and u >= 8:
                    inverse_root(2 * NT + u // 8 - 1)
                if u + 2 < UNITS:
                    norm1(u + 2)
                B = u // J1
                if u % J1 in (2, 3) and B + 2 < 2 * NT:
                    k_by_group(B + 2, u % J1 - 2)
                if u % J1 in (1, 2) and B >= 2:
                    v_by_group(B, u % J1 - 1)
            inverse_root(3 * NT - 1)

        @block.scalar
        def _(act):
            for b in range(NT):
                act.dma_start(xres[:, b, :], x_rows[:, b, :]).then_inc(s_x_in[b], 16)

            def turned_hi(i):
                act.wait_ge(s_tr, i + 1)
                nc.scalar.activation(turned(i)[0], turn_banks[i % 4][:, :].rearrange("p (c n) -> p c n", c=C), ACT.Copy
                                     ).then_inc(s_tr_hi, 1)

            for i in range(HT):
                turned_hi(i)
            act.wait_ge(s_small_in, 80)
            nc.scalar.activation(gate[:, :], gate_raw[:, :], ACT.Tanh).then_inc(s_gate, 1)
            for i in range(HT, NT):
                turned_hi(i)
            act.wait_ge(s_ident, 1)
            nc.scalar.activation(ident_r[:, :], ident[:, :], ACT.Copy).then_inc(s_idr, 1)

            def hi(i):
                act.wait_ge(s_made, i + 1)
                if ORDER[i][0] == "hw":
                    nc.scalar.activation(hw[:, :], split_bank(i)[:, :], ACT.Copy, scale=ADAPT).then_inc(s_wideT, 1)
                    act.wait_ge(s_hw, ORDER[i][1] + 1)
                acc, dst, _ = split_views(i)
                if ORDER[i][0] == "q":
                    nc.scalar.activation(dst, acc, ACT.Copy, scale=SCALE1).then_inc(s_hi, 1)
                else:
                    nc.scalar.activation(dst, acc, ACT.Copy).then_inc(s_hi, 1)

            def step(k, t, attend_next, project, split, started=True, ending=False):
                g = k * STEPS + t
                if started:
                    act.wait_ge(s_ptr, g + 1)
                    nc.scalar.activation(pT[0][:, :], ps_pt[:, :], ACT.Copy).then_inc(s_pt_hi, 1)
                if attend_next:
                    act.wait_ge(s_nmax, g + 2)
                    if not started:
                        act.wait_ge(s_w_lo, NS)
                    for j in range(G):
                        e = nc.scalar.activation(prob[:, j, :], ps_s[:, j * TOK:(j + 1) * TOK], ACT.Exp, bias=nmax[:, 1, j:j + 1],
                                                 scale=SCALE0, accum_out=rsum[:, j:j + 1])
                    e.then_inc(s_exp, 1)
                if ending:
                    for name in AHEAD.get(t, ()):
                        hi(NTH[name])
                if started:
                    act.wait_ge(s_pv, g + 1)
                    nc.scalar.activation(oT[0][:, :, :].rearrange("p g t -> p (g t)"), ps_o[:, :], ACT.Copy).then_inc(s_o_hi, 1)
                if split:
                    for i in SPLIT_AT[t]:
                        kind, h = SLICES[i]
                        if isinstance(k, int):
                            src = first_stage[i]
                            act.wait_ge(s_w0_in[i], 16)
                        else:
                            src = stage[:, i % SLOTS, :]
                            act.wait_ge(s_w_in[i % SLOTS], k * (16 * NS // SLOTS) + 16 * (i // SLOTS + 1))
                        if started:
                            if kind == "q":
                                act.wait_ge(s_qproj, g + 5)
                            elif kind == "k":
                                act.wait_ge(s_kproj, 2 * k + 2)
                            elif kind == "v":
                                act.wait_ge(s_vproj, 2 * k + 2)
                            else:
                                act.wait_ge(s_out, k * STEPS + 1)
                        nc.scalar.activation(split_dst(k + 1, i)[0], src, ACT.Copy).then_inc(s_w_hi, 1)
                if project:
                    h, half = q_head_half(t)
                    act.wait_ge(s_qproj, g + 6)
                    if t == 3:
                        act.wait_ge(s_bias, k + 2)
                    nc.scalar.activation(qT[0][:, h, half * HALF:(half + 1) * HALF], ps_q[:, :], ACT.Identity,
                                         bias=bias[:, h:h + 1]).then_inc(s_q_hi, 1)
                if not started and t in TURN_AT:
                    for i in TURN_AT[t]:
                        turned_hi(i)
                if t == 3 and started:
                    act.wait_ge(s_vtr, 2 * k + 2)
                    nc.scalar.activation(v[0][:, 4:8, :].rearrange("p b d -> p (b d)"), ps_vt[:, :], ACT.Copy).then_inc(s_v_hi, 1)
                if t == 7 and attend_next:
                    act.wait_ge(s_vtr, 2 * k + 3)
                    nc.scalar.activation(v[0][:, 0:4, :].rearrange("p b d -> p (b d)"), ps_vt[:, :], ACT.Copy).then_inc(s_v_hi, 1)
                if ending:
                    for name in BEHIND.get(t, ()):
                        hi(NTH[name])
                if project and t in (0, 4):
                    c, half = (2, 1) if t == 0 else (3, 0)
                    act.wait_ge(s_kproj, 2 * k + c)
                    nc.scalar.activation(kT[0][:, half * HALF:(half + 1) * HALF], ps_kv[:, :], ACT.Identity,
                                         bias=bias[:, G:G + 1]).then_inc(s_k_hi, 1)
                if project and t in (2, 6):
                    c = 2 if t == 2 else 3
                    act.wait_ge(s_vproj, 2 * k + c)
                    nc.scalar.activation(vT[:, :, :].rearrange("p b t -> p (b t)"), ps_kv[:, :], ACT.Identity,
                                         bias=bias[:, G + 1:G + 2]).then_inc(s_vt, 1)

            for t in range(STEPS):
                step(-1, t, t == STEPS - 1, t >= 3, True, started=False)
            with act.Fori(0, KVH - 1) as k:
                for t in range(STEPS):
                    step(k, t, True, True, True)
            for t in range(STEPS):
                step(KVH - 1, t, t < STEPS - 1, t < 3, False, ending=True)


            def gates_copied(hf):
                act.wait_ge(s_gtmade, hf + 1)
                nc.scalar.activation(gatesT[:, hf, :], bank[hf][0:NGT, :], ACT.Copy).then_inc(s_gt, 1)

            def gate_exps(hf):
                act.wait_ge(s_el, hf + 1)
                if hf == 0:
                    act.wait_ge(s_bbg, 2)
                nc.scalar.activation(gl[:, 1, :], gl[:, 0, :], ACT.Exp)
                nc.scalar.activation(gl[:, 2, 0:HT], gates_of(hf)[:, :, E], ACT.Exp, scale=-1.0, bias=nb_thr[:, :]
                                     ).then_inc(s_ee, 1)

            gates_copied(0)
            hi(NTH[("x0", 6)])
            hi(NTH[("wq", 0)])
            hi(NTH[("wq", 1)])
            gate_exps(0)
            for i in range(NTH[("x0", 7)], NTH[("wq", C - 1)] + 1):
                hi(i)
            act.wait_ge(s_nat[5], 16)
            for i in range(4):
                ins = nc.scalar.activation(sign[:, i, :], bin_nat[:, i, :], ACT.Sign)
            ins.then_inc(s_sign, 1)
            gates_copied(1)
            hi(NTH[("hw", 0)])
            gate_exps(1)
            for j in range(J1):
                hi(NTH[("wo", j)])
            hi(NTH[("hw", 1)])
            for i in range(NTH[("x1", 0)], NTH[("q", J1)] + 1):
                hi(i)

            def exp1(u):
                act.wait_ge(s_m1, u + 1)
                if u >= 2:
                    act.wait_ge(s_t1, u - 1)
                for i in range(GH):
                    e = nc.scalar.activation(prob1[:, u % 2, i, :], bank[u % 2][:, i * TOK:(i + 1) * TOK], ACT.Exp,
                                             bias=nmax1[:, u % 2, i:i + 1], accum_out=rsum1[:, u % 2, i:i + 1])
                e.then_inc(s_e1, 1)

            def o1_hi(b):
                act.wait_ge(s_pv1, 2 * GH * (b + 1))
                nc.scalar.activation(o1T[0][:, :, :].rearrange("p j t -> p (j t)"), ps_pv1[:, :], ACT.Copy).then_inc(s_o1h, 1)

            exp1(0)
            exp1(1)
            for u in range(UNITS):
                if u + 1 < J1:
                    hi(NTH[("q", J1 + 1 + u)])
                if u % 8 == 4 and u >= 8:
                    o1_hi(u // 8 - 1)
                act.wait_ge(s_t1, u + 1)
                B = u // J1
                nc.scalar.activation(p1T[0][:, B % 2, :, (u % J1) * TOK:(u % J1 + 1) * TOK],
                                     turned1[u % 2][:, :].rearrange("p (g n) -> p g n", g=GH), ACT.Copy).then_inc(s_t1h, 1)
                if u + 2 < UNITS:
                    exp1(u + 2)
                if u % 8 == 0 and u >= 16:
                    hi(NTH[("x2", u // 8 - 2)])
            hi(NTH[("x2", NT - 2)])
            o1_hi(NT - 1)
            hi(NTH[("x2", NT - 1)])

        @block.vector
        def _(dve):
            def half_stats(half):
                tiles = range(half * HT, (half + 1) * HT)
                for b in tiles:
                    dve.wait_ge(s_x_in[b], 16)
                    nc.vector.bn_stats(stats[:, b, :], xres[:, b, :]).then_inc(s_stats, 1)
                for b in tiles:
                    dve.wait_ge(s_stats, b + 1)
                    nc.vector.bn_aggr(moments[:, b, :], stats[:, b, :]).then_inc(s_moments, 1)
                dve.wait_ge(s_moments, (half + 1) * HT)
                cols = slice(half * HT, (half + 1) * HT)
                nc.vector.tensor_scalar(rstd[:, cols], moments[:, cols, 1], EPS, None, ALU.add).then_inc(s_rstd, 1)

            def half_normalised(half):
                dve.wait_ge(s_pow, half + 1)
                for b in range(half * HT, (half + 1) * HT):
                    nc.vector.tensor_scalar(xn_nat[:, b, :], xres[:, b, :], moments[:, b, 0:1], rstd[:, b:b + 1],
                                            ALU.subtract, ALU.mult).then_inc(s_xn, 1)

            def turned_lo(i):
                dve.wait_ge(s_tr_hi, i + 1)
                hi, lo = turned(i)
                nc.vector.tensor_tensor(lo, turn_banks[i % 4][:, :].rearrange("p (c n) -> p c n", c=C), hi.bitcast(F32),
                                        ALU.subtract).then_inc(s_tr_lo, 1)

            nc.vector.memset(power[:, :], -0.5).then_inc(s_rstd, 1)
            half_stats(0)
            for i in range(HT):
                turned_lo(i)
            half_normalised(0)
            half_stats(1)
            for i in range(HT, NT):
                turned_lo(i)
            half_normalised(1)
            dve.wait_ge(s_gate, 1)
            nc.vector.tensor_scalar(bo_bc[:, :], bo_bc[:, :], gate[:, 0:1], None, ALU.mult).then_inc(s_bo, 1)
            dve.wait_ge(s_bias_tr, 1)
            cols = bias_all[:, :].rearrange("p (k j) -> p k j", j=G + 2)
            nc.vector.tensor_copy(cols[:, :, 0:G], bank[6][:, 0:HEADS].rearrange("p (k j) -> p k j", j=G))
            nc.vector.tensor_copy(cols[:, :, G], bank[6][:, HEADS:HEADS + KVH])
            nc.vector.tensor_copy(cols[:, :, G + 1], bank[6][:, HEADS + KVH:HEADS + 2 * KVH]).then_inc(s_bias_all, 1)
            dve.wait_ge(s_bias_all, 1)

            def minus_hi(lo, acc, hi, bias_col=None):
                if bias_col is None:
                    return nc.vector.tensor_tensor(lo, acc, hi.bitcast(F32), ALU.subtract)
                return nc.vector.scalar_tensor_tensor(lo, acc, bias_col, hi.bitcast(F32), ALU.add, ALU.subtract)

            links = [0]

            def link(ins):
                links[0] += 1
                ins.then_inc(s_chain, 1)
                dve.wait_ge(s_chain, links[0])

            def lo(i):
                dve.wait_ge(s_hi, i + 1)
                acc, hi, dst = split_views(i)
                if ORDER[i][0] == "q":
                    nc.vector.scalar_tensor_tensor(dst, acc, SCALE1, hi.bitcast(F32), ALU.mult, ALU.subtract).then_inc(s_lo, 1)
                else:
                    nc.vector.tensor_tensor(dst, acc, hi.bitcast(F32), ALU.subtract).then_inc(s_lo, 1)

            def normalise(n, made_before):
                b = n % NT
                dve.wait_ge(s_pow2, n + 1)
                if made_before:
                    dve.wait_ge(s_made, made_before)
                nc.vector.tensor_scalar(xn[:, n % 2, :], xres[:, b, :], moments[:, b, 0:1], rstd[:, b:b + 1],
                                        ALU.subtract, ALU.mult).then_inc(s_xn2, 1)

            def tile_stats(b):
                link(nc.vector.bn_stats(stats[:, b, :], xres[:, b, :]))
                link(nc.vector.bn_aggr(moments[:, b, :], stats[:, b, :]))
                nc.vector.tensor_scalar(rstd[:, b:b + 1], moments[:, b, 1:2], EPS, None, ALU.add).then_inc(s_eps, 1)

            def step(k, t, attend_next, project, started=True, ending=False):
                g = k * STEPS + t
                if t == 3 and project:
                    if started:
                        dve.wait_ge(s_vt, 2 * k + 2)
                        dve.wait_ge(s_q_lo, g + 5)
                    nc.vector.tensor_copy(bias[:, :], bias_all[:, bass.ds((k + 1) * (G + 2), G + 2)]).then_inc(s_bias, 1)
                    dve.wait_ge(s_bias, k + 2)
                if started:
                    dve.wait_ge(s_pt_hi, g + 1)
                    minus_hi(pT[1][:, :], ps_pt[:, :], pT[0][:, :]).then_inc(s_pt_lo, 1)
                if attend_next:
                    dve.wait_ge(s_scores, g + 2)
                    nc.vector.tensor_reduce(nmax[:, 0, :], ps_s[:, :].rearrange("p (g m) -> p g m", g=G), AX.X, ALU.max,
                                            negate=True).then_inc(s_max, 1)
                    dve.wait_ge(s_max, g + 2)
                    nc.vector.tensor_scalar(nmax[:, 1, :], nmax[:, 0, :], SCALE0, None, ALU.mult).then_inc(s_nmax, 1)
                if attend_next:
                    dve.wait_ge(s_exp, g + 2)
                    nc.vector.reciprocal(rinv[:, :], rsum[:, :]).then_inc(s_rinv, 1)
                if ending:
                    for name in AHEAD.get(t, ()):
                        lo(NTH[name])
                if started:
                    dve.wait_ge(s_o_hi, g + 1)
                    minus_hi(oT[1][:, :, :].rearrange("p g t -> p (g t)"), ps_o[:, :],
                             oT[0][:, :, :].rearrange("p g t -> p (g t)")).then_inc(s_o_lo, 1)
                if project:
                    h, half = q_head_half(t)
                    cols = slice(half * HALF, (half + 1) * HALF)
                    dve.wait_ge(s_q_hi, g + 6)
                    minus_hi(qT[1][:, h, cols], ps_q[:, :], qT[0][:, h, cols], bias[:, h:h + 1]).then_inc(s_q_lo, 1)
                if not started and t in TURN_AT:
                    for i in TURN_AT[t]:
                        turned_lo(i)
                if (t == 3 and started) or (t == 7 and attend_next):
                    c, bs = (2, slice(4, 8)) if t == 3 else (3, slice(0, 4))
                    dve.wait_ge(s_v_hi, 2 * k + c)
                    minus_hi(v[1][:, bs, :].rearrange("p b d -> p (b d)"), ps_vt[:, :],
                             v[0][:, bs, :].rearrange("p b d -> p (b d)")).then_inc(s_v_lo, 1)
                if project and t in (0, 4):
                    c, half = (2, 1) if t == 0 else (3, 0)
                    cols = slice(half * HALF, (half + 1) * HALF)
                    dve.wait_ge(s_k_hi, 2 * k + c)
                    minus_hi(kT[1][:, cols], ps_kv[:, :], kT[0][:, cols], bias[:, G:G + 1]).then_inc(s_k_lo, 1)
                if ending:
                    if t > 0:
                        dve.wait_ge(s_acc, g)
                        tile_stats(t - 1)
                    for name in BEHIND.get(t, ()):
                        lo(NTH[name])
                    for b in NORMALISED.get(t, ()):
                        normalise(b, NTH[("x0", b - 2)] + 1 if b >= 2 else 0)
                if started:
                    dve.wait_ge(s_out, g + 1)
                    nc.vector.scalar_tensor_tensor(xres[:, t, :], ps_out[:, :], gate[:, 0:1], xres[:, t, :],
                                                   ALU.mult, ALU.add).then_inc(s_acc, 1)

            for t in range(STEPS):
                step(-1, t, t == STEPS - 1, t >= 3, started=False)
            dve.wait_ge(s_xres, NT)
            with dve.Fori(0, KVH - 1) as k:
                for t in range(STEPS):
                    step(k, t, True, True)
            for t in range(STEPS):
                step(KVH - 1, t, t < STEPS - 1, t < 3, ending=True)

            dve.wait_ge(s_acc, KVH * STEPS)
            tile_stats(NT - 1)
            dve.wait_ge(s_bb, 16)
            nc.vector.tensor_scalar(b_base_bc[:, :], b_base_bc[:, :], gate[:, 2:3], None, ALU.mult).then_inc(s_bbg, 1)
            dve.wait_ge(s_thr_in, 16)
            nc.vector.tensor_scalar(nb_thr[:, :], nb_thr[:, :], -1.0, None, ALU.mult).then_inc(s_bbg, 1)
            def gate_logits(hf):
                dve.wait_ge(s_gturned, hf + 1)
                logits = gates_of(hf)[:, :, 0:E]
                link(nc.vector.tensor_reduce(gl[:, 3, 0:HT], logits, AX.X, ALU.max, negate=True))
                nc.vector.tensor_tensor(gl[:, 0, :].rearrange("p (t e) -> p t e", e=E), logits,
                                        gl[:, 3, 0:HT].unsqueeze(2).broadcast_to([P, HT, E]), ALU.add).then_inc(s_el, 1)

            def weigh(hf):
                dve.wait_ge(s_ee, hf + 1)

                def te(i):
                    return gl[:, i, :].rearrange("p (t e) -> p t e", e=E)

                def over_e(i):
                    return gl[:, i, 0:HT].unsqueeze(2).broadcast_to([P, HT, E])

                link(nc.vector.tensor_reduce(gl[:, 4, 0:HT], te(1), AX.X, ALU.add))
                link(nc.vector.reciprocal(gl[:, 5, 0:HT], gl[:, 4, 0:HT]))
                link(nc.vector.tensor_tensor(te(6), te(1), over_e(5), ALU.mult))
                link(nc.vector.tensor_scalar(gl[:, 7, 0:HT], gl[:, 2, 0:HT], 1.0, None, ALU.add))
                link(nc.vector.reciprocal(gl[:, 8, 0:HT], gl[:, 7, 0:HT]))
                link(nc.vector.tensor_scalar(gl[:, 9, 0:HT], gl[:, 8, 0:HT], THR_MAX, None, ALU.mult))
                link(nc.vector.tensor_tensor(te(10), te(6), over_e(9), ALU.subtract))
                link(nc.vector.tensor_scalar(gl[:, 11, :], gl[:, 10, :], 0.0, None, ALU.max))
                link(nc.vector.tensor_reduce(gl[:, 12, 0:HT], te(11), AX.X, ALU.add))
                link(nc.vector.scalar_tensor_tensor(gl[:, 13, 0:HT], gl[:, 12, 0:HT], 0.0, gl[:, 12, 0:HT],
                                                    ALU.is_equal, ALU.add))
                link(nc.vector.reciprocal(gl[:, 14, 0:HT], gl[:, 13, 0:HT]))
                link(nc.vector.tensor_tensor(te(15), te(11), over_e(14), ALU.mult))
                if hf:
                    dve.wait_ge(s_made, NTH[("hw", 0)] + 1)
                nc.vector.tensor_copy(wide[:, :, :].rearrange("p t (e r) -> p (t e) r", r=R),
                                      gl[:, 15, :].unsqueeze(2).broadcast_to([P, HT * E, R])).then_inc(s_wide, 1)

            def weighted(hf):
                i = NTH[("hw", hf)]
                dve.wait_ge(s_wideT, hf + 1)
                nc.vector.tensor_tensor(hw[:, :], adaptersT(hf)[:, :], hw[:, :], ALU.mult).then_inc(s_hw, 1)
                lo(i)

            def add_ffn0(b):
                dve.wait_ge(s_f0, b + 1)
                dve.wait_ge(s_xb, b + 1)
                nc.vector.scalar_tensor_tensor(xres[:, b, :], bank[b % 2][:, :], gate[:, 2:3], xres[:, b, :],
                                               ALU.mult, ALU.add).then_inc(s_x2, 1)
                dve.wait_ge(s_x2, b + 1)
                tile_stats(b)

            lo(NTH[("x0", 6)])
            normalise(7, NTH[("x0", 5)] + 1)
            gate_logits(0)
            lo(NTH[("wq", 0)])
            lo(NTH[("wq", 1)])
            lo(NTH[("x0", 7)])
            weigh(0)
            lo(NTH[("wq", 2)])
            lo(NTH[("wq", 3)])
            dve.wait_ge(s_nat[5], 16)
            nc.vector.tensor_reduce(scale[:, 0, :], bin_nat[:, :, :], AX.X, ALU.add, apply_absolute_value=True
                                    ).then_inc(s_wscale, 1)
            dve.wait_ge(s_wscale, 1)
            nc.vector.tensor_scalar(scale[:, 1, :], scale[:, 0, :], 1.0 / D, None, ALU.mult).then_inc(s_wscale, 1)
            weighted(0)
            gate_logits(1)
            weigh(1)
            for b in range(HT):
                add_ffn0(b)
                if b == 1:
                    for j in range(J1):
                        lo(NTH[("wo", j)])
                    weighted(1)
            for b in (0, 1):
                normalise(NT + b, NTH[("x0", NT - 2 + b)] + 1)
            dve.wait_ge(s_wscale, 2)
            dve.wait_ge(s_clip, 1)
            for i in range(4):
                ins = nc.vector.scalar_tensor_tensor(sign[:, i, :], sign[:, i, :], scale[:, 1, i:i + 1], bin_nat[:, i, :],
                                                     ALU.mult, ALU.subtract)
            ins.then_inc(s_unclipped, 1)
            for b in range(HT, NT):
                add_ffn0(b)
                lo(NTH[("x1", b - HT)])
                normalise(NT + b - HT + 2, NTH[("x1", b - HT)] + 1)
            dve.wait_ge(s_small2, 16)
            for i in range(GH):
                ins = nc.vector.tensor_scalar(negmask[:, i, :], mask_in[:, :], MASKED, -MASKED, ALU.mult, ALU.add)
            ins.then_inc(s_mask, 1)
            for i in range(NTH[("bin", 0)], NTH[("q", J1)] + 1):
                lo(i)
                kind, b = ORDER[i]
                if kind == "x1" and b + 2 < NT:
                    normalise(NT + b + 2, i + 1)

            def max1(u):
                dve.wait_ge(s_s1, u + 1)
                nc.vector.tensor_reduce(nmax1[:, u % 2, :], bank[u % 2][:, :].rearrange("p (g m) -> p g m", g=GH), AX.X, ALU.max,
                                        negate=True).then_inc(s_m1, 1)

            def invert1(u):
                dve.wait_ge(s_e1, u + 1)
                if u >= 2:
                    dve.wait_ge(s_n1, u - 1)
                nc.vector.reciprocal(rinv1[:, u % 2, :], rsum1[:, u % 2, :]).then_inc(s_r1, 1)

            def o1_lo(b):
                dve.wait_ge(s_o1h, b + 1)
                minus_hi(o1T[1][:, :, :].rearrange("p j t -> p (j t)"), ps_pv1[:, :],
                         o1T[0][:, :, :].rearrange("p j t -> p (j t)")).then_inc(s_o1l, 1)

            def add_out1(b):
                dve.wait_ge(s_out1, b + 1)
                nc.vector.scalar_tensor_tensor(xres[:, b, :], bank[5][:, :], gate[:, 1:2], xres[:, b, :],
                                               ALU.mult, ALU.add).then_inc(s_x3, 1)
                dve.wait_ge(s_x3, b + 1)
                tile_stats(b)

            def norm_x3(b):
                normalise(2 * NT + b, NTH[("x1", NT - 2 + b)] + 1 if b < 2 else NTH[("x2", b - 2)] + 1)

            def add_ffn1(b):
                dve.wait_ge(s_f1, b + 1)
                nc.vector.scalar_tensor_tensor(xres[:, b, :], bank[6][:, :], gate[:, 3:4], xres[:, b, :],
                                               ALU.mult, ALU.add).then_inc(s_x4, 1)

            for u in (0, 1):
                max1(u)
                invert1(u)
            for u in range(UNITS):
                if u + 1 < J1:
                    lo(NTH[("q", J1 + 1 + u)])
                if u % 8 == 4 and u >= 8:
                    o1_lo(u // 8 - 1)
                if u + 2 < UNITS:
                    max1(u + 2)
                dve.wait_ge(s_t1h, u + 1)
                B = u // J1
                cols = slice((u % J1) * TOK, (u % J1 + 1) * TOK)
                nc.vector.tensor_tensor(p1T[1][:, B % 2, :, cols], turned1[u % 2][:, :].rearrange("p (g n) -> p g n", g=GH),
                                        p1T[0][:, B % 2, :, cols].bitcast(F32), ALU.subtract).then_inc(s_t1l, 1)
                if u + 2 < UNITS:
                    invert1(u + 2)
                if u % 8 == 5 and u >= 8:
                    add_out1(u // 8 - 1)
                if u % 8 == 7 and u >= 8:
                    norm_x3(u // 8 - 1)
                if u % 8 == 0 and u >= 16:
                    lo(NTH[("x2", u // 8 - 2)])
                if u % 8 == 2 and u >= 16:
                    add_ffn1(u // 8 - 2)
            lo(NTH[("x2", NT - 2)])
            add_ffn1(NT - 2)
            o1_lo(NT - 1)
            add_out1(NT - 1)
            norm_x3(NT - 1)
            lo(NTH[("x2", NT - 1)])
            add_ffn1(NT - 1)

        @block.tensor
        def _(pe):
            def turn_tile(i):
                what, b = TURNED[i]
                if what == "ctx":
                    pe.wait_ge(s_ctx_in[b], 16)
                else:
                    pe.wait_ge(s_xn, b + 1)
                if i >= 4:
                    pe.wait_ge(s_tr_lo, i - 3)
                src = ctx_nat if what == "ctx" else xn_nat
                for c in range(C):
                    mm = nc.tensor.transpose(turn_banks[i % 4][:, c * P:(c + 1) * P], src[:, b, c * P:(c + 1) * P], ident[:, :])
                mm.then_inc(s_tr, 1)

            pe.wait_ge(s_ident, 1)
            for i in range(NT):
                turn_tile(i)
            pe.wait_ge(s_small_in, 80)
            nb = HEADS + 2 * KVH
            nc.tensor.transpose(bank[6][:, 0:nb], bias_nat[:, :], ident[0:nb, 0:nb]).then_inc(s_bias_tr, 1)

            def terms(acc, pairs, first=True, last=True):
                todo = [(st[a], mv[b]) for st, mv in pairs for a, b in ((1, 0), (0, 1), (0, 0))]
                return [(acc, st, mv, first and i == 0, last and i == len(todo) - 1) for i, (st, mv) in enumerate(todo)]

            def matmul(term):
                acc, st, mv, start, stop = term
                return nc.tensor.matmul(acc, st, mv, start=start, stop=stop)

            def part(acc, pairs, first, last):
                for term in terms(acc, pairs, first, last):
                    mm = matmul(term)
                return mm

            def product(acc, pairs):
                return part(acc, pairs, True, True)

            def both(pair, *index):
                return [a[index] for a in pair]

            every = slice(None)

            def bank_free(i):
                if ORDER[i][0] == "x2":
                    pe.wait_ge(s_lo, i)
                elif i >= 4:
                    pe.wait_ge(s_lo, i - 3)
                elif i == 3:
                    pe.wait_ge(s_v_lo, 2 * KVH)
                elif i == 2:
                    pe.wait_ge(s_vt, 2 * KVH)
                elif i == 0:
                    pe.wait_ge(s_q_lo, KVH * STEPS)

            def nat_rows(lo, c):
                return nat[:, :, :].rearrange("p a n -> p (a n)")[:, lo * D + c * P:lo * D + (c + 1) * P]

            def make(name):
                kind, n = name
                i = NTH[name]
                acc = split_bank(i)
                bank_free(i)
                if kind in ("k", "q"):
                    if kind == "k":
                        w, col, src, hf = wk1, every, cT, n
                        pe.wait_ge(s_lo, NTH[("wk", 0)] + 1)
                    else:
                        w, col, src, hf = wq1, slice(n % J1 * P, (n % J1 + 1) * P), xT, n // J1
                        pe.wait_ge(s_lo, NTH[("x1", HT - 1 if hf == 0 else NT - 1)] + 1)
                    cols = slice(hf * HALF, (hf + 1) * HALF)
                    product(acc[:, :], [(both(w, every, c, col), both(src, every, c, cols)) for c in range(C)]).then_inc(s_made, 1)
                    return
                if kind == "v":
                    pe.wait_ge(s_lo, NTH[("wv", 0)] + 1)
                    for b in range(HT):
                        tok = slice((n * HT + b) * TOK, (n * HT + b + 1) * TOK)
                        mm = product(acc[:, b * KV1:(b + 1) * KV1],
                                     [(both(cT, every, c, tok), both(wv1, every, c, every)) for c in range(C)])
                    mm.then_inc(s_made, 1)
                    return
                if kind == "base":
                    pe.wait_ge(s_nat[1], 16)
                    blocks = [nat_rows(i, n) for i in range(4)]
                elif kind == "adapt":
                    pe.wait_ge(s_nat[2], 16 * 7)
                    blocks = [nat_rows(6, c) for c in range(C)]
                elif kind == "gates":
                    blocks = [gates_nat[:, c * P:(c + 1) * P] for c in range(C)]
                elif kind == "up":
                    blocks = [nat_rows(7, i) for i in range(4)]
                elif kind == "wk":
                    pe.wait_ge(s_nat[0], 32)
                    blocks = [nat_rows(4, c) for c in range(C)]
                elif kind == "wv":
                    blocks = [nat_rows(5, c) for c in range(C)]
                elif kind == "wq":
                    pe.wait_ge(s_nat[3], 16 * J1)
                    blocks = [q1_nat[:, j, n * P:(n + 1) * P] for j in range(J1)]
                elif kind == "hw":
                    pe.wait_ge(s_wide, n + 1)
                    blocks = [wide[:, t, :] for t in range(HT)]
                elif kind == "wo":
                    pe.wait_ge(s_perm, 1)
                    blocks = [nat_rows(4 + i, n) for i in range(4)]
                elif kind == "bin":
                    pe.wait_ge(s_bin, 1)
                    blocks = [bin_nat[:, i, n * P:(n + 1) * P] for i in range(4)]
                else:
                    tile = ("x0", "x1", "x2").index(kind) * NT + n
                    pe.wait_ge(s_xn2, tile + 1)
                    blocks = [xn[:, tile % 2, c * P:(c + 1) * P] for c in range(C)]
                col = 0
                for src in blocks:
                    m = src.shape[0]
                    mm = nc.tensor.transpose(acc[:, col:col + m], src, ident[0:m, 0:m])
                    col += m
                mm.then_inc(s_made, 1)

            def step(k, t, attend_next, project, started=True, ending=False):
                g = k * STEPS + t
                b = (t + 1) % NT

                def q_part(cs):
                    h, half = q_head_half(t)
                    cols = slice(half * HALF, (half + 1) * HALF)
                    mm = part(ps_q[:, :], [(both(wq, every, h, c, every), both(xT, every, c, cols)) for c in cs],
                              cs[0] == 0, cs[-1] == C - 1)
                    if cs[-1] == C - 1:
                        mm.then_inc(s_qproj, 1)

                if started:
                    pe.wait_ge(s_norm, g + 1)
                    for j in range(G):
                        mm = nc.tensor.transpose(ps_pt[:, j * TOK:(j + 1) * TOK], prob[:, j, :], ident[:, :])
                    mm.then_inc(s_ptr, 1)
                if attend_next:
                    if b == 0:
                        pe.wait_ge(s_q_lo, k * STEPS + 12)
                        pe.wait_ge(s_k_lo, 2 * k + 3)
                    if b == 4:
                        pe.wait_ge(s_q_lo, k * STEPS + 8)
                        pe.wait_ge(s_k_lo, 2 * k + 2)
                    tok = slice(b * TOK, (b + 1) * TOK)
                    for j in range(G):
                        mm = product(ps_s[:, j * TOK:(j + 1) * TOK], [(both(qT, every, j, tok), both(kT, every, tok))])
                    mm.then_inc(s_scores, 1)
                if project:
                    if not started and t in (3, 7):
                        pe.wait_ge(s_tr_lo, NT if t == 3 else NTR)
                    if 3 <= t <= 6:
                        pe.wait_ge(s_w_lo, (k + 1) * NS + SLICES.index(("q", q_head_half(t)[0])) + 1)
                    if started or t > 3:
                        pe.wait_ge(s_q_lo, g + 5)
                    q_part((0, 1))
                if ending:
                    for name in AHEAD.get(t, ()):
                        make(name)
                if started:
                    pe.wait_ge(s_pt_lo, g + 1)
                    if t in (0, 4):
                        pe.wait_ge(s_v_lo, 2 * k + (1 if t == 0 else 2))
                    product(ps_o[:, :], [(both(v, every, t, every), both(pT, every, every))]).then_inc(s_pv, 1)
                if ending:
                    for name in BEHIND.get(t, ()):
                        make(name)
                if project:
                    key = t in (3, 4, 7, 0)
                    first = t in (3, 7, 1, 5)
                    half = 0 if 3 <= t <= 6 else 1
                    w = wk if key else wv
                    if t == 3:
                        pe.wait_ge(s_w_lo, (k + 1) * NS + SLICES.index(("k", 0)) + 1)
                        if started:
                            pe.wait_ge(s_vt, 2 * k + 2)
                    if t == 7:
                        pe.wait_ge(s_vt, 2 * k + 3)
                    if t == 5:
                        pe.wait_ge(s_w_lo, (k + 1) * NS + SLICES.index(("v", 0)) + 1)
                        pe.wait_ge(s_k_lo, 2 * k + 3)
                    if t == 1:
                        pe.wait_ge(s_k_lo, 2 * k + 2)
                    cols = slice(half * HALF, (half + 1) * HALF)
                    mm = part(ps_kv[:, :], [(both(w, every, c, every), both(cT, every, c, cols))
                                            for c in ((0, 1) if first else (2, 3))], first, not first)
                    if not first:
                        mm.then_inc(s_kproj if key else s_vproj, 1)
                    q_part((2, 3))
                if not started and t in TURN_AT:
                    for i in TURN_AT[t]:
                        turn_tile(i)
                if (t == 3 and started) or (t == 7 and attend_next):
                    c = 2 if t == 3 else 3
                    pe.wait_ge(s_vt, 2 * k + c)
                    if started:
                        pe.wait_ge(s_v_lo, 2 * k + c - 1)
                    for i in range(4):
                        mm = nc.tensor.transpose(ps_vt[:, i * DH:(i + 1) * DH], vT[:, i, :], ident[:, :])
                    mm.then_inc(s_vtr, 1)
                if started:
                    if t == 0:
                        pe.wait_ge(s_w_lo, (k + 1) * NS)
                    pe.wait_ge(s_o_lo, g + 1)
                    if t > 0:
                        pe.wait_ge(s_acc, g)
                    else:
                        pe.wait_ge(s_nmax, g + 2)
                    product(ps_out[:, :], [(both(oT, every, j, every),
                                            both(wo, every, bass.ds((k % 2) * (G * D) + j * D, D))) for j in range(G)]
                            ).then_inc(s_out, 1)

            for t in range(STEPS):
                step(-1, t, t == STEPS - 1, t >= 3, started=False)
            with pe.Fori(0, KVH - 1) as k:
                for t in range(STEPS):
                    step(k, t, True, True)
            for t in range(STEPS):
                step(KVH - 1, t, t < STEPS - 1, t < 3, ending=True)

            def adapters_down(hf):
                cols = slice(hf * HALF, (hf + 1) * HALF)
                pe.wait_ge(s_lo, max(NTH[("gates", 0)], NTH[("x0", (hf + 1) * HT - 1)]) + 1)
                if hf == 1:
                    pe.wait_ge(s_acc, KVH * STEPS)
                product(bank[hf][0:NGT, :], [(both(wg, every, c, every), both(xT, every, c, cols)) for c in range(C)]
                        ).then_inc(s_gtmade, 1)
                if hf == 1:
                    make(("hw", 0))
                product(adaptersT(hf)[:, :], [(both(wa, every, c, every), both(xT, every, c, cols)) for c in range(C)])

            def turn_gates(hf):
                pe.wait_ge(s_gt, hf + 1)
                for t in range(HT):
                    mm = nc.tensor.transpose(gates_of(hf)[:, t, :], gatesT[:, hf, t * TOK:(t + 1) * TOK], ident[0:NGT, 0:NGT])
                mm.then_inc(s_gturned, 1)

            def ffn0(b):
                tok = slice(b * TOK, (b + 1) * TOK)
                t = b % HT
                if b >= 2:
                    pe.wait_ge(s_x2, b - 1)
                if b == 1:
                    pe.wait_ge(s_ee, 2)
                pe.wait_ge(s_lo, NTH[("hw", b // HT)] + 1)
                product(bank[b % 2][:, :],
                        [(both(xT, every, c, tok), both(wb, every, c, every)) for c in range(C)]
                        + [(both(hwT[b // HT], every, slice(t * TOK, (t + 1) * TOK)), both(wB, every, every))]).then_inc(s_f0, 1)

            adapters_down(0)
            make(("x0", 6))
            turn_gates(0)
            for i in range(NTH[("wq", 0)], NTH[("wq", C - 1)] + 1):
                make(ORDER[i])
            adapters_down(1)
            turn_gates(1)
            ffn0(0)
            ffn0(1)
            for j in range(J1):
                make(("wo", j))
            make(("hw", 1))
            ffn0(2)
            ffn0(3)
            for b in range(HT, NT):
                ffn0(b)
                make(("x1", b - HT))
            for i in range(NTH[("bin", 0)], NTH[("q", J1)] + 1):
                make(ORDER[i])

            def scores1(u):
                B, j = u // J1, u % J1
                b, gh = B // 2, B % 2
                tok = slice(b * TOK, (b + 1) * TOK)
                if u >= 2:
                    pe.wait_ge(s_e1, u - 1)
                if u == 0:
                    pe.wait_ge(s_lo, NTH[("q", J1 - 1)] + 1)
                    pe.wait_ge(s_mask, 1)
                    pe.wait_ge(s_idr, 1)
                if b == HT:
                    pe.wait_ge(s_lo, NTH[("q", 2 * J1 - 1)] + 1)
                pe.wait_ge(s_kd, 2 * (B + 1))
                acc = bank[u % 2][:, :]
                nc.tensor.matmul(acc, ident_r[:, :], negmask[:, :, :].rearrange("p g m -> p (g m)"), start=True, stop=False)
                for i, (a, c) in enumerate(((1, 0), (0, 1), (0, 0))):
                    mm = nc.tensor.matmul(acc, q1T[a][:, j, tok], kd[c][:, gh, :, :].rearrange("p g m -> p (g m)"),
                                          start=False, stop=(i == 2))
                mm.then_inc(s_s1, 1)

            def pv1(B, i):
                b, gh = B // 2, B % 2
                if i == 0:
                    if B == 0:
                        pe.wait_ge(s_lo, NTH[("q", 2 * J1 - 1)] + 1)
                    pe.wait_ge(s_t1l, J1 * (B + 1))
                    pe.wait_ge(s_vd, 2 * (B + 1))
                    if gh == 0 and b >= 1:
                        pe.wait_ge(s_o1l, b)
                part(ps_pv1[:, :], [(both(vd, every, gh, i, every), both(p1T, every, gh, i, every))],
                     gh == 0 and i == 0, gh == 1 and i == GH - 1).then_inc(s_pv1, 1)

            def turn_prob1(u):
                pe.wait_ge(s_n1, u + 1)
                if u >= 2:
                    pe.wait_ge(s_t1l, u - 1)
                for i in range(GH):
                    mm = nc.tensor.transpose(turned1[u % 2][:, i * TOK:(i + 1) * TOK], prob1[:, u % 2, i, :], ident[:, :])
                mm.then_inc(s_t1, 1)

            def out1(b):
                pe.wait_ge(s_o1l, b + 1)
                if b >= 1:
                    pe.wait_ge(s_x3, b)
                product(bank[5][:, :], [(both(o1T, every, j, every), both(wo1, every, j, every)) for j in range(J1)]).then_inc(s_out1, 1)

            def turn_x3(b):
                make(("x2", b))

            def ffn1(b):
                pe.wait_ge(s_lo, NTH[("x2", b)] + 1)
                if b >= 1:
                    pe.wait_ge(s_x4, b)
                tok = slice(b * TOK, (b + 1) * TOK)
                product(bank[6][:, :], [(both(xT, every, c, tok), both(wf1, every, c, every)) for c in range(C)]).then_inc(s_f1, 1)

            scores1(0)
            scores1(1)
            for u in range(UNITS):
                if u + 1 < J1:
                    make(("q", J1 + 1 + u))
                B = u // J1
                if u >= J1 + 1 and u % J1 != 1:
                    pv1((u - 1) // J1 - 1, (u - 1) % J1)
                turn_prob1(u)
                if u + 2 < UNITS:
                    scores1(u + 2)
                if u >= J1 + 1 and u % J1 == 1:
                    pv1((u - 1) // J1 - 1, 0)
                if u % 8 == 5 and u >= 8:
                    out1(u // 8 - 1)
                if u % 8 == 0 and u >= 16:
                    turn_x3(u // 8 - 2)
                if u % 8 == 2 and u >= 16:
                    ffn1(u // 8 - 2)
            pv1(2 * NT - 2, GH - 1)
            for i in range(GH):
                pv1(2 * NT - 1, i)
            turn_x3(NT - 2)
            ffn1(NT - 2)
            out1(NT - 1)
            turn_x3(NT - 1)
            ffn1(NT - 1)


_INS = ["x", "ctx_4096", "mask_SxS2_bk0", "g_xattn", "g_ffn", "L0_xattn_Wq", "L0_xattn_bq", "L0_xattn_Wkv", "L0_xattn_bkv",
        "L0_xattn_Wo", "L0_xattn_bo", "L0_ffn_W_base", "L0_ffn_b_base", "L0_ffn_W_gate", "L0_ffn_W_thr", "L0_ffn_b_thr",
        "L0_ffn_A_w", "L0_ffn_B_w", "L1_xattn_w_q", "L1_xattn_w_k", "L1_xattn_w_v", "L1_xattn_w_out", "L1_ffn_weight"]
_OUTS = [((8, 128, 512), "float32")]


def kernel(**inputs):
    import numpy as _np
    import concourse.bacc as _bacc
    from concourse import mybir as _mybir
    from concourse.bass_utils import run_bass_kernel_spmd as _run

    nc = _bacc.Bacc("TRN2", target_bir_lowering=False, num_devices=1)
    arrays, args = {}, []
    for name in _INS:
        a = _np.ascontiguousarray(inputs[name])
        arrays[f"in_{name}_dram"] = a
        args.append(nc.dram_tensor(f"in_{name}_dram", a.shape, _mybir.dt.from_np(a.dtype), kind="ExternalInput").ap())
    for i, (shape, dtype) in enumerate(_OUTS):
        dt = _mybir.dt.from_np(_np.dtype(dtype))
        args.append(nc.dram_tensor(f"out_{i}_dram", shape, dt, kind="ExternalOutput").ap())
    build(nc, *args)
    r = _run(nc, [arrays], core_ids=[0])
    return r.results[0]["out_0_dram"]
```

```python
from contextlib import ExitStack

import numpy as np

import concourse.bass as bass
from concourse import mybir

ALU = mybir.AluOpType
ACT = mybir.ActivationFunctionType
AX = mybir.AxisListType
F32 = mybir.dt.float32
F32R = mybir.dt.float32r
P = 128


def build(nc, x, ctx_in, mask, g_xattn, g_ffn, Wq, bq, Wkv, bkv, Wo, bo, W_base, b_base, W_gate, W_thr, b_thr, A_w, B_w,
          w_q, w_k, w_v, w_out, w_bin, out):
    BATCH, TOK, D = x.shape
    DH = P
    HEADS = Wq.shape[1] // DH
    KVH = Wkv.shape[1] // (2 * DH)
    G = HEADS // KVH
    C = D // P
    NT = BATCH
    HALF = NT * TOK // 2
    STEPS = NT
    SCALE0 = float(1.0 / np.sqrt(DH))
    EPS = 1e-5
    SLOTS = 2

    SLICES = [("q", 0), ("k", 0), ("q", 1), ("q", 2), ("o", 0), ("q", 3), ("v", 0), ("o", 1), ("o", 2), ("o", 3)]
    SPLIT_AT = {0: [0], 1: [1, 2], 2: [3, 4], 3: [5, 6], 4: [7], 5: [8], 6: [9], 7: []}
    NS = len(SLICES)

    E, R = A_w.shape[0], A_w.shape[1]
    NGT = E + 2
    ADAPT = 2.0
    THR_MAX = 0.125
    KV1 = w_k.shape[0]
    DH1 = D // HEADS
    G1 = KV1 // DH1
    J1 = HEADS // G1
    GH = G1 // 2
    SCALE1 = float(DH1) ** -0.5
    MASKED = float((2 - 2.0 ** -11) * 2.0 ** 127)
    UB = 2 * J1
    UNITS = NT * UB
    HT = NT // 2
    DEPTH1 = 3

    x_rows = x.rearrange("b t d -> t b d")
    ctx_rows = ctx_in.rearrange("b t d -> t b d")
    wq_rows = Wq.rearrange("(c p) n -> p c n", p=P)
    wkv_rows = Wkv.rearrange("(c p) n -> p c n", p=P)
    wo_rows = Wo.rearrange("(h p) n -> h p n", p=P)

    with ExitStack() as es:
        def sem(name):
            return es.enter_context(nc.semaphore(name))

        bank = [es.enter_context(nc.psum_tensor(f"bank{i}", [P, 512], F32)) for i in range(8)]
        ps_pt, ps_o, ps_q, ps_out, ps_kv, ps_vt = bank[1:7]
        ps_s = (bank[0], bank[7])

        KI = 1024
        first_byte = -(-nc.sbuf_base // 64) * 64

        def at(kib, name, shape, dt=F32):
            return nc.alloc_sbuf_tensor_at(name, shape, dt, offset=first_byte + int(kib * KI))

        def pair(kib, name, shape, lo_kib=None):
            size = 4 * int(np.prod(shape[1:])) / KI
            return [at(kib, name + "_hi", shape, F32R), at(kib + size if lo_kib is None else lo_kib, name + "_lo", shape, F32R)]

        xres = at(0, "xres", [P, NT, D])
        xT = pair(16, "xT", [P, C, NT * TOK])
        cT = pair(48, "cT", [P, C, NT * TOK])
        A0 = 80
        qT = pair(A0, "qT", [P, G, NT * TOK])
        kT = at(A0 + 32, "kT", [P, NT, 2, TOK], F32R)
        score = at(A0 + 122, "scores", [P, G, TOK])
        v = pair(A0 + 40, "v", [P, NT, DH])
        vT = at(A0 + 48, "vT", [P, 4, TOK])
        wq = pair(A0 + 50, "wq", [P, G, C, DH])
        wk = pair(A0 + 66, "wk", [P, C, DH])
        wv = pair(A0 + 70, "wv", [P, C, DH])
        wo = pair(A0 + 74, "wo", [P, 2 * G * D])
        stage = at(A0 + 106, "stage", [P, SLOTS, 512])
        prob = at(A0 + 110, "prob", [P, G, TOK])
        pT = pair(A0 + 112, "pT", [P, 512])
        oT = pair(A0 + 116, "oT", [P, G, TOK])
        ctx_nat = at(A0, "ctx_nat", [P, NT, D])
        xn_nat = at(A0 + 16, "xn_nat", [P, NT, D])
        bias_nat = at(A0 + 32, "bias_nat", [HEADS + 2 * KVH, DH])
        bo_bc = at(A0 + 118, "bo_bc", [P, D])
        stage_v = at(A0 + 40, "stage_v", [P, 4, 512])
        stage_p = at(A0 + 110, "stage_p", [P, 4, 512])
        first_stage = [stage[:, i, :] for i in (0, 1)] + [stage_v[:, i, :] for i in range(4)] + [stage_p[:, i, :] for i in range(4)]
        wb = pair(A0, "w_base", [P, C, D])
        wa = pair(A0 + 16, "w_adapt", [P, C, E * R])
        wB = pair(A0 + 20, "w_up", [E * R, D])
        wq1 = pair(A0 + 66, "w_q1", [P, C, D], A0 + 24)
        wo1 = pair(A0 + 40, "w_o1", [P, J1, D], A0 + 82)
        b_base_bc = at(A0 + 48, "b_base_bc", [P, D])
        nat = at(A0 + 50, "nat", [P, 2, 4 * D])
        wk1 = pair(A0 + 66, "w_k1", [P, C, KV1])
        wv1 = pair(A0 + 70, "w_v1", [P, C, KV1])
        k1T = pair(A0 + 74, "k1T", [KV1, NT * TOK])
        v1 = pair(A0 + 90, "v1", [P, NT, KV1])
        wf1 = pair(A0 + 98, "w_f1", [P, C, D], A0 + 110)
        xn = at(A0 + 106, "xn", [P, 2, D])
        wide = at(A0 + 118, "weights_wide", [P, HT, E * R])
        gates_nat = at(A0 + 120, "gates_nat", [NGT, D])
        hwT = [pair(A0 + (120, 98)[hf], f"hwT{hf}", [E * R, HT * TOK]) for hf in (0, 1)]
        gl = at(48, "gate_work", [P, 16, HT * E])
        hw = at(50, "adapters_weighted", [P, HT * TOK])
        gatesT = at(52, "gatesT", [NGT, 2, HT * TOK])
        bin_nat = at(56, "w_bin_nat", [P, 4, D])
        q1_nat = at(64, "w_q1_nat", [P, J1, D])
        o1_nat = at(72, "w_o1_nat", [P, 4, D])
        sign = at(A0 + 110, "sign", [P, 4, D])
        q1T = pair(48, "q1T", [P, J1, NT * TOK])
        p1T = pair(A0, "p1T", [P, 2, GH, J1 * TOK])
        o1T = pair(A0 + 32, "o1T", [KV1, J1, TOK])
        prob1 = [at(A0 + (36, 38, 118)[i], f"prob1_{i}", [P, GH, TOK]) for i in range(DEPTH1)]
        negmask = at(A0 + 48, "negmask", [P, GH, TOK], F32R)
        kd = pair(A0 + 50, "k_by_group", [KV1, 2, GH, TOK])
        vd = pair(A0 + 58, "v_by_group", [P, 2, GH, KV1])
        small_at = [A0 + 124.0]

        def small(name, shape, dt=F32):
            size = -(-int(np.prod(shape[1:])) * (1 if dt == mybir.dt.uint8 else 4) // 32) * 32
            small_at[0] += size / KI
            return at(small_at[0] - size / KI, name, shape, dt)

        ident = small("ident", [P, P])
        ident_r = small("ident_r", [P, P], F32R)
        gate_raw = small("gate_raw", [P, 4])
        gate = small("gate", [P, 4])
        stats = small("stats", [P, NT, 6])
        moments = small("moments", [P, NT, 2])
        rstd = small("rstd", [P, NT])
        power = small("power", [P, NT])
        bias_all = small("bias_all", [P, KVH * (G + 2)])
        bias = small("bias", [P, G + 2])
        nmax = small("nmax", [P, 2, G])
        rsum = small("rsum", [P, G])
        rinv = small("rinv", [P, G])
        wg = [small("w_gates_hi", [P, C, NGT], F32R), small("w_gates_lo", [P, C, NGT], F32R)]
        nb_thr = small("nb_thr", [P, 1])
        scale = small("w_bin_scale_cols", [P, 2, 4])
        mask_in = small("mask_in", [P, TOK], mybir.dt.uint8)
        group_of = small("group_of", [P, G1])
        nmax1 = small("nmax1", [P, DEPTH1, GH])
        rsum1 = small("rsum1", [P, DEPTH1, GH])
        rinv1 = small("rinv1", [P, DEPTH1, GH])

        s_ident0, s_ident = sem("ident_zeroed"), sem("ident_ready")
        s_x_in = [sem(f"x_in{b}") for b in range(NT)]
        s_ctx_in = [sem(f"ctx_in{b}") for b in range(NT)]
        s_small_in = sem("small_in")
        s_gate = sem("gate_ready")
        s_stats, s_moments, s_rstd = sem("stats"), sem("moments"), sem("rstd")
        s_pow = sem("rstd_ready")
        s_xn = sem("x_normalised")
        s_bo = sem("bo_gated")
        s_xres = sem("xres_ready")
        s_tr, s_tr_hi, s_tr_lo = sem("transposed"), sem("transposed_hi"), sem("transposed_lo")
        s_bias_tr, s_bias_all, s_bias = sem("bias_transposed"), sem("bias_all"), sem("bias_now")
        s_w0_in = [sem(f"first_weight_in{i}") for i in range(NS)]
        s_w_in = [sem(f"weight_in{i}") for i in range(SLOTS)]
        s_w_hi, s_w_lo = sem("weight_hi"), sem("weight_lo")
        s_qproj, s_q_hi, s_q_lo = sem("q_projected"), sem("q_hi"), sem("q_lo")
        s_kproj, s_k_hi, s_k_lo = sem("k_projected"), sem("k_hi"), sem("k_lo")
        s_vproj, s_vt, s_vtr, s_v_hi, s_v_lo = sem("v_projected"), sem("vT_ready"), sem("v_transposed"), sem("v_hi"), sem("v_lo")
        s_s_lo, s_sum = sem("scores_lo_copied"), sem("scores_summed")
        s_scores, s_max, s_nmax, s_exp = sem("scores"), sem("row_max"), sem("neg_max"), sem("exped")
        s_rinv, s_norm, s_ptr = sem("rsum_inverted"), sem("prob_normalised"), sem("prob_transposed")
        s_pt_hi, s_pt_lo, s_pv, s_o_hi, s_o_lo = sem("pT_hi"), sem("pT_lo"), sem("pv"), sem("oT_hi"), sem("oT_lo")
        s_out, s_acc = sem("out_projected"), sem("out_added")
        s_store = sem("stored")
        s_nat = [sem(f"natural_in{i}") for i in range(6)]
        s_thr_in, s_wscale, s_sign, s_clip, s_unclipped = (sem("b_thr_in"), sem("w_bin_scale"), sem("w_bin_sign"),
                                                           sem("w_bin_clipped"), sem("w_bin_less_clip"))
        s_perm, s_gtmade, s_gt, s_gturned = sem("w_out_permuted"), sem("gatesT_made"), sem("gatesT_copied"), sem("gates_turned")
        s_small2 = sem("small2_in")
        s_gzero = sem("gate_rows_zeroed")
        s_made, s_hi, s_lo = sem("split_made"), sem("split_hi"), sem("split_lo")
        s_eps, s_pow2, s_xn2 = sem("variance_eps"), sem("rstd2_ready"), sem("xn_ready")
        s_bb, s_bbg, s_xb = sem("b_base_in"), sem("b_base_gated"), sem("b_base_added")
        s_el, s_ee, s_hw = sem("gate_logits"), sem("gate_exps"), sem("adapters_weighted")
        s_wide, s_wideT = sem("weights_wide"), sem("weights_wide_transposed")
        s_f0, s_x2 = sem("ffn0_done"), sem("x2_ready")
        s_bin = sem("w_bin_ready")
        s_idr, s_mask, s_grp0, s_grp1, s_grp = sem("ident_r"), sem("negmask"), sem("group0"), sem("group1"), sem("group_of")
        s_vz, s_kd, s_vd = sem("v_zeroed"), sem("k_by_group"), sem("v_by_group")
        s_s1, s_m1, s_e1, s_r1, s_n1 = sem("scores1"), sem("max1"), sem("exp1"), sem("rinv1"), sem("norm1")
        s_t1, s_t1h, s_t1l, s_pv1 = sem("p1_transposed"), sem("p1T_hi"), sem("p1T_lo"), sem("pv1")
        s_o1h, s_o1l, s_out1, s_x3 = sem("o1T_hi"), sem("o1T_lo"), sem("out1"), sem("x3_ready")
        s_f1, s_x4 = sem("ffn1_done"), sem("x4_ready")
        s_chain = sem("vector_chain")

        NTR = 2 * NT

        def q_head_half(t):
            return (t - 3) % 8 % 4, 0 if 3 <= t <= 6 else 1

        def split_dst(kvh, i):
            kind, h = SLICES[i]
            if kind == "q":
                return tuple(w[:, h, :, :].rearrange("p c n -> p (c n)") for w in wq)
            if kind == "o":
                return tuple(w[:, bass.ds((kvh % 2) * (G * D) + h * D, D)] for w in wo)
            return tuple(w[:, :, :].rearrange("p c n -> p (c n)") for w in (wk if kind == "k" else wv))

        TURNED = [("ctx", b) for b in range(HT)] + [("x", b) for b in range(HT)] \
            + [(what, b) for b in range(HT, NT) for what in ("ctx", "x")]
        turn_banks = [bank[i] for i in (0, 1, 2, 4)]
        BO_AT = {3: [0], 4: [1, 2], 5: [3, 4], 6: [5, 6], 7: [7]}
        TURN_AT = {3: [8, 9], 4: [10, 11], 5: [12, 13], 6: [14, 15]}

        def turned(i):
            what, b = TURNED[i]
            return [part[:, :, b * TOK:(b + 1) * TOK] for part in (cT if what == "ctx" else xT)]

        AHEAD = {3: [("wk", 0)], 4: [("x0", 0)], 5: [("x0", 2)], 6: [("x0", 3)], 7: [("v", 1)]}
        BEHIND = {3: [("wv", 0)], 4: [("k", 0), ("x0", 1)], 5: [("k", 1)], 6: [("v", 0), ("x0", 4)],
                  7: [("base", c) for c in range(C)] + [("adapt", 0), ("gates", 0), ("up", 0), ("x0", 5)]}
        NORMALISED = {2: [0], 3: [1], 4: [2, 3], 5: [4], 6: [5], 7: [6]}
        ORDER = ([name for t in range(3, STEPS) for name in AHEAD[t] + BEHIND[t]]
                 + [("x0", 6), ("wq", 0), ("wq", 1), ("x0", 7), ("wq", 2), ("wq", 3), ("hw", 0)] + [("wo", j) for j in range(J1)]
                 + [("hw", 1)] + [("x1", b) for b in range(HT)] + [("bin", c) for c in range(C)] + [("x1", HT)]
                 + [name for i in range(J1) for name in [("q", i)] + ([("x1", HT + 1 + i)] if HT + 1 + i < NT else [])]
                 + [("q", J1 + j) for j in range(J1)]
                 + [("x2", b) for b in range(NT)])
        NTH = {name: i for i, name in enumerate(ORDER)}
        RING = (3, 7, 5, 6)
        EARLY = NTH[AHEAD[STEPS - 1][0]]

        def bank_of(i):
            return 7 if ORDER[i][0] == "x2" else (3, 5, 6)[i % 3] if i < EARLY else RING[i % 4]

        def split_bank(i):
            return bank[bank_of(i)]

        def scores_of(part):
            return [b[:, :].rearrange("p (g a m) -> p g a m", g=2, a=2)[:, :, part, :] for b in ps_s]

        def split_views(i):
            kind, n = ORDER[i]
            acc = split_bank(i)
            four = acc[:, :].rearrange("p (c n) -> p c n", c=4)
            tok = slice(n * TOK, (n + 1) * TOK)
            half = slice(n * HALF, (n + 1) * HALF)
            if kind == "base":
                return acc[:, :], wb[0][:, n, :], wb[1][:, n, :]
            if kind == "adapt":
                return four, wa[0][:, :, :], wa[1][:, :, :]
            if kind == "gates":
                return acc[:, 0:C * NGT].rearrange("p (c n) -> p c n", c=C), wg[0][:, :, :], wg[1][:, :, :]
            if kind == "up":
                return acc[:, :], wB[0][:, :], wB[1][:, :]
            if kind == "wk":
                return four, wk1[0][:, :, :], wk1[1][:, :, :]
            if kind == "wv":
                return four, wv1[0][:, :, :], wv1[1][:, :, :]
            if kind == "k":
                return acc[:, :], k1T[0][:, half], k1T[1][:, half]
            if kind == "v":
                return four, v1[0][:, n * HT:(n + 1) * HT, :], v1[1][:, n * HT:(n + 1) * HT, :]
            if kind in ("x0", "x1", "x2"):
                return four, xT[0][:, :, tok], xT[1][:, :, tok]
            if kind == "wq":
                return acc[:, :], wq1[0][:, n, :], wq1[1][:, n, :]
            if kind == "hw":
                return hw[:, :], hwT[n][0][:, :], hwT[n][1][:, :]
            if kind == "wo":
                return acc[:, :], wo1[0][:, n, :], wo1[1][:, n, :]
            if kind == "bin":
                return acc[:, :], wf1[0][:, n, :], wf1[1][:, n, :]
            half = slice(n // J1 * HALF, (n // J1 + 1) * HALF)
            return acc[:, :], q1T[0][:, n % J1, half], q1T[1][:, n % J1, half]

        def adaptersT(hf):
            return bank[(2, 4)[hf]]

        def gates_of(hf):
            return bank[hf][:, 0:HT * NGT].rearrange("p (t n) -> p t n", n=NGT)

        scored1 = bank[0:DEPTH1]
        ps_pv1 = bank[3]

        def turned1(u):
            return bank[4 if u < J1 or u % 2 == 0 else 5]

        def ps_out1(b):
            return bank[6] if b < NT - 1 else bank[0]

        block = es.enter_context(nc.Block())

        @block.sync
        def _(sp):
            def load(kvh, i, slot, arrived):
                kind, h = SLICES[i]
                if kind == "o":
                    dst, src = slot, wo_rows[bass.ds(kvh * G + h, 1), :, :].rearrange("a p n -> p (a n)")
                else:
                    dst = slot.rearrange("p (c n) -> p c n", c=C)
                    if kind == "q":
                        src = wq_rows[:, :, bass.ds(kvh * (G * DH) + h * DH, DH)]
                    elif kind == "k":
                        src = wkv_rows[:, :, bass.ds(kvh * DH, DH)]
                    else:
                        src = wkv_rows[:, :, bass.ds(kvh * DH + KVH * DH, DH)]
                sp.dma_start(dst, src).then_inc(arrived, 16)

            def load_x(b):
                sp.dma_start(xres[:, b, :], x_rows[:, b, :]).then_inc(s_x_in[b], 16)

            def load_ctx(b):
                sp.dma_start(ctx_nat[:, b, :], ctx_rows[:, b, :]).then_inc(s_ctx_in[b], 16)

            for b in range(2, HT):
                load_x(b)
            for b in range(HT):
                load_ctx(b)
            for i in range(2):
                load(0, i, first_stage[i], s_w0_in[i])
            for b in range(HT, NT):
                load_ctx(b)
                load_x(b)
            for i in range(2, NS):
                load(0, i, first_stage[i], s_w0_in[i])
            with sp.Fori(1, KVH) as kvh:
                for i in range(NS):
                    sp.wait_ge(s_w_lo, kvh * NS + (i - SLOTS + 1))
                    load(kvh, i, stage[:, i % SLOTS, :], s_w_in[i % SLOTS])
            sp.wait_ge(s_qproj, KVH * STEPS)

            def rows(lo):
                return nat[:, :, :].rearrange("p a n -> p (a n)")[:, lo * D:(lo + 1) * D]

            def tiled(lo, w):
                dst = nat[:, :, :].rearrange("p a n -> p (a n)")[:, lo * D:(lo + 4) * D]
                return dst.rearrange("p (i n) -> p i n", i=4), w.rearrange("(i p) n -> p i n", p=P)

            sp.dma_start(rows(4), w_k).then_inc(s_nat[0], 16)
            sp.dma_start(rows(5), w_v).then_inc(s_nat[0], 16)
            sp.dma_start(*tiled(0, W_base)).then_inc(s_nat[1], 16)
            sp.dma_start(rows(6), A_w.rearrange("e r d -> (e r) d")).then_inc(s_nat[2], 16)
            for i in range(4):
                sp.dma_start(rows(7)[:, i * P:(i + 1) * P].rearrange("p (e r) -> p e r", e=E),
                             B_w[:, i * P:(i + 1) * P, :].rearrange("e p r -> p e r")).then_inc(s_nat[2], 16)
            sp.wait_ge(s_gzero, 1)
            sp.dma_start(gates_nat[0:E, :], W_gate).then_inc(s_nat[2], 16)
            sp.dma_start(gates_nat[E:E + 1, :], W_thr.rearrange("(a d) -> a d", a=1)).then_inc(s_nat[2], 16)
            sp.wait_ge(s_vtr, 2 * KVH)
            sp.dma_start(b_base_bc[:, :], b_base.partition_broadcast(P)).then_inc(s_bb, 16)
            sp.dma_start(mask_in[:, :], mask).then_inc(s_small2, 16)
            sp.wait_ge(s_made, NTH[("v", 1)] + 1)
            for j in range(J1):
                sp.dma_start(q1_nat[:, j, :], w_q.rearrange("(g j d) n -> j g d n", j=J1, d=DH1)[j]).then_inc(s_nat[3], 16)
            sp.dma_start(o1_nat[:, :, :], w_out.rearrange("(i p) n -> p i n", p=P)).then_inc(s_nat[4], 16)
            sp.dma_start(bin_nat[:, :, :], w_bin.rearrange("(i p) n -> p i n", p=P)).then_inc(s_nat[5], 16)
            for b in range(NT):
                sp.wait_ge(s_x4, b + 1)
                sp.dma_start(out.rearrange("b t d -> t b d")[:, b, :], xres[:, b, :]).then_inc(s_store, 16)
            sp.wait_ge(s_store, 16 * NT)

        @block.gpsimd
        def _(pool):
            nc.gpsimd.memset(ident[:, :], 0.0).then_inc(s_ident0, 1)
            pool.wait_ge(s_ident0, 1)
            nc.gpsimd.affine_select(out=ident[:, :], in_=ident[:, :], compare_op=ALU.not_equal, fill=1.0, base=0,
                                    pattern=[[-1, P]], channel_multiplier=1).then_inc(s_ident, 1)
            nc.gpsimd.memset(gates_nat[:, :], 0.0).then_inc(s_gzero, 1)
            pool.dma_start(gate_raw[:, 0:2], g_xattn.partition_broadcast(P)).then_inc(s_small_in, 16)
            pool.dma_start(gate_raw[:, 2:4], g_ffn.partition_broadcast(P)).then_inc(s_small_in, 16)
            pool.dma_start(bo_bc[:, :], bo.partition_broadcast(P)).then_inc(s_small_in, 16)
            pool.dma_start(bias_nat[0:HEADS, :], bq.rearrange("(h d) -> h d", d=DH)).then_inc(s_small_in, 16)
            pool.dma_start(bias_nat[HEADS:, :], bkv.rearrange("(h d) -> h d", d=DH)).then_inc(s_small_in, 16)
            pool.dma_start(nb_thr[:, :], b_thr.partition_broadcast(P)).then_inc(s_thr_in, 16)

            def half_root(half):
                pool.wait_ge(s_rstd, 2 + half)
                cols = slice(half * HT, (half + 1) * HT)
                nc.gpsimd.tensor_tensor(rstd[:, cols], rstd[:, cols], power[:, cols], ALU.pow).then_inc(s_pow, 1)

            def add_bo(b):
                pool.wait_ge(s_bo, 1)
                pool.wait_ge(s_xn, b + 1)
                nc.gpsimd.tensor_tensor(xres[:, b, :], xres[:, b, :], bo_bc[:, :], ALU.add).then_inc(s_xres, 1)

            def step(k, t, attend_next, split):
                if split:
                    for i in SPLIT_AT[t]:
                        hi, lo = split_dst(k + 1, i)
                        pool.wait_ge(s_w_hi, (k + 1) * NS + i + 1)
                        src = first_stage[i] if isinstance(k, int) else stage[:, i % SLOTS, :]
                        nc.gpsimd.tensor_tensor(lo, src, hi.bitcast(F32), ALU.subtract).then_inc(s_w_lo, 1)
                if attend_next:
                    n = k * STEPS + t + 1
                    pool.wait_ge(s_rinv, n + 1)
                    nc.gpsimd.tensor_tensor(prob[:, :, :], prob[:, :, :], rinv[:, :].unsqueeze(2).broadcast_to([P, G, TOK]),
                                            ALU.mult).then_inc(s_norm, 1)

            def inverse_root(n):
                pool.wait_ge(s_eps, n + 1)
                col = slice(n % NT, n % NT + 1)
                nc.gpsimd.tensor_tensor(rstd[:, col], rstd[:, col], power[:, 0:1], ALU.pow).then_inc(s_pow2, 1)

            half_root(0)
            for t in range(STEPS):
                step(-1, t, False, True)
                if t == 1:
                    half_root(1)
                for b in BO_AT.get(t, ()):
                    add_bo(b)
            step(-1, STEPS - 1, True, False)
            with pool.Fori(0, KVH - 1) as k:
                for t in range(STEPS):
                    step(k, t, True, True)
            for t in range(STEPS):
                step(KVH - 1, t, t < STEPS - 1, False)
                if t > 0:
                    inverse_root(t - 1)
            inverse_root(NT - 1)

            pool.wait_ge(s_bbg, 1)
            def add_b_base(b):
                pool.wait_ge(s_xn2, b + 1)
                nc.gpsimd.tensor_tensor(xres[:, b, :], xres[:, b, :], b_base_bc[:, :], ALU.add).then_inc(s_xb, 1)

            for b in range(NT - 2):
                add_b_base(b)

            pool.wait_ge(s_nat[4], 16)
            pool.wait_ge(s_made, NTH[("up", 0)] + 1)
            for i in range(4):
                ins = nc.gpsimd.tensor_copy(nat[:, 1, i * D:(i + 1) * D].rearrange("p (j g d) -> p j g d", j=J1, d=DH1),
                                            o1_nat[:, i, :].rearrange("p (g j d) -> p j g d", j=J1, d=DH1))
            ins.then_inc(s_perm, 1)
            for b in range(NT - 2, NT):
                add_b_base(b)

            pool.wait_ge(s_sign, 1)
            pool.wait_ge(s_wscale, 1)
            for i in range(4):
                ins = nc.gpsimd.tensor_scalar(bin_nat[:, i, :], bin_nat[:, i, :], -1.0, 1.0, ALU.max, ALU.min)
            ins.then_inc(s_clip, 1)
            for n in range(NT, NT + HT):
                inverse_root(n)
            pool.wait_ge(s_unclipped, 1)
            for i in range(4):
                ins = nc.gpsimd.tensor_tensor(bin_nat[:, i, :], sign[:, i, :], bin_nat[:, i, :], ALU.add)
            ins.then_inc(s_bin, 1)
            for n in range(NT + HT, 2 * NT):
                inverse_root(n)

            nc.gpsimd.memset(group_of[:, :], 1.0).then_inc(s_grp0, 1)
            pool.wait_ge(s_grp0, 1)
            nc.gpsimd.affine_select(out=group_of[:, :], in_=group_of[:, :], compare_op=ALU.is_ge, fill=0.0, base=0,
                                    pattern=[[-DH1, G1]], channel_multiplier=1).then_inc(s_grp1, 1)
            pool.wait_ge(s_grp1, 1)
            nc.gpsimd.affine_select(out=group_of[:, :], in_=group_of[:, :], compare_op=ALU.is_ge, fill=0.0, base=DH1 - 1,
                                    pattern=[[DH1, G1]], channel_multiplier=-1).then_inc(s_grp, 1)
            pool.wait_ge(s_made, NTH[("wo", J1 - 1)] + 1)
            for part in vd:
                nc.gpsimd.memset(part[:, :, :, :].bitcast(F32), 0.0).then_inc(s_vz, 1)

            def k_by_group(B, part):
                b, gh = B // 2, B % 2
                if B >= 2:
                    pool.wait_ge(s_s1, J1 * (B - 1))
                nc.gpsimd.tensor_tensor(kd[part][:, gh, :, :],
                                        k1T[part][:, b * TOK:(b + 1) * TOK].bitcast(F32).unsqueeze(1).broadcast_to([KV1, GH, TOK]),
                                        group_of[:, gh * GH:(gh + 1) * GH].unsqueeze(2).broadcast_to([KV1, GH, TOK]),
                                        ALU.mult).then_inc(s_kd, 1)

            def v_by_group(B, part):
                b, gh = B // 2, B % 2
                if B >= 2:
                    pool.wait_ge(s_pv1, GH * (B - 1))
                step_ = KV1 + DH1
                flat = vd[part][:, gh, :, :].rearrange("p g n -> p (g n)")
                for i in range(GH):
                    at = i * step_ + gh * GH * DH1
                    ins = nc.gpsimd.tensor_copy(flat[:, at:at + DH1],
                                                v1[part][:, b, (gh * GH + i) * DH1:(gh * GH + i + 1) * DH1].bitcast(F32))
                ins.then_inc(s_vd, 1)

            def norm1(u):
                pool.wait_ge(s_r1, u + 1)
                nc.gpsimd.tensor_tensor(prob1[u % DEPTH1][:, :, :], prob1[u % DEPTH1][:, :, :],
                                        rinv1[:, u % DEPTH1, :].unsqueeze(2).broadcast_to([P, GH, TOK]), ALU.mult).then_inc(s_n1, 1)

            pool.wait_ge(s_grp, 1)
            for B in (0, 1):
                for part in (0, 1):
                    k_by_group(B, part)
            pool.wait_ge(s_vz, 2)
            for B in (0, 1):
                for part in (0, 1):
                    v_by_group(B, part)
            for u in (0, 1):
                norm1(u)
            for u in range(UNITS):
                if u % UB == 6 and u >= UB:
                    inverse_root(2 * NT + u // UB - 1)
                if u + 2 < UNITS:
                    norm1(u + 2)
                B = u // J1
                if u % J1 in (0, 1) and B + 2 < 2 * NT:
                    k_by_group(B + 2, u % J1)
                if u % J1 in (2, 3) and B >= 2:
                    v_by_group(B, u % J1 - 2)
            inverse_root(3 * NT - 1)

        @block.scalar
        def _(act):
            for b in (0, 1):
                act.dma_start(xres[:, b, :], x_rows[:, b, :]).then_inc(s_x_in[b], 16)

            def turned_hi(i):
                act.wait_ge(s_tr, i + 1)
                nc.scalar.activation(turned(i)[0], turn_banks[i % 4][:, :].rearrange("p (c n) -> p c n", c=C), ACT.Copy
                                     ).then_inc(s_tr_hi, 1)

            for i in range(HT):
                turned_hi(i)

            def hi(i):
                act.wait_ge(s_made, i + 1)
                if ORDER[i][0] == "hw":
                    nc.scalar.activation(hw[:, :], split_bank(i)[:, :], ACT.Copy, scale=ADAPT).then_inc(s_wideT, 1)
                    act.wait_ge(s_hw, ORDER[i][1] + 1)
                acc, dst, _ = split_views(i)
                if ORDER[i][0] == "q":
                    nc.scalar.activation(dst, acc, ACT.Copy, scale=SCALE1).then_inc(s_hi, 1)
                else:
                    nc.scalar.activation(dst, acc, ACT.Copy).then_inc(s_hi, 1)

            def step(k, t, attend_next, project, split, started=True, ending=False):
                g = k * STEPS + t
                if started:
                    act.wait_ge(s_ptr, g + 1)
                    nc.scalar.activation(pT[0][:, :], ps_pt[:, :], ACT.Copy).then_inc(s_pt_hi, 1)
                if attend_next:
                    act.wait_ge(s_scores, g + 2)
                    for i, third in enumerate(scores_of(1)):
                        ins = nc.scalar.activation(score[:, 2 * i:2 * i + 2, :], third, ACT.Copy)
                    ins.then_inc(s_s_lo, 1)
                if split:
                    for i in SPLIT_AT[t]:
                        kind, h = SLICES[i]
                        if isinstance(k, int):
                            src = first_stage[i]
                            act.wait_ge(s_w0_in[i], 16)
                        else:
                            src = stage[:, i % SLOTS, :]
                            act.wait_ge(s_w_in[i % SLOTS], k * (16 * NS // SLOTS) + 16 * (i // SLOTS + 1))
                        if started:
                            if kind == "q":
                                act.wait_ge(s_qproj, g + 5)
                            elif kind == "k":
                                act.wait_ge(s_kproj, 2 * k + 2)
                            elif kind == "v":
                                act.wait_ge(s_vproj, 2 * k + 2)
                            else:
                                act.wait_ge(s_out, k * STEPS + 1)
                        nc.scalar.activation(split_dst(k + 1, i)[0], src, ACT.Copy).then_inc(s_w_hi, 1)
                if ending:
                    for name in AHEAD.get(t, ()):
                        hi(NTH[name])
                if started:
                    act.wait_ge(s_pv, g + 1)
                    nc.scalar.activation(oT[0][:, :, :].rearrange("p g t -> p (g t)"), ps_o[:, :], ACT.Copy).then_inc(s_o_hi, 1)
                if attend_next:
                    act.wait_ge(s_nmax, g + 2)
                    if not started:
                        act.wait_ge(s_w_lo, NS)
                    for j in range(G):
                        e = nc.scalar.activation(prob[:, j, :], score[:, j, :], ACT.Exp, bias=nmax[:, 1, j:j + 1],
                                                 scale=SCALE0, accum_out=rsum[:, j:j + 1])
                    e.then_inc(s_exp, 1)
                if project:
                    h, half = q_head_half(t)
                    act.wait_ge(s_qproj, g + 6)
                    if t == 3:
                        act.wait_ge(s_bias, k + 2)
                    nc.scalar.activation(qT[0][:, h, half * HALF:(half + 1) * HALF], ps_q[:, :], ACT.Identity,
                                         bias=bias[:, h:h + 1]).then_inc(s_q_hi, 1)
                if not started and t in TURN_AT:
                    for i in TURN_AT[t]:
                        turned_hi(i)
                if t == 3 and started:
                    act.wait_ge(s_vtr, 2 * k + 2)
                    nc.scalar.activation(v[0][:, 4:8, :].rearrange("p b d -> p (b d)"), ps_vt[:, :], ACT.Copy).then_inc(s_v_hi, 1)
                if t == 7 and attend_next:
                    act.wait_ge(s_vtr, 2 * k + 3)
                    nc.scalar.activation(v[0][:, 0:4, :].rearrange("p b d -> p (b d)"), ps_vt[:, :], ACT.Copy).then_inc(s_v_hi, 1)
                if ending:
                    for name in BEHIND.get(t, ()):
                        hi(NTH[name])
                if project and t in (0, 4):
                    c, half = (2, 1) if t == 0 else (3, 0)
                    act.wait_ge(s_kproj, 2 * k + c)
                    nc.scalar.activation(kT[:, half * HT:(half + 1) * HT, 0, :],
                                         ps_kv[:, :].rearrange("p (b m) -> p b m", b=HT), ACT.Identity,
                                         bias=bias[:, G:G + 1]).then_inc(s_k_hi, 1)
                if project and t in (2, 6):
                    c = 2 if t == 2 else 3
                    act.wait_ge(s_vproj, 2 * k + c)
                    nc.scalar.activation(vT[:, :, :].rearrange("p b t -> p (b t)"), ps_kv[:, :], ACT.Identity,
                                         bias=bias[:, G + 1:G + 2]).then_inc(s_vt, 1)

            for t in range(STEPS):
                step(-1, t, t == STEPS - 1, t >= 3, True, started=False)
                if t == 0:
                    for i in range(HT, NT):
                        turned_hi(i)
                    act.wait_ge(s_small_in, 80)
                    nc.scalar.activation(gate[:, :], gate_raw[:, :], ACT.Tanh).then_inc(s_gate, 1)
                    act.wait_ge(s_ident, 1)
                    nc.scalar.activation(ident_r[:, :], ident[:, :], ACT.Copy).then_inc(s_idr, 1)
            with act.Fori(0, KVH - 1) as k:
                for t in range(STEPS):
                    step(k, t, True, True, True)
            for t in range(STEPS):
                step(KVH - 1, t, t < STEPS - 1, t < 3, False, ending=True)


            def gates_copied(hf):
                act.wait_ge(s_gtmade, hf + 1)
                nc.scalar.activation(gatesT[:, hf, :], bank[hf][0:NGT, :], ACT.Copy).then_inc(s_gt, 1)

            def gate_exps(hf):
                act.wait_ge(s_el, hf + 1)
                if hf == 0:
                    act.wait_ge(s_bbg, 2)
                nc.scalar.activation(gl[:, 1, :], gl[:, 0, :], ACT.Exp)
                nc.scalar.activation(gl[:, 2, 0:HT], gates_of(hf)[:, :, E], ACT.Exp, scale=-1.0, bias=nb_thr[:, :]
                                     ).then_inc(s_ee, 1)

            gates_copied(0)
            hi(NTH[("x0", 6)])
            hi(NTH[("wq", 0)])
            hi(NTH[("wq", 1)])
            gate_exps(0)
            for i in range(NTH[("x0", 7)], NTH[("wq", C - 1)] + 1):
                hi(i)
            act.wait_ge(s_nat[5], 16)
            for i in range(4):
                ins = nc.scalar.activation(sign[:, i, :], bin_nat[:, i, :], ACT.Sign)
            ins.then_inc(s_sign, 1)
            gates_copied(1)
            hi(NTH[("hw", 0)])
            for j in range(J1):
                hi(NTH[("wo", j)])
            gate_exps(1)
            hi(NTH[("hw", 1)])
            for i in range(NTH[("x1", 0)], NTH[("q", J1)] + 1):
                hi(i)

            def exp1(u):
                act.wait_ge(s_m1, u + 1)
                if u >= DEPTH1:
                    act.wait_ge(s_t1, u - DEPTH1 + 1)
                for i in range(GH):
                    e = nc.scalar.activation(prob1[u % DEPTH1][:, i, :], scored1[u % DEPTH1][:, i * TOK:(i + 1) * TOK], ACT.Exp,
                                             bias=nmax1[:, u % DEPTH1, i:i + 1], accum_out=rsum1[:, u % DEPTH1, i:i + 1])
                e.then_inc(s_e1, 1)

            def o1_hi(b):
                act.wait_ge(s_pv1, 2 * GH * (b + 1))
                nc.scalar.activation(o1T[0][:, :, :].rearrange("p j t -> p (j t)"), ps_pv1[:, :], ACT.Copy).then_inc(s_o1h, 1)

            for u in (0, 1):
                exp1(u)
            for u in range(UNITS):
                if u + 1 < J1:
                    hi(NTH[("q", J1 + 1 + u)])
                act.wait_ge(s_t1, u + 1)
                B = u // J1
                nc.scalar.activation(p1T[0][:, B % 2, :, (u % J1) * TOK:(u % J1 + 1) * TOK],
                                     turned1(u)[:, :].rearrange("p (g n) -> p g n", g=GH), ACT.Copy).then_inc(s_t1h, 1)
                if u % UB == 4 and u >= UB:
                    o1_hi(u // UB - 1)
                if u + 2 < UNITS:
                    exp1(u + 2)
                if u % UB == 0 and u >= 2 * UB:
                    hi(NTH[("x2", u // UB - 2)])
            hi(NTH[("x2", NT - 2)])
            o1_hi(NT - 1)
            hi(NTH[("x2", NT - 1)])

        @block.vector
        def _(dve):
            def half_stats(half):
                tiles = range(half * HT, (half + 1) * HT)
                for b in tiles:
                    dve.wait_ge(s_x_in[b], 16)
                    nc.vector.bn_stats(stats[:, b, :], xres[:, b, :]).then_inc(s_stats, 1)
                for b in tiles:
                    dve.wait_ge(s_stats, b + 1)
                    nc.vector.bn_aggr(moments[:, b, :], stats[:, b, :]).then_inc(s_moments, 1)
                dve.wait_ge(s_moments, (half + 1) * HT)
                cols = slice(half * HT, (half + 1) * HT)
                nc.vector.tensor_scalar(rstd[:, cols], moments[:, cols, 1], EPS, None, ALU.add).then_inc(s_rstd, 1)

            def normalised(b):
                dve.wait_ge(s_pow, b // HT + 1)
                nc.vector.tensor_scalar(xn_nat[:, b, :], xres[:, b, :], moments[:, b, 0:1], rstd[:, b:b + 1],
                                        ALU.subtract, ALU.mult).then_inc(s_xn, 1)

            def turned_lo(i):
                dve.wait_ge(s_tr_hi, i + 1)
                hi, lo = turned(i)
                nc.vector.tensor_tensor(lo, turn_banks[i % 4][:, :].rearrange("p (c n) -> p c n", c=C), hi.bitcast(F32),
                                        ALU.subtract).then_inc(s_tr_lo, 1)

            nc.vector.memset(power[:, :], -0.5).then_inc(s_rstd, 1)
            half_stats(0)
            turned_lo(0)
            normalised(0)
            for b in range(1, HT):
                normalised(b)
                turned_lo(b)
            for i in range(HT, NT):
                turned_lo(i)
            dve.wait_ge(s_bias_tr, 1)
            cols = bias_all[:, :].rearrange("p (k j) -> p k j", j=G + 2)
            nc.vector.tensor_copy(cols[:, :, 0:G], bank[6][:, 0:HEADS].rearrange("p (k j) -> p k j", j=G))
            nc.vector.tensor_copy(cols[:, :, G], bank[6][:, HEADS:HEADS + KVH])
            nc.vector.tensor_copy(cols[:, :, G + 1], bank[6][:, HEADS + KVH:HEADS + 2 * KVH]).then_inc(s_bias_all, 1)
            dve.wait_ge(s_bias_all, 1)
            nc.vector.tensor_copy(bias[:, :], bias_all[:, 0:G + 2]).then_inc(s_bias, 1)
            half_stats(1)
            normalised(HT)
            dve.wait_ge(s_gate, 1)
            nc.vector.tensor_scalar(bo_bc[:, :], bo_bc[:, :], gate[:, 0:1], None, ALU.mult).then_inc(s_bo, 1)
            def minus_hi(lo, acc, hi, bias_col=None):
                if bias_col is None:
                    return nc.vector.tensor_tensor(lo, acc, hi.bitcast(F32), ALU.subtract)
                return nc.vector.scalar_tensor_tensor(lo, acc, bias_col, hi.bitcast(F32), ALU.add, ALU.subtract)

            links = [0]

            def link(ins):
                links[0] += 1
                ins.then_inc(s_chain, 1)
                dve.wait_ge(s_chain, links[0])

            def lo(i):
                dve.wait_ge(s_hi, i + 1)
                acc, hi, dst = split_views(i)
                if ORDER[i][0] == "q":
                    nc.vector.scalar_tensor_tensor(dst, acc, SCALE1, hi.bitcast(F32), ALU.mult, ALU.subtract).then_inc(s_lo, 1)
                else:
                    nc.vector.tensor_tensor(dst, acc, hi.bitcast(F32), ALU.subtract).then_inc(s_lo, 1)

            def normalise(n, made_before):
                b = n % NT
                dve.wait_ge(s_pow2, n + 1)
                if made_before:
                    dve.wait_ge(s_made, made_before)
                nc.vector.tensor_scalar(xn[:, n % 2, :], xres[:, b, :], moments[:, b, 0:1], rstd[:, b:b + 1],
                                        ALU.subtract, ALU.mult).then_inc(s_xn2, 1)

            def tile_stats(b):
                link(nc.vector.bn_stats(stats[:, b, :], xres[:, b, :]))
                link(nc.vector.bn_aggr(moments[:, b, :], stats[:, b, :]))
                nc.vector.tensor_scalar(rstd[:, b:b + 1], moments[:, b, 1:2], EPS, None, ALU.add).then_inc(s_eps, 1)

            def step(k, t, attend_next, project, started=True, ending=False):
                g = k * STEPS + t
                if t == 3 and project and started:
                    dve.wait_ge(s_vt, 2 * k + 2)
                    dve.wait_ge(s_q_lo, g + 5)
                    nc.vector.tensor_copy(bias[:, :], bias_all[:, bass.ds((k + 1) * (G + 2), G + 2)]).then_inc(s_bias, 1)
                    dve.wait_ge(s_bias, k + 2)
                if started:
                    dve.wait_ge(s_pt_hi, g + 1)
                    minus_hi(pT[1][:, :], ps_pt[:, :], pT[0][:, :]).then_inc(s_pt_lo, 1)
                if attend_next:
                    dve.wait_ge(s_s_lo, g + 2)
                    for i, first in enumerate(scores_of(0)):
                        ins = nc.vector.tensor_tensor(score[:, 2 * i:2 * i + 2, :], first, score[:, 2 * i:2 * i + 2, :], ALU.add)
                    ins.then_inc(s_sum, 1)
                    dve.wait_ge(s_sum, g + 2)
                    nc.vector.tensor_reduce(nmax[:, 0, :], score[:, :, :], AX.X, ALU.max,
                                            negate=True).then_inc(s_max, 1)
                    dve.wait_ge(s_max, g + 2)
                    nc.vector.tensor_scalar(nmax[:, 1, :], nmax[:, 0, :], SCALE0, None, ALU.mult).then_inc(s_nmax, 1)
                if ending:
                    for name in AHEAD.get(t, ()):
                        lo(NTH[name])
                if started:
                    dve.wait_ge(s_o_hi, g + 1)
                    minus_hi(oT[1][:, :, :].rearrange("p g t -> p (g t)"), ps_o[:, :],
                             oT[0][:, :, :].rearrange("p g t -> p (g t)")).then_inc(s_o_lo, 1)
                if attend_next:
                    dve.wait_ge(s_exp, g + 2)
                    nc.vector.reciprocal(rinv[:, :], rsum[:, :]).then_inc(s_rinv, 1)
                if project:
                    h, half = q_head_half(t)
                    cols = slice(half * HALF, (half + 1) * HALF)
                    dve.wait_ge(s_q_hi, g + 6)
                    minus_hi(qT[1][:, h, cols], ps_q[:, :], qT[0][:, h, cols], bias[:, h:h + 1]).then_inc(s_q_lo, 1)
                if not started and t in TURN_AT:
                    if t < STEPS - 2:
                        normalised(HT + t - 2)
                    for i in TURN_AT[t]:
                        turned_lo(i)
                if (t == 3 and started) or (t == 7 and attend_next):
                    c, bs = (2, slice(4, 8)) if t == 3 else (3, slice(0, 4))
                    dve.wait_ge(s_v_hi, 2 * k + c)
                    minus_hi(v[1][:, bs, :].rearrange("p b d -> p (b d)"), ps_vt[:, :],
                             v[0][:, bs, :].rearrange("p b d -> p (b d)")).then_inc(s_v_lo, 1)
                if project and t in (0, 4):
                    c, half = (2, 1) if t == 0 else (3, 0)
                    bs = slice(half * HT, (half + 1) * HT)
                    dve.wait_ge(s_k_hi, 2 * k + c)
                    minus_hi(kT[:, bs, 1, :], ps_kv[:, :].rearrange("p (b m) -> p b m", b=HT), kT[:, bs, 0, :],
                             bias[:, G:G + 1]).then_inc(s_k_lo, 1)
                if ending:
                    if t > 0:
                        dve.wait_ge(s_acc, g)
                        tile_stats(t - 1)
                    for name in BEHIND.get(t, ()):
                        lo(NTH[name])
                    for b in NORMALISED.get(t, ()):
                        normalise(b, NTH[("x0", b - 2)] + 1 if b >= 2 else 0)
                if started:
                    dve.wait_ge(s_out, g + 1)
                    nc.vector.scalar_tensor_tensor(xres[:, t, :], ps_out[:, :], gate[:, 0:1], xres[:, t, :],
                                                   ALU.mult, ALU.add).then_inc(s_acc, 1)

            for t in range(STEPS):
                step(-1, t, t == STEPS - 1, t >= 3, started=False)
            dve.wait_ge(s_xres, NT)
            with dve.Fori(0, KVH - 1) as k:
                for t in range(STEPS):
                    step(k, t, True, True)
            for t in range(STEPS):
                step(KVH - 1, t, t < STEPS - 1, t < 3, ending=True)

            dve.wait_ge(s_acc, KVH * STEPS)
            tile_stats(NT - 1)
            dve.wait_ge(s_bb, 16)
            nc.vector.tensor_scalar(b_base_bc[:, :], b_base_bc[:, :], gate[:, 2:3], None, ALU.mult).then_inc(s_bbg, 1)
            dve.wait_ge(s_thr_in, 16)
            nc.vector.tensor_scalar(nb_thr[:, :], nb_thr[:, :], -1.0, None, ALU.mult).then_inc(s_bbg, 1)
            def gate_logits(hf):
                dve.wait_ge(s_gturned, hf + 1)
                logits = gates_of(hf)[:, :, 0:E]
                link(nc.vector.tensor_reduce(gl[:, 3, 0:HT], logits, AX.X, ALU.max, negate=True))
                nc.vector.tensor_tensor(gl[:, 0, :].rearrange("p (t e) -> p t e", e=E), logits,
                                        gl[:, 3, 0:HT].unsqueeze(2).broadcast_to([P, HT, E]), ALU.add).then_inc(s_el, 1)

            def weigh(hf):
                dve.wait_ge(s_ee, hf + 1)

                def te(i):
                    return gl[:, i, :].rearrange("p (t e) -> p t e", e=E)

                def over_e(i):
                    return gl[:, i, 0:HT].unsqueeze(2).broadcast_to([P, HT, E])

                link(nc.vector.tensor_reduce(gl[:, 4, 0:HT], te(1), AX.X, ALU.add))
                link(nc.vector.reciprocal(gl[:, 5, 0:HT], gl[:, 4, 0:HT]))
                link(nc.vector.tensor_tensor(te(6), te(1), over_e(5), ALU.mult))
                link(nc.vector.tensor_scalar(gl[:, 7, 0:HT], gl[:, 2, 0:HT], 1.0, None, ALU.add))
                link(nc.vector.reciprocal(gl[:, 8, 0:HT], gl[:, 7, 0:HT]))
                link(nc.vector.tensor_scalar(gl[:, 9, 0:HT], gl[:, 8, 0:HT], THR_MAX, None, ALU.mult))
                link(nc.vector.tensor_tensor(te(10), te(6), over_e(9), ALU.subtract))
                link(nc.vector.tensor_scalar(gl[:, 11, :], gl[:, 10, :], 0.0, None, ALU.max))
                link(nc.vector.tensor_reduce(gl[:, 12, 0:HT], te(11), AX.X, ALU.add))
                link(nc.vector.scalar_tensor_tensor(gl[:, 13, 0:HT], gl[:, 12, 0:HT], 0.0, gl[:, 12, 0:HT],
                                                    ALU.is_equal, ALU.add))
                link(nc.vector.reciprocal(gl[:, 14, 0:HT], gl[:, 13, 0:HT]))
                link(nc.vector.tensor_tensor(te(15), te(11), over_e(14), ALU.mult))
                if hf:
                    dve.wait_ge(s_made, NTH[("hw", 0)] + 1)
                nc.vector.tensor_copy(wide[:, :, :].rearrange("p t (e r) -> p (t e) r", r=R),
                                      gl[:, 15, :].unsqueeze(2).broadcast_to([P, HT * E, R])).then_inc(s_wide, 1)

            def weighted(hf):
                i = NTH[("hw", hf)]
                dve.wait_ge(s_wideT, hf + 1)
                nc.vector.tensor_tensor(hw[:, :], adaptersT(hf)[:, :], hw[:, :], ALU.mult).then_inc(s_hw, 1)
                lo(i)

            def add_ffn0(b):
                dve.wait_ge(s_f0, b + 1)
                dve.wait_ge(s_xb, b + 1)
                nc.vector.scalar_tensor_tensor(xres[:, b, :], bank[b % 2][:, :], gate[:, 2:3], xres[:, b, :],
                                               ALU.mult, ALU.add).then_inc(s_x2, 1)
                dve.wait_ge(s_x2, b + 1)
                tile_stats(b)

            lo(NTH[("x0", 6)])
            normalise(7, NTH[("x0", 5)] + 1)
            gate_logits(0)
            lo(NTH[("wq", 0)])
            lo(NTH[("wq", 1)])
            lo(NTH[("x0", 7)])
            weigh(0)
            lo(NTH[("wq", 2)])
            lo(NTH[("wq", 3)])
            dve.wait_ge(s_nat[5], 16)
            nc.vector.tensor_reduce(scale[:, 0, :], bin_nat[:, :, :], AX.X, ALU.add, apply_absolute_value=True
                                    ).then_inc(s_wscale, 1)
            dve.wait_ge(s_wscale, 1)
            nc.vector.tensor_scalar(scale[:, 1, :], scale[:, 0, :], 1.0 / D, None, ALU.mult).then_inc(s_wscale, 1)
            weighted(0)
            gate_logits(1)
            for j in range(J1):
                lo(NTH[("wo", j)])
            weigh(1)
            for b in range(HT):
                add_ffn0(b)
                if b == 1:
                    weighted(1)
            for b in (0, 1):
                normalise(NT + b, NTH[("x0", NT - 2 + b)] + 1)
            dve.wait_ge(s_wscale, 2)
            dve.wait_ge(s_clip, 1)
            for i in range(4):
                ins = nc.vector.scalar_tensor_tensor(sign[:, i, :], sign[:, i, :], scale[:, 1, i:i + 1], bin_nat[:, i, :],
                                                     ALU.mult, ALU.subtract)
            ins.then_inc(s_unclipped, 1)
            for b in range(HT, NT):
                add_ffn0(b)
                lo(NTH[("x1", b - HT)])
                normalise(NT + b - HT + 2, NTH[("x1", b - HT)] + 1)
            dve.wait_ge(s_small2, 16)
            for i in range(GH):
                ins = nc.vector.tensor_scalar(negmask[:, i, :], mask_in[:, :], MASKED, -MASKED, ALU.mult, ALU.add)
            ins.then_inc(s_mask, 1)
            for i in range(NTH[("bin", 0)], NTH[("q", J1)] + 1):
                lo(i)
                kind, b = ORDER[i]
                if kind == "x1" and b + 2 < NT:
                    normalise(NT + b + 2, i + 1)

            def max1(u):
                dve.wait_ge(s_s1, u + 1)
                nc.vector.tensor_reduce(nmax1[:, u % DEPTH1, :], scored1[u % DEPTH1][:, :].rearrange("p (g m) -> p g m", g=GH),
                                        AX.X, ALU.max, negate=True).then_inc(s_m1, 1)

            def invert1(u):
                dve.wait_ge(s_e1, u + 1)
                if u >= DEPTH1:
                    dve.wait_ge(s_n1, u - DEPTH1 + 1)
                nc.vector.reciprocal(rinv1[:, u % DEPTH1, :], rsum1[:, u % DEPTH1, :]).then_inc(s_r1, 1)

            def o1_lo(b):
                dve.wait_ge(s_o1h, b + 1)
                minus_hi(o1T[1][:, :, :].rearrange("p j t -> p (j t)"), ps_pv1[:, :],
                         o1T[0][:, :, :].rearrange("p j t -> p (j t)")).then_inc(s_o1l, 1)

            def add_out1(b):
                dve.wait_ge(s_out1, b + 1)
                nc.vector.scalar_tensor_tensor(xres[:, b, :], ps_out1(b)[:, :], gate[:, 1:2], xres[:, b, :],
                                               ALU.mult, ALU.add).then_inc(s_x3, 1)
                dve.wait_ge(s_x3, b + 1)
                tile_stats(b)

            def norm_x3(b):
                normalise(2 * NT + b, NTH[("x1", NT - 2 + b)] + 1 if b < 2 else NTH[("x2", b - 2)] + 1)

            def add_ffn1(b):
                dve.wait_ge(s_f1, b + 1)
                nc.vector.scalar_tensor_tensor(xres[:, b, :], bank[6][:, :], gate[:, 3:4], xres[:, b, :],
                                               ALU.mult, ALU.add).then_inc(s_x4, 1)

            for u in range(DEPTH1):
                max1(u)
            for u in (0, 1):
                invert1(u)
            for u in range(UNITS):
                if u + 1 < J1:
                    lo(NTH[("q", J1 + 1 + u)])
                dve.wait_ge(s_t1h, u + 1)
                B = u // J1
                cols = slice((u % J1) * TOK, (u % J1 + 1) * TOK)
                nc.vector.tensor_tensor(p1T[1][:, B % 2, :, cols], turned1(u)[:, :].rearrange("p (g n) -> p g n", g=GH),
                                        p1T[0][:, B % 2, :, cols].bitcast(F32), ALU.subtract).then_inc(s_t1l, 1)
                if u % UB == 4 and u >= UB:
                    o1_lo(u // UB - 1)
                if u + DEPTH1 < UNITS:
                    max1(u + DEPTH1)
                if u + 2 < UNITS:
                    invert1(u + 2)
                if u % UB == 5 and u >= UB:
                    add_out1(u // UB - 1)
                if u % UB == 7 and u >= UB:
                    norm_x3(u // UB - 1)
                if u % UB == 0 and u >= 2 * UB:
                    lo(NTH[("x2", u // UB - 2)])
                if u % UB == 2 and u >= 2 * UB:
                    add_ffn1(u // UB - 2)
            lo(NTH[("x2", NT - 2)])
            o1_lo(NT - 1)
            add_ffn1(NT - 2)
            add_out1(NT - 1)
            norm_x3(NT - 1)
            lo(NTH[("x2", NT - 1)])
            add_ffn1(NT - 1)

        @block.tensor
        def _(pe):
            def turn_tile(i):
                what, b = TURNED[i]
                if what == "ctx":
                    pe.wait_ge(s_ctx_in[b], 16)
                else:
                    pe.wait_ge(s_xn, b + 1)
                if i >= 4:
                    pe.wait_ge(s_tr_lo, i - 3)
                src = ctx_nat if what == "ctx" else xn_nat
                for c in range(C):
                    mm = nc.tensor.transpose(turn_banks[i % 4][:, c * P:(c + 1) * P], src[:, b, c * P:(c + 1) * P], ident[:, :])
                mm.then_inc(s_tr, 1)

            pe.wait_ge(s_ident, 1)
            for i in range(NT):
                turn_tile(i)
            pe.wait_ge(s_small_in, 80)
            nb = HEADS + 2 * KVH
            nc.tensor.transpose(bank[6][:, 0:nb], bias_nat[:, :], ident[0:nb, 0:nb]).then_inc(s_bias_tr, 1)

            def part(acc, pairs, first, last):
                todo = [(st[a], mv[b]) for st, mv in pairs for a, b in ((1, 0), (0, 1), (0, 0))]
                for i, (st, mv) in enumerate(todo):
                    mm = nc.tensor.matmul(acc, st, mv, start=(first and i == 0), stop=(last and i == len(todo) - 1))
                return mm

            def product(acc, pairs):
                return part(acc, pairs, True, True)

            def both(pair, *index):
                return [a[index] for a in pair]

            every = slice(None)

            def bank_free(i):
                before = [j for j in range(i) if bank_of(j) == bank_of(i)]
                if before:
                    pe.wait_ge(s_lo, before[-1] + 1)
                elif bank_of(i) == 6:
                    pe.wait_ge(s_v_lo, 2 * KVH)
                elif bank_of(i) == 5:
                    pe.wait_ge(s_vt, 2 * KVH)
                elif bank_of(i) == 3:
                    pe.wait_ge(s_q_lo, KVH * STEPS)
                else:
                    pe.wait_ge(s_sum, KVH * STEPS)

            def nat_rows(lo, c):
                return nat[:, :, :].rearrange("p a n -> p (a n)")[:, lo * D + c * P:lo * D + (c + 1) * P]

            def make(name):
                kind, n = name
                i = NTH[name]
                acc = split_bank(i)
                bank_free(i)
                if kind in ("k", "q"):
                    if kind == "k":
                        w, col, src, hf = wk1, every, cT, n
                        pe.wait_ge(s_lo, NTH[("wk", 0)] + 1)
                    else:
                        w, col, src, hf = wq1, slice(n % J1 * P, (n % J1 + 1) * P), xT, n // J1
                        pe.wait_ge(s_lo, NTH[("x1", HT - 1 if hf == 0 else NT - 1)] + 1)
                    cols = slice(hf * HALF, (hf + 1) * HALF)
                    product(acc[:, :], [(both(w, every, c, col), both(src, every, c, cols)) for c in range(C)]).then_inc(s_made, 1)
                    return
                if kind == "v":
                    pe.wait_ge(s_lo, NTH[("wv", 0)] + 1)
                    for b in range(HT):
                        tok = slice((n * HT + b) * TOK, (n * HT + b + 1) * TOK)
                        mm = product(acc[:, b * KV1:(b + 1) * KV1],
                                     [(both(cT, every, c, tok), both(wv1, every, c, every)) for c in range(C)])
                    mm.then_inc(s_made, 1)
                    return
                if kind == "base":
                    pe.wait_ge(s_nat[1], 16)
                    blocks = [nat_rows(i, n) for i in range(4)]
                elif kind == "adapt":
                    pe.wait_ge(s_nat[2], 16 * 7)
                    blocks = [nat_rows(6, c) for c in range(C)]
                elif kind == "gates":
                    blocks = [gates_nat[:, c * P:(c + 1) * P] for c in range(C)]
                elif kind == "up":
                    blocks = [nat_rows(7, i) for i in range(4)]
                elif kind == "wk":
                    pe.wait_ge(s_nat[0], 32)
                    blocks = [nat_rows(4, c) for c in range(C)]
                elif kind == "wv":
                    blocks = [nat_rows(5, c) for c in range(C)]
                elif kind == "wq":
                    pe.wait_ge(s_nat[3], 16 * J1)
                    blocks = [q1_nat[:, j, n * P:(n + 1) * P] for j in range(J1)]
                elif kind == "hw":
                    pe.wait_ge(s_wide, n + 1)
                    blocks = [wide[:, t, :] for t in range(HT)]
                elif kind == "wo":
                    pe.wait_ge(s_perm, 1)
                    blocks = [nat_rows(4 + i, n) for i in range(4)]
                elif kind == "bin":
                    pe.wait_ge(s_bin, 1)
                    blocks = [bin_nat[:, i, n * P:(n + 1) * P] for i in range(4)]
                else:
                    tile = ("x0", "x1", "x2").index(kind) * NT + n
                    pe.wait_ge(s_xn2, tile + 1)
                    blocks = [xn[:, tile % 2, c * P:(c + 1) * P] for c in range(C)]
                col = 0
                for src in blocks:
                    m = src.shape[0]
                    mm = nc.tensor.transpose(acc[:, col:col + m], src, ident[0:m, 0:m])
                    col += m
                mm.then_inc(s_made, 1)

            def step(k, t, attend_next, project, started=True, ending=False):
                g = k * STEPS + t
                b = (t + 1) % NT

                def q_part(cs):
                    h, half = q_head_half(t)
                    cols = slice(half * HALF, (half + 1) * HALF)
                    mm = part(ps_q[:, :], [(both(wq, every, h, c, every), both(xT, every, c, cols)) for c in cs],
                              cs[0] == 0, cs[-1] == C - 1)
                    if cs[-1] == C - 1:
                        mm.then_inc(s_qproj, 1)

                def turn_v():
                    c = 2 if t == 3 else 3
                    pe.wait_ge(s_vt, 2 * k + c)
                    if started:
                        pe.wait_ge(s_v_lo, 2 * k + c - 1)
                    for i in range(4):
                        mm = nc.tensor.transpose(ps_vt[:, i * DH:(i + 1) * DH], vT[:, i, :], ident[:, :])
                    mm.then_inc(s_vtr, 1)

                if started:
                    pe.wait_ge(s_norm, g + 1)
                    for j in range(G):
                        mm = nc.tensor.transpose(ps_pt[:, j * TOK:(j + 1) * TOK], prob[:, j, :], ident[:, :])
                    mm.then_inc(s_ptr, 1)
                if attend_next:
                    if b == 0:
                        pe.wait_ge(s_q_lo, k * STEPS + 12)
                        pe.wait_ge(s_k_lo, 2 * k + 3)
                    if b == 4:
                        pe.wait_ge(s_q_lo, k * STEPS + 8)
                        pe.wait_ge(s_k_lo, 2 * k + 2)
                    tok = slice(b * TOK, (b + 1) * TOK)
                    for j in range(G):
                        acc = ps_s[j // 2][:, j % 2 * 2 * TOK:(j % 2 + 1) * 2 * TOK]
                        nc.tensor.matmul(acc, qT[0][:, j, tok], kT[:, b, :, :].rearrange("p a m -> p (a m)"),
                                         start=True, stop=False)
                        mm = nc.tensor.matmul(acc[:, 0:TOK], qT[1][:, j, tok], kT[:, b, 0, :], start=False, stop=True)
                    mm.then_inc(s_scores, 1)
                if project:
                    if not started and t in (3, 7):
                        pe.wait_ge(s_tr_lo, NT if t == 3 else NTR)
                    if 3 <= t <= 6:
                        pe.wait_ge(s_w_lo, (k + 1) * NS + SLICES.index(("q", q_head_half(t)[0])) + 1)
                    if started or t > 3:
                        pe.wait_ge(s_q_lo, g + 5)
                    q_part((0, 1))
                    if not started:
                        q_part((2, 3))
                if ending:
                    for name in AHEAD.get(t, ()):
                        make(name)
                if started:
                    pe.wait_ge(s_pt_lo, g + 1)
                    if t in (0, 4):
                        pe.wait_ge(s_v_lo, 2 * k + (1 if t == 0 else 2))
                    product(ps_o[:, :], [(both(v, every, t, every), both(pT, every, every))]).then_inc(s_pv, 1)
                if ending:
                    if t == 3:
                        turn_v()
                    for name in BEHIND.get(t, ()):
                        make(name)
                if project:
                    key = t in (3, 4, 7, 0)
                    first = t in (3, 7, 1, 5)
                    half = 0 if 3 <= t <= 6 else 1
                    w = wk if key else wv
                    if t == 3:
                        pe.wait_ge(s_w_lo, (k + 1) * NS + SLICES.index(("k", 0)) + 1)
                        if started:
                            pe.wait_ge(s_vt, 2 * k + 2)
                    if t == 7:
                        pe.wait_ge(s_vt, 2 * k + 3)
                    if t == 5:
                        pe.wait_ge(s_w_lo, (k + 1) * NS + SLICES.index(("v", 0)) + 1)
                        pe.wait_ge(s_k_lo, 2 * k + 3)
                    if t == 1:
                        pe.wait_ge(s_k_lo, 2 * k + 2)
                    cols = slice(half * HALF, (half + 1) * HALF)
                    mm = part(ps_kv[:, :], [(both(w, every, c, every), both(cT, every, c, cols))
                                            for c in ((0, 1) if first else (2, 3))], first, not first)
                    if not first:
                        mm.then_inc(s_kproj if key else s_vproj, 1)
                    if started:
                        q_part((2, 3))
                if not started and t in TURN_AT:
                    for i in TURN_AT[t]:
                        turn_tile(i)
                if (t == 3 and started and not ending) or (t == 7 and attend_next):
                    turn_v()
                if started:
                    if t == 0:
                        pe.wait_ge(s_w_lo, (k + 1) * NS)
                    pe.wait_ge(s_o_lo, g + 1)
                    if t > 0:
                        pe.wait_ge(s_acc, g)
                    else:
                        pe.wait_ge(s_nmax, g + 2)
                    product(ps_out[:, :], [(both(oT, every, j, every),
                                            both(wo, every, bass.ds((k % 2) * (G * D) + j * D, D))) for j in range(G)]
                            ).then_inc(s_out, 1)

            for t in range(STEPS):
                step(-1, t, t == STEPS - 1, t >= 3, started=False)
            with pe.Fori(0, KVH - 1) as k:
                for t in range(STEPS):
                    step(k, t, True, True)
            for t in range(STEPS):
                step(KVH - 1, t, t < STEPS - 1, t < 3, ending=True)

            def adapters_down(hf):
                cols = slice(hf * HALF, (hf + 1) * HALF)
                pe.wait_ge(s_lo, max(NTH[("gates", 0)], NTH[("x0", (hf + 1) * HT - 1)]) + 1)
                if hf == 1:
                    pe.wait_ge(s_acc, KVH * STEPS)
                product(bank[hf][0:NGT, :], [(both(wg, every, c, every), both(xT, every, c, cols)) for c in range(C)]
                        ).then_inc(s_gtmade, 1)
                if hf == 1:
                    make(("hw", 0))
                product(adaptersT(hf)[:, :], [(both(wa, every, c, every), both(xT, every, c, cols)) for c in range(C)])

            def turn_gates(hf):
                pe.wait_ge(s_gt, hf + 1)
                for t in range(HT):
                    mm = nc.tensor.transpose(gates_of(hf)[:, t, :], gatesT[:, hf, t * TOK:(t + 1) * TOK], ident[0:NGT, 0:NGT])
                mm.then_inc(s_gturned, 1)

            def ffn0(b):
                tok = slice(b * TOK, (b + 1) * TOK)
                t = b % HT
                if b >= 2:
                    pe.wait_ge(s_x2, b - 1)
                if b == 1:
                    pe.wait_ge(s_ee, 2)
                pe.wait_ge(s_lo, NTH[("hw", b // HT)] + 1)
                product(bank[b % 2][:, :],
                        [(both(xT, every, c, tok), both(wb, every, c, every)) for c in range(C)]
                        + [(both(hwT[b // HT], every, slice(t * TOK, (t + 1) * TOK)), both(wB, every, every))]).then_inc(s_f0, 1)

            adapters_down(0)
            make(("x0", 6))
            turn_gates(0)
            for i in range(NTH[("wq", 0)], NTH[("wq", C - 1)] + 1):
                make(ORDER[i])
            adapters_down(1)
            turn_gates(1)
            for j in range(J1):
                make(("wo", j))
            ffn0(0)
            ffn0(1)
            make(("hw", 1))
            ffn0(2)
            ffn0(3)
            for b in range(HT, NT):
                ffn0(b)
                make(("x1", b - HT))
            for i in range(NTH[("bin", 0)], NTH[("q", J1)] + 1):
                make(ORDER[i])

            def scores1(u):
                B, j = u // J1, u % J1
                b, gh = B // 2, B % 2
                tok = slice(b * TOK, (b + 1) * TOK)
                if u >= DEPTH1:
                    pe.wait_ge(s_e1, u - DEPTH1 + 1)
                if u == 0:
                    pe.wait_ge(s_lo, NTH[("q", J1 - 1)] + 1)
                    pe.wait_ge(s_mask, 1)
                    pe.wait_ge(s_idr, 1)
                if b == HT:
                    pe.wait_ge(s_lo, NTH[("q", 2 * J1 - 1)] + 1)
                pe.wait_ge(s_kd, 2 * (B + 1))
                acc = scored1[u % DEPTH1][:, :]
                nc.tensor.matmul(acc, ident_r[:, :], negmask[:, :, :].rearrange("p g m -> p (g m)"), start=True, stop=False)
                for i, (a, c) in enumerate(((1, 0), (0, 1), (0, 0))):
                    mm = nc.tensor.matmul(acc, q1T[a][:, j, tok], kd[c][:, gh, :, :].rearrange("p g m -> p (g m)"),
                                          start=False, stop=(i == 2))
                mm.then_inc(s_s1, 1)

            def pv1(B, i):
                b, gh = B // 2, B % 2
                if i == 0:
                    if B == 0:
                        pe.wait_ge(s_lo, NTH[("q", 2 * J1 - 1)] + 1)
                    pe.wait_ge(s_t1l, J1 * (B + 1))
                    pe.wait_ge(s_vd, 2 * (B + 1))
                    if gh == 0 and b >= 1:
                        pe.wait_ge(s_o1l, b)
                part(ps_pv1[:, :], [(both(vd, every, gh, i, every), both(p1T, every, gh, i, every))],
                     gh == 0 and i == 0, gh == 1 and i == GH - 1).then_inc(s_pv1, 1)

            def turn_prob1(u):
                pe.wait_ge(s_n1, u + 1)
                if u >= 1:
                    pe.wait_ge(s_t1l, u if u <= J1 else u - 1)
                if u == J1 + 1:
                    pe.wait_ge(s_lo, NTH[("q", 2 * J1 - 1)] + 1)
                for i in range(GH):
                    mm = nc.tensor.transpose(turned1(u)[:, i * TOK:(i + 1) * TOK], prob1[u % DEPTH1][:, i, :], ident[:, :])
                mm.then_inc(s_t1, 1)

            def out1(b):
                pe.wait_ge(s_o1l, b + 1)
                if 1 <= b < NT - 1:
                    pe.wait_ge(s_x4, b)
                product(ps_out1(b)[:, :], [(both(o1T, every, j, every), both(wo1, every, j, every)) for j in range(J1)]
                        ).then_inc(s_out1, 1)

            def turn_x3(b):
                make(("x2", b))

            def ffn1(b):
                pe.wait_ge(s_lo, NTH[("x2", b)] + 1)
                if b >= 1:
                    pe.wait_ge(s_x4, b)
                tok = slice(b * TOK, (b + 1) * TOK)
                product(bank[6][:, :], [(both(xT, every, c, tok), both(wf1, every, c, every)) for c in range(C)]).then_inc(s_f1, 1)

            for u in range(DEPTH1):
                scores1(u)
            for u in range(UNITS):
                if u + 1 < J1:
                    make(("q", J1 + 1 + u))
                B = u // J1
                if u >= J1 + 1 and u % J1 != 1:
                    pv1((u - 1) // J1 - 1, (u - 1) % J1)
                turn_prob1(u)
                if u + DEPTH1 < UNITS:
                    scores1(u + DEPTH1)
                if u >= J1 + 1 and u % J1 == 1:
                    pv1((u - 1) // J1 - 1, 0)
                if u % UB == 5 and u >= UB:
                    out1(u // UB - 1)
                if u % UB == 0 and u >= 2 * UB:
                    turn_x3(u // UB - 2)
                if u % UB == 2 and u >= 2 * UB:
                    ffn1(u // UB - 2)
            pv1(2 * NT - 2, GH - 1)
            turn_x3(NT - 2)
            for i in range(GH):
                pv1(2 * NT - 1, i)
            ffn1(NT - 2)
            out1(NT - 1)
            turn_x3(NT - 1)
            ffn1(NT - 1)


_INS = ["x", "ctx_4096", "mask_SxS2_bk0", "g_xattn", "g_ffn", "L0_xattn_Wq", "L0_xattn_bq", "L0_xattn_Wkv", "L0_xattn_bkv",
        "L0_xattn_Wo", "L0_xattn_bo", "L0_ffn_W_base", "L0_ffn_b_base", "L0_ffn_W_gate", "L0_ffn_W_thr", "L0_ffn_b_thr",
        "L0_ffn_A_w", "L0_ffn_B_w", "L1_xattn_w_q", "L1_xattn_w_k", "L1_xattn_w_v", "L1_xattn_w_out", "L1_ffn_weight"]
_OUTS = [((8, 128, 512), "float32")]


def kernel(**inputs):
    import numpy as _np
    import concourse.bacc as _bacc
    from concourse import mybir as _mybir
    from concourse.bass_utils import run_bass_kernel_spmd as _run

    nc = _bacc.Bacc("TRN2", target_bir_lowering=False, num_devices=1)
    arrays, args = {}, []
    for name in _INS:
        a = _np.ascontiguousarray(inputs[name])
        arrays[f"in_{name}_dram"] = a
        args.append(nc.dram_tensor(f"in_{name}_dram", a.shape, _mybir.dt.from_np(a.dtype), kind="ExternalInput").ap())
    for i, (shape, dtype) in enumerate(_OUTS):
        dt = _mybir.dt.from_np(_np.dtype(dtype))
        args.append(nc.dram_tensor(f"out_{i}_dram", shape, dt, kind="ExternalOutput").ap())
    build(nc, *args)
    r = _run(nc, [arrays], core_ids=[0])
    return r.results[0]["out_0_dram"]
```
